# Optimizing a Trainium2 kernel written in Bass

```python
import numpy as np
import jax
import jax.numpy as jnp

def _softmax(x, axis=-1):
    return jax.nn.softmax(x, axis=axis)

def _gelu(x):
    return jax.nn.gelu(x, approximate=True)

def _silu(x):
    return jax.nn.silu(x)

def _sigmoid(x):
    return jax.nn.sigmoid(x)

def _layernorm(x, axis=-1, eps=1e-05):
    m = jnp.mean(x, axis=axis, keepdims=True)
    v = jnp.var(x, axis=axis, keepdims=True)
    return (x - m) / jnp.sqrt(v + eps)

def _scatter_add(tgt, idx, src, axis=0):
    return tgt.at[idx].add(src)

def _segment_sum(src, seg, n):
    return jax.ops.segment_sum(src, seg, n)
kernel_name = 'mk_pixart_resid_d4_seqx_r8_b17e47'

def setup_inputs(seed: int=0):
    np.random.seed(seed)
    _w = jnp.asarray

    def _rec_inputs():
        import jax
        import jax.numpy as jnp
        _rk = jax.random.key(seed)
        x = -0.0002928 + 1 * jax.random.normal(jax.random.fold_in(_rk, 1), (8, 256, 128), jnp.float32)
        _lenS = 256 - jax.random.randint(jax.random.fold_in(_rk, 7), (8,), 0, max(1, 256 // 4) + 1, jnp.int32)
        _lenS2 = 1601 - jax.random.randint(jax.random.fold_in(_rk, 8), (8,), 0, max(1, 1601 // 4) + 1, jnp.int32)
        _ctx_1024P = jax.random.normal(jax.random.fold_in(_rk, 11), (8, 16, 128), jnp.float32)
        _ctx_1024c = jax.random.dirichlet(jax.random.fold_in(_rk, 511), 0.3 * jnp.ones((16,), jnp.float32), (8, 1601))
        _ctx_1024t = jnp.einsum('bsk,bkd->bsd', _ctx_1024c, _ctx_1024P)
        _ctx_1024t = _ctx_1024t * jax.lax.rsqrt(jnp.mean(jnp.square(_ctx_1024t)) + 1e-12) * 0.953939
        ctx_1024 = -1.39393e-06 + 0.999914 * (_ctx_1024t + 0.3 * jax.random.normal(jax.random.fold_in(_rk, 611), (8, 1601, 128), jnp.float32))
        condB_tau = jax.random.uniform(jax.random.fold_in(_rk, 12), (8,), jnp.float32, 0.0, 1.23395)
        fside_BxS2_0 = -0.00205293 + 0.99739 * jax.random.normal(jax.random.fold_in(_rk, 13), (8, 1601), jnp.float32)
        condB_pt = jax.random.uniform(jax.random.fold_in(_rk, 15), (8,), jnp.float32, 0.0, 226.919)
        return (x, ctx_1024, condB_tau, fside_BxS2_0, condB_pt, _lenS2)
    x, ctx_1024, condB_tau, fside_BxS2_0, condB_pt, _lenS2 = _rec_inputs()

    def _L0_xcond_setup():
        import jax, jax.numpy as jnp
        import numpy as np
        B, S, D, H = (2, 256, 128, 16)
        DK = D // H

        def _split_heads(x):
            b, s, _ = x.shape
            return x.reshape(b, s, H, DK).transpose(0, 2, 1, 3)
        key = jax.random.key(seed)
        ks = jax.random.split(key, 14)
        inp = {'query': jax.random.normal(ks[0], (B, S, D), jnp.float32), 'key': jax.random.normal(ks[1], (B, S, D), jnp.float32), 'value': jax.random.normal(ks[2], (B, S, D), jnp.float32), 'tau': jax.random.uniform(ks[3], (B, 1), jnp.float32, 0.5, 1.5), 'delta': jax.random.normal(ks[4], (B, S), jnp.float32)}
        sc = 1.0 / np.sqrt(D)
        for i, name in enumerate(['q', 'k', 'v', 'o']):
            inp[f'W{name}'] = jax.random.normal(ks[5 + 2 * i], (D, D), jnp.float32) * sc
            inp[f'b{name}'] = jax.random.normal(ks[6 + 2 * i], (D,), jnp.float32) * 0.01
        return inp
    _L0_xcond_all = _L0_xcond_setup()
    _L0_xcond_in = {k: v for k, v in _L0_xcond_all.items() if k in ('Wq', 'bq', 'Wk', 'bk', 'Wv', 'bv', 'Wo', 'bo')}
    del _L0_xcond_all

    def _L0_ffn_setup():
        import jax, jax.numpy as jnp
        import numpy as np
        EMBED_DIM = 128
        HIDDEN = 4 * EMBED_DIM
        BATCH, SEQ = (4, 512)
        EPS = 1e-05

        def _quant_weight(w):
            s = jnp.clip(jnp.mean(jnp.abs(w)), EPS, None)
            wq = jnp.clip(jnp.round(w / s), -1.0, 1.0) * s
            return w + jax.lax.stop_gradient(wq - w)

        def _quant_act(x):
            scale = 127.0 / jnp.clip(jnp.max(jnp.abs(x), axis=-1, keepdims=True), EPS, None)
            xq = jnp.clip(jnp.round(x * scale), -128.0, 127.0) / scale
            return x + jax.lax.stop_gradient(xq - x)

        def _bitlinear(x, w):
            return jnp.einsum('bsi,oi->bso', _quant_act(x), _quant_weight(w))
        key = jax.random.key(seed)
        k1, k2, k3 = jax.random.split(key, 3)
        x = jax.random.normal(k1, (BATCH, SEQ, EMBED_DIM), dtype=jnp.float32)
        w1 = jax.random.normal(k2, (HIDDEN, EMBED_DIM), dtype=jnp.float32) * (1.0 / np.sqrt(EMBED_DIM))
        w2 = jax.random.normal(k3, (EMBED_DIM, HIDDEN), dtype=jnp.float32) * (1.0 / np.sqrt(HIDDEN))
        return {'x': x, 'w1': w1, 'w2': w2}
    _L0_ffn_all = _L0_ffn_setup()
    _L0_ffn_in = {k: v for k, v in _L0_ffn_all.items() if k in ('w1', 'w2')}
    del _L0_ffn_all

    def _L1_xcond_setup():
        import jax, jax.numpy as jnp
        import numpy as np
        D_MODEL = 128
        N_HEADS = 16
        key = jax.random.key(seed)
        ks = jax.random.split(key, 16)
        B, L, S, D = (4, 256, 256, D_MODEL)
        inp = {'q': jax.random.normal(ks[0], (B, L, D), jnp.float32), 'k': jax.random.normal(ks[1], (B, S, D), jnp.float32), 'v': jax.random.normal(ks[2], (B, S, D), jnp.float32), 'tau': jax.random.uniform(ks[3], (B, 1), jnp.float32, 0.5, 1.5), 'delta': jax.random.normal(ks[4], (B, S), jnp.float32)}
        s = 1.0 / np.sqrt(D)
        inp['Wq'] = jax.random.normal(ks[5], (D, D), jnp.float32) * s
        inp['bq'] = jnp.zeros((D,), jnp.float32)
        inp['Wk'] = jax.random.normal(ks[6], (D, D), jnp.float32) * s
        inp['bk'] = jnp.zeros((D,), jnp.float32)
        inp['Wv'] = jax.random.normal(ks[7], (D, D), jnp.float32) * s
        inp['bv'] = jnp.zeros((D,), jnp.float32)
        inp['Wo'] = jax.random.normal(ks[8], (D, D), jnp.float32) * s
        inp['bo'] = jnp.zeros((D,), jnp.float32)
        return inp
    _L1_xcond_all = _L1_xcond_setup()
    _L1_xcond_in = {k: v for k, v in _L1_xcond_all.items() if k in ('Wq', 'bq', 'Wk', 'bk', 'Wv', 'bv', 'Wo', 'bo')}
    del _L1_xcond_all

    def _L1_ffn_setup():
        import jax, jax.numpy as jnp
        import numpy as np
        NUM_EXPERTS = 8
        TOP_K = 2
        DIM = 128
        HIDDEN = 512
        B, S = (2, 128)
        key = jax.random.key(seed)
        k_x, k_g, k_1, k_2, k_3 = jax.random.split(key, 5)
        s_d = 1.0 / np.sqrt(DIM)
        s_h = 1.0 / np.sqrt(HIDDEN)
        return {'x': jax.random.normal(k_x, (B, S, DIM), dtype=jnp.float32), 'gate_w': jax.random.normal(k_g, (NUM_EXPERTS, DIM), dtype=jnp.float32) * s_d, 'w1': jax.random.normal(k_1, (NUM_EXPERTS, HIDDEN, DIM), dtype=jnp.float32) * s_d, 'w2': jax.random.normal(k_2, (NUM_EXPERTS, DIM, HIDDEN), dtype=jnp.float32) * s_h, 'w3': jax.random.normal(k_3, (NUM_EXPERTS, HIDDEN, DIM), dtype=jnp.float32) * s_d}
    _L1_ffn_all = _L1_ffn_setup()
    _L1_ffn_in = {k: v for k, v in _L1_ffn_all.items() if k in ('gate_w', 'w1', 'w2', 'w3')}
    del _L1_ffn_all

    def _L2_xcond_setup():
        import jax, jax.numpy as jnp
        import numpy as np
        N, L, H, Q = (64, 258, 128, 32)
        WINDOW = 16.0
        DEV_POW = 128.0
        key = jax.random.key(seed)
        k1, k2, k3, k4, k5, k6 = jax.random.split(key, 6)
        encoder_outputs = jax.random.normal(k1, (N, L, H), dtype=jnp.float32)
        decoder_h_t = jax.random.normal(k2, (N, Q, H), dtype=jnp.float32)
        src_len = jax.random.randint(k3, (N,), 32, L + 1).astype(jnp.int32)
        p_t = jax.random.uniform(k4, (N,), dtype=jnp.float32) * (src_len.astype(jnp.float32) - 1.0)
        W_a = jax.random.normal(k5, (H, H), dtype=jnp.float32) * (1.0 / np.sqrt(H))
        W_c = jax.random.normal(k6, (H, 2 * H), dtype=jnp.float32) * (1.0 / np.sqrt(2 * H))
        return {'encoder_outputs': encoder_outputs, 'decoder_h_t': decoder_h_t, 'src_len': src_len, 'p_t': p_t, 'W_a': W_a, 'W_c': W_c}
    _L2_xcond_all = _L2_xcond_setup()
    _L2_xcond_in = {k: v for k, v in _L2_xcond_all.items() if k in ('W_a', 'W_c')}
    del _L2_xcond_all

    def _L2_ffn_setup():
        import jax, jax.numpy as jnp
        import numpy as np
        EPS = 1e-09
        key = jax.random.key(seed)
        k1, k2, k3, k4 = jax.random.split(key, 4)
        B, T, H, D, E = (2, 256, 128, 128, 8)
        x = jax.random.normal(k1, (B, T, H), dtype=jnp.float32)
        gate_w = jax.random.normal(k2, (E, H), dtype=jnp.float32) * 0.02
        gate_up_proj = jax.random.normal(k3, (E, H, 2 * D), dtype=jnp.float32) * 0.02
        down_proj = jax.random.normal(k4, (E, D, H), dtype=jnp.float32) * 0.02
        return {'x': x, 'gate_w': gate_w, 'gate_up_proj': gate_up_proj, 'down_proj': down_proj}
    _L2_ffn_all = _L2_ffn_setup()
    _L2_ffn_in = {k: v for k, v in _L2_ffn_all.items() if k in ('gate_w', 'gate_up_proj', 'down_proj')}
    del _L2_ffn_all

    def _L3_xcond_setup():
        import jax, jax.numpy as jnp
        import numpy as np
        B, S, D, H = (2, 256, 128, 16)
        DK = D // H

        def _split_heads(x):
            b, s, _ = x.shape
            return x.reshape(b, s, H, DK).transpose(0, 2, 1, 3)
        key = jax.random.key(seed)
        ks = jax.random.split(key, 14)
        inp = {'query': jax.random.normal(ks[0], (B, S, D), jnp.float32), 'key': jax.random.normal(ks[1], (B, S, D), jnp.float32), 'value': jax.random.normal(ks[2], (B, S, D), jnp.float32), 'tau': jax.random.uniform(ks[3], (B, 1), jnp.float32, 0.5, 1.5), 'delta': jax.random.normal(ks[4], (B, S), jnp.float32)}
        sc = 1.0 / np.sqrt(D)
        for i, name in enumerate(['q', 'k', 'v', 'o']):
            inp[f'W{name}'] = jax.random.normal(ks[5 + 2 * i], (D, D), jnp.float32) * sc
            inp[f'b{name}'] = jax.random.normal(ks[6 + 2 * i], (D,), jnp.float32) * 0.01
        return inp
    _L3_xcond_all = _L3_xcond_setup()
    _L3_xcond_in = {k: v for k, v in _L3_xcond_all.items() if k in ('Wq', 'bq', 'Wk', 'bk', 'Wv', 'bv', 'Wo', 'bo')}
    del _L3_xcond_all

    def _L3_ffn_setup():
        import jax, jax.numpy as jnp
        import numpy as np
        DIM = 128
        HIDDEN = 256
        N_EXPERTS = 8
        TOP_K = 2
        EPS = 1e-06

        def rms_norm(x, scale, eps=EPS):
            ms = jnp.mean(jnp.square(x.astype(jnp.float32)), axis=-1, keepdims=True)
            s = scale.astype(jnp.float32) * jax.lax.rsqrt(ms + eps)
            return x * s.astype(x.dtype)

        def moe_linear(xf, ids, W):
            E = W.shape[0]
            out = jnp.zeros((xf.shape[0], W.shape[1]), dtype=xf.dtype)
            for e in range(E):
                out = out + jnp.where((ids == e)[:, None], xf @ W[e].T, 0.0)
            return out
        key = jax.random.key(seed)
        k1, k2, k3, k4 = jax.random.split(key, 4)
        x = jax.random.normal(k1, (4, 512, DIM), dtype=jnp.float32)
        norm_scale = jnp.ones((DIM,), dtype=jnp.float32)
        w_router = jax.random.normal(k2, (N_EXPERTS, DIM), dtype=jnp.float32) / np.sqrt(DIM)
        lim_up = np.sqrt(6.0 / (DIM + 2 * HIDDEN))
        w_up = jax.random.uniform(k3, (N_EXPERTS, 2 * HIDDEN, DIM), dtype=jnp.float32, minval=-lim_up, maxval=lim_up)
        lim_dn = np.sqrt(6.0 / (HIDDEN + DIM))
        w_down = jax.random.uniform(k4, (N_EXPERTS, DIM, HIDDEN), dtype=jnp.float32, minval=-lim_dn, maxval=lim_dn)
        return {'x': x, 'norm_scale': norm_scale, 'w_router': w_router, 'w_up': w_up, 'w_down': w_down}
    _L3_ffn_all = _L3_ffn_setup()
    _L3_ffn_in = {k: v for k, v in _L3_ffn_all.items() if k in ('norm_scale', 'w_router', 'w_up', 'w_down')}
    del _L3_ffn_all
    return {'x': x, 'ctx_1024': ctx_1024, 'condB_tau': condB_tau, 'fside_BxS2_0': fside_BxS2_0, 'condB_pt': condB_pt, '_lenS2': _lenS2, 'L0_xcond_Wq': _L0_xcond_in['Wq'], 'L0_xcond_bq': _L0_xcond_in['bq'], 'L0_xcond_Wk': _L0_xcond_in['Wk'], 'L0_xcond_bk': _L0_xcond_in['bk'], 'L0_xcond_Wv': _L0_xcond_in['Wv'], 'L0_xcond_bv': _L0_xcond_in['bv'], 'L0_xcond_Wo': _L0_xcond_in['Wo'], 'L0_xcond_bo': _L0_xcond_in['bo'], 'L0_ffn_w1': _L0_ffn_in['w1'], 'L0_ffn_w2': _L0_ffn_in['w2'], 'L1_xcond_Wq': _L1_xcond_in['Wq'], 'L1_xcond_bq': _L1_xcond_in['bq'], 'L1_xcond_Wk': _L1_xcond_in['Wk'], 'L1_xcond_bk': _L1_xcond_in['bk'], 'L1_xcond_Wv': _L1_xcond_in['Wv'], 'L1_xcond_bv': _L1_xcond_in['bv'], 'L1_xcond_Wo': _L1_xcond_in['Wo'], 'L1_xcond_bo': _L1_xcond_in['bo'], 'L1_ffn_gate_w': _L1_ffn_in['gate_w'], 'L1_ffn_w1': _L1_ffn_in['w1'], 'L1_ffn_w2': _L1_ffn_in['w2'], 'L1_ffn_w3': _L1_ffn_in['w3'], 'L2_xcond_W_a': _L2_xcond_in['W_a'], 'L2_xcond_W_c': _L2_xcond_in['W_c'], 'L2_ffn_gate_w': _L2_ffn_in['gate_w'], 'L2_ffn_gate_up_proj': _L2_ffn_in['gate_up_proj'], 'L2_ffn_down_proj': _L2_ffn_in['down_proj'], 'L3_xcond_Wq': _L3_xcond_in['Wq'], 'L3_xcond_bq': _L3_xcond_in['bq'], 'L3_xcond_Wk': _L3_xcond_in['Wk'], 'L3_xcond_bk': _L3_xcond_in['bk'], 'L3_xcond_Wv': _L3_xcond_in['Wv'], 'L3_xcond_bv': _L3_xcond_in['bv'], 'L3_xcond_Wo': _L3_xcond_in['Wo'], 'L3_xcond_bo': _L3_xcond_in['bo'], 'L3_ffn_norm_scale': _L3_ffn_in['norm_scale'], 'L3_ffn_w_router': _L3_ffn_in['w_router'], 'L3_ffn_w_up': _L3_ffn_in['w_up'], 'L3_ffn_w_down': _L3_ffn_in['w_down']}

def reference(x, ctx_1024, condB_tau, fside_BxS2_0, condB_pt, _lenS2, L0_xcond_Wq, L0_xcond_bq, L0_xcond_Wk, L0_xcond_bk, L0_xcond_Wv, L0_xcond_bv, L0_xcond_Wo, L0_xcond_bo, L0_ffn_w1, L0_ffn_w2, L1_xcond_Wq, L1_xcond_bq, L1_xcond_Wk, L1_xcond_bk, L1_xcond_Wv, L1_xcond_bv, L1_xcond_Wo, L1_xcond_bo, L1_ffn_gate_w, L1_ffn_w1, L1_ffn_w2, L1_ffn_w3, L2_xcond_W_a, L2_xcond_W_c, L2_ffn_gate_w, L2_ffn_gate_up_proj, L2_ffn_down_proj, L3_xcond_Wq, L3_xcond_bq, L3_xcond_Wk, L3_xcond_bk, L3_xcond_Wv, L3_xcond_bv, L3_xcond_Wo, L3_xcond_bo, L3_ffn_norm_scale, L3_ffn_w_router, L3_ffn_w_up, L3_ffn_w_down):
    import jax
    import jax.numpy as jnp

    def _L0_xcond_ref(query, key, value, tau, delta, Wq, bq, Wk, bk, Wv, bv, Wo, bo):
        import jax, jax.numpy as jnp
        import numpy as np
        B, S, D, H = (2, 256, 128, 16)
        DK = D // H

        def _split_heads(x):
            b, s, _ = x.shape
            return x.reshape(b, s, H, DK).transpose(0, 2, 1, 3)
        q = _split_heads(query @ Wq.T + bq)
        k = _split_heads(key @ Wk.T + bk)
        v = _split_heads(value @ Wv.T + bv)
        scores = jnp.einsum('bhqd,bhkd->bhqk', q, k)
        scores = scores * tau[:, :, None, None] + delta[:, None, None, :]
        scores = scores / jnp.sqrt(jnp.asarray(DK, scores.dtype))
        p_attn = jax.nn.softmax(scores, axis=-1)
        x = jnp.einsum('bhqk,bhkd->bhqd', p_attn, v)
        x = x.transpose(0, 2, 1, 3).reshape(query.shape[0], -1, H * DK)
        return x @ Wo.T + bo

    def _L0_ffn_ref(x, w1, w2):
        import jax, jax.numpy as jnp
        import numpy as np
        EMBED_DIM = 128
        HIDDEN = 4 * EMBED_DIM
        BATCH, SEQ = (4, 512)
        EPS = 1e-05

        def _quant_weight(w):
            s = jnp.clip(jnp.mean(jnp.abs(w)), EPS, None)
            wq = jnp.clip(jnp.round(w / s), -1.0, 1.0) * s
            return w + jax.lax.stop_gradient(wq - w)

        def _quant_act(x):
            scale = 127.0 / jnp.clip(jnp.max(jnp.abs(x), axis=-1, keepdims=True), EPS, None)
            xq = jnp.clip(jnp.round(x * scale), -128.0, 127.0) / scale
            return x + jax.lax.stop_gradient(xq - x)

        def _bitlinear(x, w):
            return jnp.einsum('bsi,oi->bso', _quant_act(x), _quant_weight(w))
        h = jax.nn.gelu(_bitlinear(x, w1), approximate=False)
        return _bitlinear(h, w2)

    def _L1_xcond_ref(q, k, v, tau, delta, Wq, bq, Wk, bk, Wv, bv, Wo, bo):
        import jax, jax.numpy as jnp
        import numpy as np
        D_MODEL = 128
        N_HEADS = 16
        B, L, D = q.shape
        S = k.shape[1]
        H = N_HEADS
        E = D // H
        qh = (q @ Wq.T + bq).reshape(B, L, H, E)
        kh = (k @ Wk.T + bk).reshape(B, S, H, E)
        vh = (v @ Wv.T + bv).reshape(B, S, H, E)
        scale = 1.0 / np.sqrt(E).astype(np.float32)
        scores = jnp.einsum('blhe,bshe->bhls', qh, kh)
        scores = scores * tau[:, None, None, :] + delta[:, None, None, :]
        a = jax.nn.softmax(scale * scores, axis=-1)
        out = jnp.einsum('bhls,bshd->blhd', a, vh).reshape(B, L, D)
        return out @ Wo.T + bo

    def _L1_ffn_ref(x, gate_w, w1, w2, w3):
        import jax, jax.numpy as jnp
        import numpy as np
        NUM_EXPERTS = 8
        TOP_K = 2
        DIM = 128
        HIDDEN = 512
        B, S = (2, 128)
        orig_shape = x.shape
        xt = x.reshape(-1, orig_shape[-1])
        scores = xt @ gate_w.T
        top_vals, top_idx = jax.lax.top_k(scores, TOP_K)
        top_w = jax.nn.softmax(top_vals, axis=-1)
        combine = jnp.einsum('tke,tk->te', jax.nn.one_hot(top_idx, NUM_EXPERTS, dtype=xt.dtype), top_w)
        h = jax.nn.silu(jnp.einsum('td,ehd->eth', xt, w1)) * jnp.einsum('td,ehd->eth', xt, w3)
        ye = jnp.einsum('eth,edh->etd', h, w2)
        y = jnp.einsum('te,etd->td', combine, ye)
        return y.reshape(orig_shape)

    def _L2_xcond_ref(encoder_outputs, decoder_h_t, src_len, p_t, W_a, W_c):
        import jax, jax.numpy as jnp
        import numpy as np
        N, L, H, Q = (64, 258, 128, 32)
        WINDOW = 16.0
        DEV_POW = 128.0
        n, l, h = encoder_outputs.shape
        idx = jnp.arange(l, dtype=jnp.float32)
        src_end = src_len.astype(jnp.float32)
        attn_start = jnp.maximum(p_t - WINDOW, 0.0)
        attn_end = jnp.minimum(p_t + WINDOW, src_end)
        mask = (idx[None, :] < attn_start[:, None]) | (idx[None, :] > attn_end[:, None])
        score = jnp.einsum('nqh,hk,nlk->nql', decoder_h_t, W_a, encoder_outputs)
        score = jnp.where(mask[:, None, :], -1000000000.0, score)
        align = jax.nn.softmax(score, axis=2)
        gauss = jnp.exp(-(idx[None, :] - p_t[:, None]) ** 2 / DEV_POW)
        align = align * gauss[:, None, :]
        context = jnp.einsum('nql,nlh->nqh', align, encoder_outputs)
        cat = jnp.concatenate([context, decoder_h_t], axis=2)
        return jnp.tanh(cat @ W_c.T)

    def _L2_ffn_ref(x, gate_w, gate_up_proj, down_proj):
        import jax, jax.numpy as jnp
        import numpy as np
        EPS = 1e-09
        B, T, H = x.shape
        E = gate_w.shape[0]
        top_k = 2
        hidden = x.reshape(-1, H)
        router_logits = hidden @ gate_w.T
        routing_weights = jax.nn.softmax(router_logits.astype(jnp.float32), axis=-1)
        topk_weights, topk_indices = jax.lax.top_k(routing_weights, top_k)
        topk_weights = topk_weights / (jnp.sum(topk_weights, axis=-1, keepdims=True) + EPS)
        N = hidden.shape[0]
        routed = jnp.zeros((N, E), dtype=router_logits.dtype)
        rows = jnp.arange(N)[:, None]
        routed = routed.at[rows, topk_indices].set(topk_weights.astype(router_logits.dtype))
        routed = routed / (jnp.sum(routed, axis=-1, keepdims=True) + EPS)
        routed = routed.astype(hidden.dtype)
        gate_up = jnp.einsum('th,ehq->teq', hidden, gate_up_proj)
        gate, up = jnp.split(gate_up, 2, axis=-1)
        expert_outputs = jnp.einsum('teq,eqh->teh', jax.nn.silu(gate) * up, down_proj)
        out = jnp.sum(expert_outputs * routed[:, :, None], axis=1)
        return out.reshape(B, T, H)

    def _L3_xcond_ref(query, key, value, tau, delta, Wq, bq, Wk, bk, Wv, bv, Wo, bo):
        import jax, jax.numpy as jnp
        import numpy as np
        B, S, D, H = (2, 256, 128, 16)
        DK = D // H

        def _split_heads(x):
            b, s, _ = x.shape
            return x.reshape(b, s, H, DK).transpose(0, 2, 1, 3)
        q = _split_heads(query @ Wq.T + bq)
        k = _split_heads(key @ Wk.T + bk)
        v = _split_heads(value @ Wv.T + bv)
        scores = jnp.einsum('bhqd,bhkd->bhqk', q, k)
        scores = scores * tau[:, :, None, None] + delta[:, None, None, :]
        scores = scores / jnp.sqrt(jnp.asarray(DK, scores.dtype))
        p_attn = jax.nn.softmax(scores, axis=-1)
        x = jnp.einsum('bhqk,bhkd->bhqd', p_attn, v)
        x = x.transpose(0, 2, 1, 3).reshape(query.shape[0], -1, H * DK)
        return x @ Wo.T + bo

    def _L3_ffn_ref(x, norm_scale, w_router, w_up, w_down):
        import jax, jax.numpy as jnp
        import numpy as np
        DIM = 128
        HIDDEN = 256
        N_EXPERTS = 8
        TOP_K = 2
        EPS = 1e-06

        def rms_norm(x, scale, eps=EPS):
            ms = jnp.mean(jnp.square(x.astype(jnp.float32)), axis=-1, keepdims=True)
            s = scale.astype(jnp.float32) * jax.lax.rsqrt(ms + eps)
            return x * s.astype(x.dtype)

        def moe_linear(xf, ids, W):
            E = W.shape[0]
            out = jnp.zeros((xf.shape[0], W.shape[1]), dtype=xf.dtype)
            for e in range(E):
                out = out + jnp.where((ids == e)[:, None], xf @ W[e].T, 0.0)
            return out
        B, S, D = x.shape
        skip = x
        xn = rms_norm(x, norm_scale)
        scores = (xn @ w_router.T).astype(jnp.float32)
        scores_topk, idx = jax.lax.top_k(scores, TOP_K)
        weights = jax.nn.softmax(scores_topk, axis=-1)
        xf = jnp.broadcast_to(xn[..., None, :], (B, S, TOP_K, D)).reshape(-1, D)
        ids = idx.reshape(-1)
        up = moe_linear(xf, ids, w_up)
        u, gate = jnp.split(up, 2, axis=-1)
        h = u * jax.nn.silu(gate)
        down = moe_linear(h, ids, w_down)
        down = down.reshape(B, S, TOP_K, D)
        out = jnp.sum(down * weights[..., None].astype(down.dtype), axis=-2)
        return out + skip
    x = x + _L0_xcond_ref(_layernorm(x, axis=-1), ctx_1024, ctx_1024, condB_tau[:, None], fside_BxS2_0, L0_xcond_Wq, L0_xcond_bq, L0_xcond_Wk, L0_xcond_bk, L0_xcond_Wv, L0_xcond_bv, L0_xcond_Wo, L0_xcond_bo)
    x = x + _L0_ffn_ref(_layernorm(x, axis=-1), L0_ffn_w1, L0_ffn_w2)
    x = x + _L1_xcond_ref(_layernorm(x, axis=-1), ctx_1024, ctx_1024, condB_tau[:, None], fside_BxS2_0, L1_xcond_Wq, L1_xcond_bq, L1_xcond_Wk, L1_xcond_bk, L1_xcond_Wv, L1_xcond_bv, L1_xcond_Wo, L1_xcond_bo)
    x = x + _L1_ffn_ref(_layernorm(x, axis=-1), L1_ffn_gate_w, L1_ffn_w1, L1_ffn_w2, L1_ffn_w3)
    x = x + _L2_xcond_ref(ctx_1024, _layernorm(x, axis=-1), _lenS2, condB_pt, L2_xcond_W_a, L2_xcond_W_c)
    x = x + _L2_ffn_ref(_layernorm(x, axis=-1), L2_ffn_gate_w, L2_ffn_gate_up_proj, L2_ffn_down_proj)
    x = x + _L3_xcond_ref(_layernorm(x, axis=-1), ctx_1024, ctx_1024, condB_tau[:, None], fside_BxS2_0, L3_xcond_Wq, L3_xcond_bq, L3_xcond_Wk, L3_xcond_bk, L3_xcond_Wv, L3_xcond_bv, L3_xcond_Wo, L3_xcond_bo)
    x = x + _L3_ffn_ref(_layernorm(x, axis=-1), L3_ffn_norm_scale, L3_ffn_w_router, L3_ffn_w_up, L3_ffn_w_down)
    return x

_drawn_inputs = setup_inputs


def setup_inputs(seed=0):
    import zlib

    import numpy as np

    out = dict(_drawn_inputs(seed))
    spreads = {'L1_xcond_bq': (0.0, 0.317),
     'L1_xcond_bk': (0.0, 2.0),
     'L1_xcond_bv': (0.0, 0.1),
     'L1_xcond_bo': (0.0, 0.1),
     'L3_ffn_norm_scale': (1.0, 0.6)}
    factors = {'L0_xcond_bq': 6.33,
     'L0_xcond_bk': 64.0,
     'L0_xcond_bo': 2.789,
     'L2_ffn_gate_w': 8.0,
     'L2_ffn_gate_up_proj': 8.0,
     'L2_ffn_down_proj': 8.0,
     'L3_xcond_bq': 64.0,
     'L3_xcond_bk': 64.0,
     'L3_xcond_bv': 7.042,
     'L3_xcond_bo': 7.729}
    for name, (base, spread) in spreads.items():
        noise = np.random.default_rng([zlib.crc32(name.encode()), seed]).standard_normal(out[name].shape)
        drawn = base * np.exp(spread * noise) if base else spread * noise
        out[name] = jnp.asarray(drawn.astype(out[name].dtype))
    for name, factor in factors.items():
        out[name] = (out[name] * factor).astype(out[name].dtype)
    return out
```

```python
from contextlib import ExitStack

import concourse.bass as bass
from concourse import mybir
from concourse.alu_op_type import AluOpType as ALU

F32 = mybir.dt.float32
F32R = mybir.dt.float32r
BF16 = mybir.dt.bfloat16
U32 = mybir.dt.uint32
I32 = mybir.dt.int32
ACT = mybir.ActivationFunctionType
AX = mybir.AxisListType

B, S, D = 8, 256, 128
L = 1601
H, DK = 16, 8
P = 128
TILES = B * S // P
TOK = B * S
QT = S // P
KC = -(-L // P)
LAST = L - (KC - 1) * P
G, J = 4, 4
ROWS = J * DK
E = 8
LN_EPS, RMS_EPS, L2_EPS, Q_EPS = 1e-5, 1e-6, 1e-9, 1e-5
ROUND = 1.5 * 2.0 ** 23
EXPERT_TOK = 512

UNITS = KC * 2
LAG = 3
GUARD_TILES = J * QT * 2
GUARD_SPLIT = 1024
GUARD_AT = {1 + (k * 18) // GUARD_TILES: [] for k in range(GUARD_TILES)}
for _k in range(GUARD_TILES):
    GUARD_AT[1 + (_k * 18) // GUARD_TILES].append(_k)
MAX_AT = 18
SIDE = {
    0: [(6, "T"), (9, "AT"), (12, "WO"), (15, "Q"), (21, "R")],
    1: [(6, "T"), (8, "K0"), (10, "K1"), (12, "K2"), (14, "K3"), (16, "Q"), (21, "R")],
    2: [(6, "T"), (8, "V0"), (10, "V1"), (12, "V2"), (14, "V3"), (16, "Q"), (21, "R")],
    3: [(6, "T"), (16, "Q"), (21, "R")],
}


def side_items(first, last):
    out, n = [], 0
    for g in range(G):
        here = {}
        for unit, item in SIDE[g]:
            if first and g == 0 and item in ("T", "AT", "WO"):
                continue
            if last and (item[0] in "KV" or (item == "Q" and g >= 2) or (item == "R" and g == 3)):
                continue
            here[unit] = (item, n)
            n += 1
        out.append(here)
    return out, n


SIDE_START = 4 + 4 + 2 + 1
N_FIRST, N_MID = side_items(True, False)[1], side_items(False, False)[1]
N_LAST = side_items(False, True)[1]
AFTER_V3 = sum(item[0] != "V" for unit, item in SIDE[2] if unit > 14) + len(SIDE[3])


def side_base(b, first, last):
    if first:
        return SIDE_START
    if last:
        return SIDE_START + N_FIRST + N_MID * (B - 2)
    return SIDE_START + N_FIRST - N_MID + b * N_MID


def chunk_rows(c):
    return LAST if c == KC - 1 else P


def build(nc, t, out):
    top = ExitStack()

    def sb(name, shape, dt=F32, ctx=top):
        return ctx.enter_context(nc.sbuf_tensor(name, shape, dt))

    def psum(name, shape, ctx):
        return ctx.enter_context(nc.psum_tensor(name, shape, F32))

    def sem(name, ctx=top):
        return ctx.enter_context(nc.semaphore(name))

    with top:
        m = {
            "x": sb("x_sb", [P, TOK]),
            "xnT": sb("xnT", [P, TOK]),
            "ident": sb("ident", [P, P]),
            "qmask": sb("qmask", [P, J]),
            "shiftmask": sb("shiftmask", [P, J]),
            "restmask": sb("restmask", [P, J]),
            "tau": sb("tau_all", [P, B]),
            "wffn": sb("wffn", [P, 12288]),
            "nm": sb("nm", [P, QT, 32]),
        }
        split = nc.dram_tensor("delta_split", (2, B, L), F32, kind="Internal").ap()
        weights_in = sem("ffn_weights_in")
        setup(nc, t, m, split, sem, sb, weights_in)
        for layer in (0, 1):
            norm(nc, t, m, f"L{layer}a", False)
            attention(nc, t, m, split, layer)
            if layer == 0:
                quantised_ffn(nc, t, m)
            else:
                norm(nc, t, m, "L1f", False)
                experts(nc, t, m, 1, weights_in, 32)
        norm(nc, t, m, "L2a", False)
        local_attention(nc, t, m, weights_in)
        norm(nc, t, m, "L2f", False)
        experts(nc, t, m, 2, weights_in, 96)
        norm(nc, t, m, "L3a", False)
        attention(nc, t, m, split, 3)
        norm(nc, t, m, "L3f", True)
        experts(nc, t, m, 3, weights_in, 96)
        finish(nc, m, out, sem)


def setup(nc, t, m, split, sem, sb, weights_in):
    with ExitStack() as ctx:
        loaded, stepped, stored = sems = sem("setup_loaded", ctx), sem("setup_stepped", ctx), sem("setup_stored", ctx)
        delta = sb("delta", [B, L], F32, ctx)
        high = sb("delta_high", [B, L], F32R, ctx)
        low = sb("delta_low", [B, L], F32R, ctx)
        ctx.callback(clear, nc, sems)
        block = ctx.enter_context(nc.Block())

        @block.sync
        def _(sp):
            sp.dma_start(delta[:, :], t["fside_BxS2_0"]).then_inc(loaded, 16)
            sp.dma_start(m["x"][:, :].rearrange("p (n d) -> p n d", d=D),
                         t["x"].rearrange("b (n p) d -> p (b n) d", p=P)).then_inc(loaded, 16)
            for name in ("ident", "qmask", "shiftmask", "restmask"):
                sp.dma_start(m[name][:, :], t[name]).then_inc(loaded, 16)
            sp.dma_start(m["tau"][:, :], t["condB_tau"][None, :].to_broadcast([P, B])).then_inc(loaded, 16)
            sp.wait_ge(stepped, 2)
            sp.dma_start(split[0], high[:, :].bitcast(F32)).then_inc(stored, 16)
            sp.dma_start(split[1], low[:, :].bitcast(F32)).then_inc(stored, 16)
            sp.dma_start(m["wffn"][:, 0:E * 1024].rearrange("p (e n) -> p e n", e=E), t["L1_up"]).then_inc(weights_in, 16)
            sp.dma_start(m["wffn"][:, E * 1024:12288].rearrange("p (e n) -> p e n", e=E), t["L1_down"]).then_inc(weights_in, 16)
            sp.wait_ge(stored, 32)
            sp.wait_ge(loaded, 7 * 16)

        @block.vector
        def _(dve):
            dve.wait_ge(loaded, 7 * 16)
            nc.vector.tensor_copy(high[:, :], delta[:, :]).then_inc(stepped, 1)
            dve.wait_ge(stepped, 1)
            nc.vector.tensor_tensor(low[:, :], delta[:, :], high[:, :].bitcast(F32), ALU.subtract).then_inc(stepped, 1)
            nc.vector.memset(m["nm"][:, :, :], 0.0).then_inc(stepped, 1)
            dve.wait_ge(stepped, 3)
            nc.vector.memset(m["nm"][:, :, J:J + 2], 1.0).then_inc(stepped, 1)


def clear(nc, sems):
    with nc.Block() as block:
        @block.sync
        def _(sp):
            for s in sems:
                sp.sem_clear(s)


def finish(nc, m, out, sem):
    stored = sem("out_stored")
    with nc.Block() as block:
        @block.sync
        def _(sp):
            sp.dma_start(out.rearrange("b (n p) d -> p (b n) d", p=P),
                         m["x"][:, :].rearrange("p (n d) -> p n d", d=D)).then_inc(stored, 16)
            sp.wait_ge(stored, 16)


def norm(nc, t, m, tag, rms, xn=None):
    with ExitStack() as ctx:
        def sb(name, shape, dt=F32):
            return ctx.enter_context(nc.sbuf_tensor(f"{tag}_{name}", shape, dt))

        sems = []

        def sem(name):
            sems.append(ctx.enter_context(nc.semaphore(f"{tag}_{name}")))
            return sems[-1]

        turn = xn is None
        xn = sb("xn", [P, TOK]) if turn else xn
        square = sb("square", [P, TOK])
        stat = sb("stat", [P, 8, TILES])
        total, mean, power, spread, rstd = (stat[:, i, :] for i in range(5))
        gain = sb("gain", [P, D])
        banks = [ctx.enter_context(nc.psum_tensor(f"{tag}_ps{i}", [P, 4 * P], F32)) for i in range(4)]
        stepped, squared, rooted, turned, taken, gain_in = (sem(n) for n in ("stepped", "squared", "rooted", "turned", "taken", "gain_in"))
        x3 = m["x"][:, :].rearrange("p (n d) -> p n d", d=D)
        xn3 = xn[:, :].rearrange("p (n d) -> p n d", d=D)
        square3 = square[:, :].rearrange("p (n d) -> p n d", d=D)
        normalised = 11 if rms else 7
        ctx.callback(clear, nc, sems)
        block = ctx.enter_context(nc.Block())

        def per_token(a):
            return a[:, :, None].to_broadcast([P, TILES, D])

        if rms:
            @block.sync
            def _(sp):
                sp.dma_start(gain[:, :], t["L3_ffn_norm_scale"][None, :].to_broadcast([P, D])).then_inc(gain_in, 16)
                sp.wait_ge(gain_in, 16)

        @block.vector
        def _(dve):
            n = 0

            def done(instruction):
                nonlocal n
                n += 1
                instruction.then_inc(stepped, 1)
                dve.wait_ge(stepped, n)

            done(nc.vector.tensor_reduce(total, x3, axis=AX.X, op=ALU.add))
            done(nc.vector.tensor_scalar(mean, total, 1.0 / D, None, ALU.mult))
            done(nc.vector.tensor_tensor(xn3, x3, per_token(mean), ALU.subtract))
            dve.wait_ge(squared, 1)
            done(nc.vector.tensor_reduce(total, square3, axis=AX.X, op=ALU.add))
            done(nc.vector.tensor_scalar(power, total, 1.0 / D, LN_EPS, ALU.mult, ALU.add))
            dve.wait_ge(rooted, 1)
            done(nc.vector.reciprocal(rstd, spread))
            done(nc.vector.tensor_tensor(xn3, xn3, per_token(rstd), ALU.mult))
            if rms:
                dve.wait_ge(squared, 2)
                done(nc.vector.tensor_reduce(total, square3, axis=AX.X, op=ALU.add))
                done(nc.vector.tensor_scalar(power, total, 1.0 / D, RMS_EPS, ALU.mult, ALU.add))
                done(nc.vector.tensor_tensor(m["x"][:, :], m["x"][:, :], xn[:, :], ALU.add))
                dve.wait_ge(rooted, 2)
                nc.vector.reciprocal(rstd, spread).then_inc(taken, 1)
                dve.wait_ge(taken, 1)
                nc.vector.tensor_tensor(xn3, xn3, per_token(rstd), ALU.mult).then_inc(taken, 1)
                dve.wait_ge(taken, 2)
                dve.wait_ge(gain_in, 16)
                done(nc.vector.tensor_tensor(xn3, xn3, gain[:, None, :].to_broadcast([P, TILES, D]), ALU.mult))
            for i in (1, 3) if turn else ():
                dve.wait_ge(turned, i + 1)
                nc.vector.tensor_copy(m["xnT"][:, i * 512:(i + 1) * 512], banks[i][:, :])

        @block.scalar
        def _(act):
            act.wait_ge(stepped, 3)
            nc.scalar.activation(square[:, :], xn[:, :], ACT.Square).then_inc(squared, 1)
            act.wait_ge(stepped, 5)
            nc.scalar.activation(spread, power, ACT.Sqrt).then_inc(rooted, 1)
            if rms:
                act.wait_ge(stepped, 7)
                nc.scalar.activation(square[:, :], xn[:, :], ACT.Square).then_inc(squared, 1)
                act.wait_ge(stepped, 9)
                nc.scalar.activation(spread, power, ACT.Sqrt).then_inc(rooted, 1)
            for i in (0, 2) if turn else ():
                act.wait_ge(turned, i + 1)
                nc.scalar.activation(m["xnT"][:, i * 512:(i + 1) * 512], banks[i][:, :], ACT.Copy)

        @block.tensor
        def _(pe):
            pe.wait_ge(stepped, normalised)
            for i in range(4) if turn else ():
                for k in range(4):
                    tile = 4 * i + k
                    last = nc.tensor.transpose(banks[i][:, k * P:(k + 1) * P], xn[:, tile * P:(tile + 1) * P], m["ident"][:, :])
                last.then_inc(turned, 1)


def attention(nc, t, m, split, layer):
    tag = f"L{layer}"
    with ExitStack() as ctx:
        def sb(name, shape, dt=F32):
            return ctx.enter_context(nc.sbuf_tensor(f"{tag}_{name}", shape, dt))

        sems = []

        def sem(name):
            sems.append(ctx.enter_context(nc.semaphore(f"{tag}_{name}")))
            return sems[-1]

        def psum(name, shape):
            return ctx.enter_context(nc.psum_tensor(f"{tag}_{name}", shape, F32))

        ident = m["ident"]
        wq = sb("wq", [P, G, 3, ROWS])
        wk, wv, wo = sb("wk", [P, D]), sb("wv", [P, D]), sb("wo", [P, D])
        bq = sb("bq", [3 * ROWS, G])
        taubq = sb("taubq", [3 * ROWS, G, B])
        bk = sb("bk", [P, 1])
        bv, bo = sb("bv", [P, D]), sb("bo", [P, D])
        ctxT = sb("ctxT", [P, L])
        khigh, klow = sb("khigh", [P, L], F32R), sb("klow", [P, L], F32R)
        kst = [sb(f"kst{g}", [P, L], F32R) for g in range(G)]
        qst = [sb(f"qst{g}", [P, J, S], F32R) for g in range(G)]
        tq = [sb(f"tq{i}", [3 * ROWS, S]) for i in range(2)]
        tqh = sb("tqh", [3 * ROWS, S], F32R)
        vc = sb("vc", [P, KC, D])
        vx = sb("vx", [P, H, KC, 32])
        probs = [sb(f"probs{i}", [P, 2 * S]) for i in range(4)]
        partmax = sb("partmax", [P, QT, J, 2])
        nm = m["nm"]
        osb = sb("osb", [P, S])
        rcp = sb("rcp", [P, QT, J])
        att, attb = sb("att", [P, QT, D]), sb("attb", [P, QT, D])
        attT = sb("attT", [P, S])
        wotmp = sb("wotmp", [P, S])

        guard_ps = [psum(f"guard{i}", [P, 1024]) for i in range(2)]
        score_ps = [psum(f"score{i}", [P, 512]) for i in range(2)]
        o_ps = psum("o_ps", [P, 512])
        side = psum("side", [P, 512])

        w_in = sem("w_in")
        ctx_in = sem("ctx_in")
        kst_in = [sem(f"kst_in{g}") for g in range(G)]
        side_ready, side_taken = sem("side_ready"), sem("side_taken")
        guard_scored, guard_reduced = sem("guard_scored"), sem("guard_reduced")
        scores_ready, exp_done, pv_done = sem("scores_ready"), sem("exp_done"), sem("pv_done")
        o_taken = sem("o_taken")
        max_ready, shift_ready = sem("max_ready"), sem("shift_ready")
        khigh_ready, klow_ready = sem("khigh_ready"), sem("klow_ready")
        tq_ready, tq_high, tq_split = sem("tq_ready"), sem("tq_high"), sem("tq_split")
        qst_ready = sem("qst_ready")
        rcp_ready, att_done, attb_ready, attT_ready = sem("rcp_ready"), sem("att_done"), sem("attb_ready"), sem("attT_ready")
        wo_taken, x_added = sem("wo_taken"), sem("x_added")
        vx_ready, vx_cleared, spread_turn = sem("vx_ready"), sem("vx_cleared"), sem("spread_turn")
        taubq_ready, kst_cleared = sem("taubq_ready"), sem("kst_cleared")
        ctx.callback(clear, nc, sems)
        block = ctx.enter_context(nc.Block())

        LOADS = 3 * G + 3 + 1 + 1 + 2

        def step(b, g):
            return b * G + g

        def keys(c):
            return slice(c * P, c * P + chunk_rows(c))

        @block.sync
        def _(sp):
            for g in range(G):
                for r in range(3):
                    sp.dma_start(wq[:, g, r, :], t[f"{tag}_WqT"][:, g * ROWS:(g + 1) * ROWS]).then_inc(w_in, 16)
            for name, where in (("Wk", wk), ("Wv", wv), ("Wo", wo)):
                sp.dma_start(where[:, :], t[f"{tag}_{name}T"]).then_inc(w_in, 16)
            sp.dma_start(bq[:, :], t[f"{tag}_bq_rows"]).then_inc(w_in, 16)
            sp.dma_start(bk[:, :], t[f"{tag}_xcond_bk"][:, None]).then_inc(w_in, 16)
            sp.dma_start(bv[:, :], t[f"{tag}_xcond_bv"][None, :].to_broadcast([P, D])).then_inc(w_in, 16)
            sp.dma_start(bo[:, :], t[f"{tag}_xcond_bo"][None, :].to_broadcast([P, D])).then_inc(w_in, 16)

            def load_context(b):
                sp.dma_start(ctxT[:, :], t["ctxT"][bass.ds(b, 1), :, :].rearrange("o p l -> (o p) l")).then_inc(ctx_in, 16)

            def fill_stack(b, g):
                rows = slice(g * ROWS, (g + 1) * ROWS)
                for r, part in enumerate((khigh, klow, khigh)):
                    sp.dma_start(kst[g][r * ROWS:(r + 1) * ROWS, :].bitcast(F32), part[rows, :].bitcast(F32)).then_inc(kst_in[g], 16)
                sp.dma_start(kst[g][100:102, :].bitcast(F32), split[:, bass.ds(b, 1), :].rearrange("a o l -> (a o) l")).then_inc(kst_in[g], 16)

            load_context(0)
            sp.wait_ge(klow_ready, 4)
            sp.wait_ge(kst_cleared, G)
            for g in range(G):
                fill_stack(0, g)

            def batch(b, first, last):
                if not first:
                    sp.wait_ge(scores_ready, step(b, 0) * UNITS)
                    fill_stack(b, 3)
                if last:
                    return
                sp.wait_ge(side_ready, 8 if first else side_base(b, first, last) - AFTER_V3)
                load_context(b + 1)
                sp.wait_ge(klow_ready, 4 * b + 8)
                sp.wait_ge(scores_ready, step(b, 1) * UNITS)
                fill_stack(b + 1, 0)
                for g in (1, 2):
                    sp.wait_ge(scores_ready, step(b, g + 1) * UNITS)
                    fill_stack(b + 1, g)

            batch(0, True, False)
            with sp.Fori(1, B - 1) as b:
                batch(b, False, False)
            batch(B - 1, False, True)
            sp.wait_ge(w_in, LOADS * 16)

        @block.tensor
        def _(pe):
            def wait_side(n):
                pe.wait_ge(side_taken, n)

            def item(name, b, g, n):
                if not (name == "K0" and isinstance(n, int) and n == 0):
                    wait_side(n)
                if name[0] == "K":
                    c = int(name[1])
                    if c == 0:
                        pe.wait_ge(ctx_in, 16 * b + 32)
                    width = min(512, L - 512 * c)
                    last = nc.tensor.matmul(side[:, 0:width], wk[:, :], ctxT[:, 512 * c:512 * c + width], start=True, stop=True)
                elif name[0] == "V":
                    v = int(name[1])
                    for i, c in enumerate(range(4 * v, min(4 * v + 4, KC))):
                        last = nc.tensor.matmul(side[0:chunk_rows(c), i * P:(i + 1) * P], ctxT[:, keys(c)], wv[:, :], start=True, stop=True)
                elif name == "Q":
                    g2, b2 = (g + 2) % G, b + (g + 2) // G
                    last = nc.tensor.matmul(side[0:3 * ROWS, 0:S], wq[:, g2, :, :].rearrange("p r c -> p (r c)"),
                                            m["xnT"][:, bass.ds(b2 * S, S)], start=True, stop=True)
                elif name == "R":
                    pe.wait_ge(max_ready, step(b, g) + 2)
                    for q in range(QT):
                        last = nc.tensor.matmul(side[96:128, q * P:(q + 1) * P], nm[:, q, :], ident[:, :], start=True, stop=True)
                elif name == "T":
                    pe.wait_ge(o_taken, step(b, g))
                    for q in range(QT):
                        last = nc.tensor.transpose(side[:, q * P:(q + 1) * P], osb[:, q * P:(q + 1) * P], ident[:, :])
                elif name == "AT":
                    pe.wait_ge(attb_ready, b)
                    for q in range(QT):
                        last = nc.tensor.transpose(side[:, q * P:(q + 1) * P], attb[:, q, :], ident[:, :])
                elif name == "WO":
                    pe.wait_ge(attT_ready, b)
                    for q in range(QT):
                        last = nc.tensor.matmul(side[:, q * P:(q + 1) * P], attT[:, q * P:(q + 1) * P], wo[:, :], start=True, stop=True)
                last.then_inc(side_ready, 1)

            def guard(s, g, k):
                j, q, half = k // (2 * QT), k // 2 % QT, k % 2
                if k >= 2:
                    pe.wait_ge(guard_reduced, s * GUARD_TILES + k - 1)
                elif not (isinstance(s, int) and s == 0):
                    pe.wait_ge(guard_reduced, s * GUARD_TILES + k - 1)
                ps, q_side = guard_ps[half], qst[g][:, j, q * P:(q + 1) * P]
                if half == 0:
                    nc.tensor.matmul(ps[:, 0:512], q_side, kst[g][:, 0:512], start=True, stop=True)
                    last = nc.tensor.matmul(ps[:, 512:1024], q_side, kst[g][:, 512:1024], start=True, stop=True)
                else:
                    nc.tensor.matmul(ps[:, 0:512], q_side, kst[g][:, 1024:1536], start=True, stop=True)
                    last = nc.tensor.matmul(ps[:, 512:512 + LAST + 1], q_side, kst[g][:, L - LAST - 1:L], start=True, stop=True)
                last.then_inc(guard_scored, 1)

            def values(s, g, u):
                c, pair = u // 2, u % 2
                pe.wait_ge(exp_done, s * UNITS + u + 1)
                n = chunk_rows(c)
                for i in range(2):
                    j = 2 * pair + i
                    last = nc.tensor.matmul(o_ps[32 * j:32 * j + 32, 0:S], vx[0:n, g * J + j, c, :],
                                            probs[(2 * g + u) % 4][0:n, i * S:(i + 1) * S], start=c == 0, stop=c == KC - 1)
                last.then_inc(pv_done, 1)

            pe.wait_ge(w_in, LOADS * 16)
            for n, name in enumerate(["K0", "K1", "K2", "K3", "V0", "V1", "V2", "V3"]):
                item(name, -1, 1, n)
            for n, s in ((8, 0), (9, 1)):
                item("Q", 0, s - 2, n)
            pe.wait_ge(kst_in[0], 64)
            pe.wait_ge(qst_ready, 2)
            for k in range(GUARD_TILES):
                guard(0, 0, k)
            item("R", 0, -1, 10)

            def batch(b, first, last):
                items, _ = side_items(first, last)
                base = side_base(b, first, last)
                for g in range(G):
                    s, g1 = step(b, g), (g + 1) % G
                    more = not (last and g == G - 1)
                    for u in range(UNITS):
                        if u in items[g]:
                            name, n = items[g][u]
                            item(name, b, g, base + n)
                        if u in GUARD_AT and more:
                            if u == min(GUARD_AT):
                                b1 = b + (g + 1) // G
                                pe.wait_ge(kst_in[g1], 64 * b1 + 64)
                                pe.wait_ge(qst_ready, 2 * s + 4)
                            for k in GUARD_AT[u]:
                                guard(s + 1, g1, k)
                        if u == 0:
                            pe.wait_ge(shift_ready, s + 1)
                        if not (first and g == 0 and u < 2):
                            pe.wait_ge(exp_done, s * UNITS + u - 1)
                        c, pair = u // 2, u % 2
                        nc.tensor.matmul(score_ps[u % 2][0:chunk_rows(c), :], kst[g][:, keys(c)],
                                         qst[g][:, 2 * pair:2 * pair + 2, :].rearrange("p j q -> p (j q)"),
                                         start=True, stop=True).then_inc(scores_ready, 1)
                        if u >= LAG:
                            if u == LAG:
                                pe.wait_ge(vx_ready, s + 1)
                                if not (first and g == 0):
                                    pe.wait_ge(o_taken, s)
                            values(s, g, u - LAG)
                        elif not (first and g == 0):
                            values(s - 1, (g - 1) % G, UNITS - LAG + u)

            batch(0, True, False)
            with pe.Fori(1, B - 1) as b:
                batch(b, False, False)
            batch(B - 1, False, True)
            for u in range(UNITS - LAG, UNITS):
                values(B * G - 1, G - 1, u)
            n = SIDE_START + N_FIRST + N_MID * (B - 2) + N_LAST
            for i, name in enumerate(("T", "AT", "WO")):
                item(name, B, 0, n + i)

        @block.scalar
        def _(act):
            def item(name, b, g, n):
                if name[0] in "KVQ" or name == "AT":
                    act.wait_ge(side_ready, n + 1)
                if name[0] == "K":
                    c = int(name[1])
                    width = min(512, L - 512 * c)
                    if c == 0 and not (isinstance(b, int) and b == -1):
                        act.wait_ge(kst_in[3], 64 * b + 64)
                    nc.scalar.activation(khigh[:, 512 * c:512 * c + width], side[:, 0:width], ACT.Identity,
                                         bias=bk[:, 0:1]).then_inc(khigh_ready, 1)
                elif name[0] == "V":
                    v = int(name[1])
                    if v == 0:
                        act.wait_ge(vx_cleared, 2) if isinstance(b, int) and b == -1 else act.wait_ge(vx_ready, b * G + G)
                    if v < 3:
                        copied = nc.scalar.activation(vc[:, 4 * v:4 * v + 4, :].rearrange("p c d -> p (c d)"), side[:, :], ACT.Copy)
                    else:
                        copied = nc.scalar.activation(vc[0:LAST, KC - 1, :], side[0:LAST, 0:D], ACT.Copy)
                    copied.then_inc(side_taken, 1)
                elif name == "Q":
                    g2, b2 = (g + 2) % G, b + (g + 2) // G
                    s2 = step(b, g) + 2
                    if not (isinstance(s2, int) and s2 < 2):
                        act.wait_ge(qst_ready, 2 * (s2 - 1))
                    nc.scalar.activation(tq[g2 % 2][:, :], side[0:3 * ROWS, 0:S], ACT.Identity,
                                         scale=m["tau"][0:3 * ROWS, bass.ds(b2, 1)],
                                         bias=taubq[:, g2, bass.ds(b2, 1)]).then_inc(tq_ready, 1)
                elif name == "AT":
                    if not (isinstance(b, int) and b == 1):
                        act.wait_ge(wo_taken, b - 1)
                    nc.scalar.activation(attT[:, :], side[:, 0:S], ACT.Copy).then_inc(attT_ready, 1)
                    act.wait_ge(attT_ready, b)
                    nc.scalar.sem_inc(side_taken, 1)

            def take_output(s):
                act.wait_ge(pv_done, s * UNITS + UNITS)
                if not (isinstance(s, int) and s == 0):
                    act.wait_ge(att_done, s)
                nc.scalar.activation(osb[:, :], o_ps[:, 0:S], ACT.Copy).then_inc(o_taken, 1)

            act.wait_ge(w_in, LOADS * 16)
            act.wait_ge(taubq_ready, 1)
            for n, name in enumerate(["K0", "K1", "K2", "K3", "V0", "V1", "V2", "V3"]):
                item(name, -1, 1, n)
            for n, s in ((8, 0), (9, 1)):
                item("Q", 0, s - 2, n)

            def batch(b, first, last):
                items, _ = side_items(first, last)
                base = side_base(b, first, last)
                for g in range(G):
                    s = step(b, g)
                    for u in range(UNITS):
                        c = u // 2
                        act.wait_ge(scores_ready, s * UNITS + u + 1)
                        if not (first and g == 0 and u < 4):
                            act.wait_ge(pv_done, s * UNITS + u - 3)
                        n = chunk_rows(c)
                        nc.scalar.activation(probs[(2 * g + u) % 4][0:n, :], score_ps[u % 2][0:n, :], ACT.Exp,
                                             scale=float(DK) ** -0.5).then_inc(exp_done, 1)
                        if u == LAG - 1 and not (first and g == 0):
                            take_output(s - 1)
                        if u in items[g]:
                            name, n = items[g][u]
                            item(name, b, g, base + n)

            batch(0, True, False)
            with act.Fori(1, B - 1) as b:
                batch(b, False, False)
            batch(B - 1, False, True)
            take_output(B * G - 1)
            item("AT", B, 0, SIDE_START + N_FIRST + N_MID * (B - 2) + N_LAST + 1)

        @block.vector
        def _(dve):
            def item(name, b, g, n):
                if name[0] == "K":
                    c = int(name[1])
                    width = min(512, L - 512 * c)
                    dve.wait_ge(khigh_ready, 4 * b + 4 + c + 1)
                    at = slice(512 * c, 512 * c + width)
                    nc.vector.scalar_tensor_tensor(klow[:, at], side[:, 0:width], bk[:, 0:1], khigh[:, at].bitcast(F32),
                                                   ALU.add, ALU.subtract).then_inc(klow_ready, 1)
                    dve.wait_ge(klow_ready, 4 * b + 4 + c + 1)
                    nc.vector.sem_inc(side_taken, 1)
                elif name == "Q":
                    s2 = step(b, g) + 2
                    x = tq[(g + 2) % 2]
                    dve.wait_ge(tq_ready, s2 + 1)
                    low = slice(2 * ROWS, 3 * ROWS)
                    if not (isinstance(s2, int) and s2 == 0):
                        dve.wait_ge(tq_split, s2)
                    nc.vector.tensor_copy(tqh[low, :], x[low, :]).then_inc(tq_high, 1)
                    dve.wait_ge(tq_high, s2 + 1)
                    nc.vector.tensor_tensor(x[low, :], x[low, :], tqh[low, :].bitcast(F32), ALU.subtract).then_inc(tq_split, 1)
                    nc.vector.sem_inc(side_taken, 1)
                elif name == "R":
                    g1 = (g + 1) % G
                    dve.wait_ge(side_ready, n + 1)
                    nc.vector.tensor_tensor(qst[g1][96:128, :, :], side[96:128, None, 0:S].to_broadcast([32, J, S]),
                                            m["shiftmask"][96:128, :, None].to_broadcast([32, J, S]), ALU.mult)\
                        .then_inc(shift_ready, 1)
                    dve.wait_ge(shift_ready, step(b, g) + 2)
                    nc.vector.sem_inc(side_taken, 1)
                elif name == "T":
                    g0 = (g - 1) % G
                    s0 = step(b, g) - 1
                    dve.wait_ge(side_ready, n + 1)
                    turned = side[:, 0:S].rearrange("p (q j r) -> p q j r", q=QT, r=32)
                    nc.vector.reciprocal(rcp[:, :, :], turned[:, :, :, DK]).then_inc(rcp_ready, 1)
                    dve.wait_ge(rcp_ready, s0 + 1)
                    if g0 == 0 and not (isinstance(b, int) and b == 0):
                        dve.wait_ge(attb_ready, b)
                    for q in range(QT):
                        last = nc.vector.tensor_tensor(att[:, q, g0 * ROWS:(g0 + 1) * ROWS].rearrange("p (j e) -> p j e", e=DK),
                                                       turned[:, q, :, 0:DK], rcp[:, q, :, None].to_broadcast([P, J, DK]), ALU.mult)
                    last.then_inc(att_done, 1)
                    dve.wait_ge(att_done, s0 + 1)
                    nc.vector.sem_inc(side_taken, 1)
                    if g0 == G - 1:
                        nc.vector.tensor_tensor(attb[:, :, :], att[:, :, :], bv[:, None, :].to_broadcast([P, QT, D]), ALU.add)\
                            .then_inc(attb_ready, 1)
                elif name == "WO":
                    dve.wait_ge(side_ready, n + 1)
                    nc.vector.tensor_tensor(wotmp[:, :].rearrange("p (q d) -> p q d", q=QT), side[:, 0:S].rearrange("p (q d) -> p q d", q=QT),
                                            bo[:, None, :].to_broadcast([P, QT, D]), ALU.add).then_inc(wo_taken, 1)
                    dve.wait_ge(wo_taken, b)
                    nc.vector.sem_inc(side_taken, 1)
                    xs = m["x"][:, bass.ds((b - 1) * S, S)]
                    nc.vector.tensor_tensor(xs, xs, wotmp[:, :], ALU.add).then_inc(x_added, 1)
                    dve.wait_ge(x_added, b)

            def reduce(s, k):
                j, q, half = k // (2 * QT), k // 2 % QT, k % 2
                width = GUARD_SPLIT if half == 0 else 512 + LAST + 1
                if k == 0 and not (isinstance(s, int) and s == 0):
                    dve.wait_ge(max_ready, s)
                dve.wait_ge(guard_scored, s * GUARD_TILES + k + 1)
                nc.vector.tensor_reduce(partmax[:, q, j, half:half + 1], guard_ps[half][:, 0:width], axis=AX.X, op=ALU.max)\
                    .then_inc(guard_reduced, 1)

            def join(s):
                dve.wait_ge(guard_reduced, s * GUARD_TILES + GUARD_TILES)
                nc.vector.tensor_tensor(nm[:, :, 0:J], partmax[:, :, :, 0], partmax[:, :, :, 1], ALU.max).then_inc(max_ready, 1)

            dve.wait_ge(w_in, LOADS * 16)
            for g in range(G):
                last = nc.vector.tensor_scalar(taubq[:, g, :], m["tau"][0:3 * ROWS, :], bq[:, g:g + 1], None, ALU.mult)
            last.then_inc(taubq_ready, 1)
            for g in range(G):
                nc.vector.tensor_copy(kst[g][96:128, :], m["restmask"][96:128, 0:1].to_broadcast([32, L])).then_inc(kst_cleared, 1)
            for n, name in enumerate(["K0", "K1", "K2", "K3"]):
                item(name, -1, 1, n)
            for n, s in ((8, 0), (9, 1)):
                item("Q", 0, s - 2, n)
            for k in range(GUARD_TILES):
                reduce(0, k)
            join(0)
            item("R", 0, -1, 10)

            def batch(b, first, last):
                items, _ = side_items(first, last)
                base = side_base(b, first, last)
                for g in range(G):
                    s = step(b, g)
                    for u in range(UNITS):
                        if u in GUARD_AT and not (last and g == G - 1):
                            for k in GUARD_AT[u]:
                                reduce(s + 1, k)
                        if u == MAX_AT and not (last and g == G - 1):
                            join(s + 1)
                        if u in items[g]:
                            name, n = items[g][u]
                            item(name, b, g, base + n)

            batch(0, True, False)
            with dve.Fori(1, B - 1) as b:
                batch(b, False, False)
            batch(B - 1, False, True)
            n = SIDE_START + N_FIRST + N_MID * (B - 2) + N_LAST
            item("T", B, 0, n)
            item("WO", B, 0, n + 2)

        @block.gpsimd
        def _(pool):
            def spread(b, g, stacks):
                pool.wait_ge(qst_ready, 2 * stacks)
                if not (isinstance(b, int) and b == 0 and g == 0):
                    pool.wait_ge(vx_ready, step(b, g))
                nc.gpsimd.sem_inc(spread_turn, 1)
                nc.gpsimd.tensor_copy(vx[:, g * J:(g + 1) * J, :, 0:DK],
                                      vc[:, :, g * ROWS:(g + 1) * ROWS].rearrange("p c (j e) -> p j c e", e=DK)).then_inc(vx_ready, 1)

            def stack(b, g):
                g2, s2 = (g + 2) % G, step(b, g) + 2
                pool.wait_ge(tq_split, s2 + 1)
                if not (isinstance(s2, int) and s2 < G):
                    pool.wait_ge(scores_ready, (s2 - 3) * UNITS)
                if not (isinstance(s2, int) and s2 == 0):
                    pool.wait_ge(qst_ready, 2 * s2)
                if g >= 0:
                    pool.wait_ge(vx_ready, G * b + G)
                nc.gpsimd.tensor_tensor(qst[g2][96:128, :, :], m["ident"][96:128, None, 0:1].to_broadcast([32, J, S]),
                                        m["restmask"][96:128, 1:2, None].to_broadcast([32, J, S]), ALU.add).then_inc(qst_ready, 1)
                pool.wait_ge(qst_ready, 2 * s2 + 1)
                nc.gpsimd.tensor_tensor(qst[g2][0:3 * ROWS, :, :], tq[g2 % 2][:, None, :].to_broadcast([3 * ROWS, J, S]),
                                        m["qmask"][0:3 * ROWS, :, None].to_broadcast([3 * ROWS, J, S]), ALU.mult).then_inc(qst_ready, 1)

            nc.gpsimd.memset(vx[:, :, :, :], 1.0).then_inc(vx_cleared, 1)
            pool.wait_ge(vx_cleared, 1)
            nc.gpsimd.memset(vc[:, :, :], 0.0).then_inc(vx_cleared, 1)
            pool.wait_ge(vx_cleared, 2)
            stack(0, -2)
            stack(0, -1)
            pool.wait_ge(side_taken, 8)
            for g in range(G):
                spread(0, g, 2)

            def batch(b, first, last):
                items, _ = side_items(first, last)
                base = side_base(b, first, last)
                for g in range(G):
                    if g == 0 and not first:
                        pool.wait_ge(pv_done, step(b, 0) * UNITS)
                        spread(b, 3, G * b + 2)
                    if not (last and g >= 2):
                        stack(b, g)
                    if g == 3 and not last:
                        n = [n for here in items for name, n in here.values() if name == "V3"][0]
                        pool.wait_ge(side_taken, base + n + 1)
                        for i in range(3):
                            pool.wait_ge(pv_done, step(b, i + 1) * UNITS)
                            spread(b + 1, i, G * b + 6)

            batch(0, True, False)
            with pool.Fori(1, B - 1) as b:
                batch(b, False, False)
            batch(B - 1, False, True)


def quantised_ffn(nc, t, m):
    HID, HC = 512, 4
    N_W = HID * D
    outer = ExitStack()
    with outer:
        xn = outer.enter_context(nc.sbuf_tensor("q_xn", [P, TOK], F32))
        norm(nc, t, m, "L0f", False, xn)
        ctx = outer

        def sb(name, shape, dt=F32):
            return ctx.enter_context(nc.sbuf_tensor(f"q_{name}", shape, dt))

        sems = []

        def sem(name):
            sems.append(ctx.enter_context(nc.semaphore(f"q_{name}")))
            return sems[-1]

        def psum(name, shape, dt=F32):
            return ctx.enter_context(nc.psum_tensor(f"q_{name}", shape, dt))

        w = sb("w", [P, 2, HID])
        scratch = sb("scratch", [P, TOK])
        wq = sb("wq", [P, 2, HID], BF16)
        identb = sb("identb", [P, P], BF16)
        ones = sb("ones", [P, P])
        wsum, ws, wr = sb("wsum", [P, 2]), sb("ws", [P, 2]), sb("wr", [P, 2])
        amax, xr, xs = sb("amax", [P, TILES]), sb("xr", [P, TILES]), sb("xs", [P, TILES])
        hscale = sb("hscale", [P, TILES])
        xq, xqT = sb("xq", [P, TOK], BF16), sb("xqT", [P, TOK], BF16)
        h = [sb(f"h{i}", [P, HID]) for i in range(2)]
        hr = [sb(f"hr{i}", [P, HID]) for i in range(2)]
        hq = [sb(f"hq{i}", [P, HID], BF16) for i in range(2)]
        hqT = [sb(f"hqT{i}", [P, HID], BF16) for i in range(2)]
        hmax = [sb(f"hmax{i}", [P, 4]) for i in range(2)]
        xT_ps = psum("xT_ps", [P, TOK], BF16)
        h_ps = [psum(f"h_ps{i}", [P, HID]) for i in range(2)]
        t_ps = [psum(f"t_ps{i}", [P, 1024], BF16) for i in range(2)]
        y_ps = [psum(f"y_ps{i}", [P, 512]) for i in range(2)]
        w_in, stepped, summed, totals, absolute, turned_x, xqT_ready = (
            sem(n) for n in ("w_in", "stepped", "summed", "totals", "absolute", "turned_x", "xqT_ready"))
        clip_turn = sem("clip_turn")
        h_ready, gelu_done, hstep, clipped, hq_ready, turned, hqT_ready, y_ready, x_added = (
            sem(n) for n in ("h_ready", "gelu_done", "hstep", "clipped", "hq_ready", "turned", "hqT_ready", "y_ready", "x_added"))
        FINAL_STEP = 14
        HSTEPS = 4
        xn3 = xn[:, :].rearrange("p (n d) -> p n d", d=D)
        sc3 = scratch[:, :].rearrange("p (n d) -> p n d", d=D)
        ctx.callback(clear, nc, sems)
        block = ctx.enter_context(nc.Block())

        @block.sync
        def _(sp):
            sp.dma_start(w[:, 0, :], t["L0_w1T"]).then_inc(w_in, 16)
            sp.dma_start(w[:, 1, :].rearrange("p (c d) -> p c d", c=HC), t["L0_w2T"].rearrange("(c p) d -> p c d", p=P)).then_inc(w_in, 16)
            sp.wait_ge(w_in, 32)

        @block.scalar
        def _(act):
            nc.scalar.activation(scratch[:, :], xn[:, :], ACT.Abs).then_inc(absolute, 1)
            act.wait_ge(w_in, 32)
            for i in range(2):
                nc.scalar.activation(h[i][:, :], w[:, i, :], ACT.Abs, accum_out=wsum[:, i:i + 1]).then_inc(summed, 1)
            act.wait_ge(turned_x, 1)
            nc.scalar.activation(xqT[:, :], xT_ps[:, :], ACT.Copy).then_inc(xqT_ready, 1)
            act.wait_ge(stepped, FINAL_STEP)

            def pair(b, first):
                for i in range(2):
                    n = 2 * b + i
                    act.wait_ge(h_ready, n + 1)
                    if not first:
                        act.wait_ge(hstep, HSTEPS * (n - 1))
                    nc.scalar.activation(h[i][:, :], h_ps[i][:, :], ACT.Gelu, scale=hscale[:, bass.ds(n, 1)]).then_inc(gelu_done, 1)
                for i in range(2):
                    n = 2 * b + i
                    act.wait_ge(turned, n + 1)
                    nc.scalar.activation(hqT[i][:, :], t_ps[i][:, 0:HID], ACT.Copy).then_inc(hqT_ready, 1)

            pair(0, True)
            with act.Fori(1, B) as b:
                pair(b, False)

        @block.vector
        def _(dve):
            k = 0

            def done(instruction):
                nonlocal k
                k += 1
                instruction.then_inc(stepped, 1)
                dve.wait_ge(stepped, k)

            done(nc.vector.memset(ones[:, :], 1.0))
            done(nc.vector.tensor_copy(identb[:, :], m["ident"][:, :]))
            dve.wait_ge(absolute, 1)
            done(nc.vector.tensor_reduce(amax[:, :], sc3, axis=AX.X, op=ALU.max))
            done(nc.vector.tensor_scalar(amax[:, :], amax[:, :], Q_EPS, None, ALU.max))
            done(nc.vector.reciprocal(xr[:, :], amax[:, :]))
            done(nc.vector.tensor_scalar(xs[:, :], xr[:, :], 127.0, None, ALU.mult))
            done(nc.vector.tensor_tensor(sc3, xn3, xs[:, :, None].to_broadcast([P, TILES, D]), ALU.mult))
            done(nc.vector.tensor_scalar(scratch[:, :], scratch[:, :], ROUND, ROUND, ALU.add, ALU.subtract))
            done(nc.vector.tensor_scalar(xq[:, :], scratch[:, :], 127.0, -128.0, ALU.min, ALU.max))
            dve.wait_ge(totals, 1)
            done(nc.vector.tensor_scalar(ws[:, :], y_ps[0][:, 0:2], 1.0 / N_W, Q_EPS, ALU.mult, ALU.max))
            done(nc.vector.reciprocal(wr[:, :], ws[:, :]))
            for i in range(2):
                nc.vector.tensor_scalar(w[:, i, :], w[:, i, :], wr[:, i:i + 1], ROUND, ALU.mult, ALU.add).then_inc(totals, 1)
                dve.wait_ge(totals, 2 + 2 * i)
                nc.vector.tensor_scalar(w[:, i, :], w[:, i, :], ROUND, -1.0, ALU.subtract, ALU.max).then_inc(totals, 1)
                dve.wait_ge(totals, 3 + 2 * i)
                last = nc.vector.tensor_scalar(wq[:, i, :], w[:, i, :], 1.0, None, ALU.min)
            done(last)
            done(nc.vector.tensor_scalar(hscale[:, :], amax[:, :], ws[:, 0:1], 1.0 / 127.0, ALU.mult, ALU.mult))
            done(nc.vector.tensor_scalar(ws[:, :], ws[:, :], 1.0 / 127.0, None, ALU.mult))
            assert k == FINAL_STEP

            def pair(b, first):
                for i in range(2):
                    n = 2 * b + i
                    q = hmax[i]
                    dve.wait_ge(gelu_done, n + 1)
                    nc.vector.tensor_reduce(q[:, 0:1], h[i][:, :], axis=AX.X, op=ALU.max, apply_absolute_value=True).then_inc(hstep, 1)
                    dve.wait_ge(hstep, HSTEPS * n + 1)
                    nc.vector.tensor_scalar(q[:, 1:2], q[:, 0:1], Q_EPS, None, ALU.max).then_inc(hstep, 1)
                    dve.wait_ge(hstep, HSTEPS * n + 2)
                    nc.vector.reciprocal(q[:, 2:3], q[:, 1:2]).then_inc(hstep, 1)
                    dve.wait_ge(hstep, HSTEPS * n + 3)
                    nc.vector.tensor_scalar(hr[i][:, :], h[i][:, :], q[:, 2:3], 127.0, ALU.mult, ALU.mult).then_inc(hstep, 1)
                    dve.wait_ge(hstep, HSTEPS * n + 4)
                    nc.vector.tensor_scalar(hr[i][:, :], hr[i][:, :], ROUND, ROUND, ALU.add, ALU.subtract).then_inc(clipped, 1)
                    nc.vector.tensor_scalar(q[:, 3:4], q[:, 1:2], ws[:, 1:2], None, ALU.mult).then_inc(clipped, 1)
                for i in range(2):
                    n = 2 * b + i
                    xt = m["x"][:, bass.ds(n * P, P)]
                    dve.wait_ge(y_ready, n + 1)
                    dve.wait_ge(clipped, 2 * n + 2)
                    nc.vector.scalar_tensor_tensor(xt, y_ps[i][:, 0:D], hmax[i][:, 3:4], xt, ALU.mult, ALU.add).then_inc(x_added, 1)
                dve.wait_ge(x_added, 2 * b + 2)

            pair(0, True)
            with dve.Fori(1, B) as b:
                pair(b, False)

        @block.gpsimd
        def _(pool):
            def pair(b, first):
                for i in range(2):
                    n = 2 * b + i
                    pool.wait_ge(clipped, 2 * n + 1)
                    if not first:
                        pool.wait_ge(turned, n - 1)
                    nc.gpsimd.sem_inc(clip_turn, 1)
                    nc.gpsimd.tensor_scalar(hq[i][:, :], hr[i][:, :], 127.0, -128.0, ALU.min, ALU.max).then_inc(hq_ready, 1)

            pair(0, True)
            with pool.Fori(1, B) as b:
                pair(b, False)

        @block.tensor
        def _(pe):
            pe.wait_ge(stepped, 9)
            for i in range(TILES):
                last = nc.tensor.transpose(xT_ps[:, i * P:(i + 1) * P], xq[:, i * P:(i + 1) * P], identb[:, :])
            last.then_inc(turned_x, 1)
            pe.wait_ge(summed, 2)
            nc.tensor.matmul(y_ps[0][:, 0:2], ones[:, :], wsum[:, :], start=True, stop=True).then_inc(totals, 1)
            pe.wait_ge(stepped, FINAL_STEP)
            pe.wait_ge(xqT_ready, 1)

            def pair(b, first):
                for i in range(2):
                    n = 2 * b + i
                    if not first:
                        pe.wait_ge(gelu_done, n - 1)
                    nc.tensor.matmul(h_ps[i][:, :], xqT[:, bass.ds(n * P, P)], wq[:, 0, :], start=True, stop=True).then_inc(h_ready, 1)
                for i in range(2):
                    n = 2 * b + i
                    pe.wait_ge(hq_ready, n + 1)
                    if not first:
                        pe.wait_ge(hqT_ready, n - 1)
                    for c in range(HC):
                        last = nc.tensor.transpose(t_ps[i][:, c * P:(c + 1) * P], hq[i][:, c * P:(c + 1) * P], identb[:, :])
                    last.then_inc(turned, 1)
                for i in range(2):
                    n = 2 * b + i
                    pe.wait_ge(hqT_ready, n + 1)
                    if not first:
                        pe.wait_ge(x_added, n - 1)
                    for c in range(HC):
                        last = nc.tensor.matmul(y_ps[i][:, 0:D], hqT[i][:, c * P:(c + 1) * P], wq[:, 1, c * P:(c + 1) * P],
                                                start=c == 0, stop=c == HC - 1)
                    last.then_inc(y_ready, 1)

            pair(0, True)
            with pe.Fori(1, B) as b:
                pair(b, False)


MIXTURES = {
    1: dict(chunks=4, up=1024, gated=0, linear=512, up_at=0, down_at=E * 1024),
    2: dict(chunks=1, up=256, gated=0, linear=128, up_at=0, down_at=E * 256),
    3: dict(chunks=2, up=512, gated=256, linear=0, up_at=E * 384, down_at=E * 896),
}


def route(nc, t, m, layer, shareT):
    tag = f"r{layer}"
    with ExitStack() as ctx:
        def sb(name, shape, dt=F32):
            return ctx.enter_context(nc.sbuf_tensor(f"{tag}_{name}", shape, dt))

        sems = []

        def sem(name):
            sems.append(ctx.enter_context(nc.semaphore(f"{tag}_{name}")))
            return sems[-1]

        gate = sb("gate", [P, E])
        number = sb("number", [P, E])
        score, share, other = (sb(n, [P, TILES, E]) for n in ("score", "share", "other"))
        best, where = sb("best", [P, TILES, 8]), sb("where", [P, TILES, 8], U32)
        wheref = sb("wheref", [P, TILES, 2])
        small = sb("small", [P, 6, TILES])
        a, b_, c_, w1, w2, d_ = (small[:, i, :] for i in range(6))
        s_ps = ctx.enter_context(nc.psum_tensor(f"{tag}_s_ps", [P, TILES * E], F32))
        t_ps = [ctx.enter_context(nc.psum_tensor(f"{tag}_t_ps{i}", [P, 512], F32)) for i in range(4)]
        loaded, scored, stepped, raised, turned = (sem(n) for n in ("loaded", "scored", "stepped", "raised", "turned"))
        softmax_first = layer == 2
        ctx.callback(clear, nc, sems)
        block = ctx.enter_context(nc.Block())

        @block.sync
        def _(sp):
            sp.dma_start(gate[:, :], t[f"L{layer}_gateT"]).then_inc(loaded, 16)
            sp.dma_start(number[:, :], t["numbers"][None, 0:E].to_broadcast([P, E])).then_inc(loaded, 16)
            sp.wait_ge(loaded, 32)

        steps_to_raise = 3 if softmax_first else 2 + 2
        steps = {}

        @block.vector
        def _(dve):
            k = 0

            def done(instruction):
                nonlocal k
                k += 1
                instruction.then_inc(stepped, 1)
                dve.wait_ge(stepped, k)

            def wide(v):
                return v[:, :, None].to_broadcast([P, TILES, E])

            dve.wait_ge(scored, 1)
            done(nc.vector.tensor_copy(score[:, :, :], s_ps[:, :].rearrange("p (n e) -> p n e", e=E)))
            if softmax_first:
                done(nc.vector.tensor_reduce(a, score[:, :, :], axis=AX.X, op=ALU.max))
                done(nc.vector.tensor_tensor(score[:, :, :], score[:, :, :], wide(a), ALU.subtract))
                dve.wait_ge(raised, 1)
                done(nc.vector.tensor_reduce(a, other[:, :, :], axis=AX.X, op=ALU.add))
                done(nc.vector.reciprocal(b_, a))
                done(nc.vector.tensor_tensor(score[:, :, :], other[:, :, :], wide(b_), ALU.mult))
            for i in range(TILES):
                last = nc.vector.max(best[:, i, :], score[:, i, :])
            done(last)
            for i in range(TILES):
                last = nc.vector.max_index(where[:, i, :], best[:, i, :], score[:, i, :])
            first, second = best[:, :, 0], best[:, :, 1]
            if softmax_first:
                done(last)
                done(nc.vector.tensor_copy(wheref[:, :, :], where[:, :, 0:2]))
                done(nc.vector.tensor_tensor(a, first, second, ALU.add))
                done(nc.vector.tensor_scalar(a, a, L2_EPS, None, ALU.add))
                done(nc.vector.reciprocal(b_, a))
                done(nc.vector.tensor_tensor(w1, first, b_, ALU.mult))
                done(nc.vector.tensor_tensor(w2, second, b_, ALU.mult))
                done(nc.vector.tensor_tensor(a, w1, w2, ALU.add))
                done(nc.vector.tensor_scalar(a, a, L2_EPS, None, ALU.add))
                done(nc.vector.reciprocal(b_, a))
                done(nc.vector.tensor_tensor(w1, w1, b_, ALU.mult))
                done(nc.vector.tensor_tensor(w2, w2, b_, ALU.mult))
            else:
                done(last)
                done(nc.vector.tensor_tensor(a, second, first, ALU.subtract))
                done(nc.vector.tensor_copy(wheref[:, :, :], where[:, :, 0:2]))
                dve.wait_ge(raised, 1)
                done(nc.vector.tensor_scalar(b_, c_, 1.0, None, ALU.add))
                done(nc.vector.reciprocal(w1, b_))
                done(nc.vector.tensor_tensor(w2, c_, w1, ALU.mult))
            numbers = number[:, None, :].to_broadcast([P, TILES, E])
            done(nc.vector.tensor_tensor(share[:, :, :], numbers, wide(wheref[:, :, 0]), ALU.is_equal))
            done(nc.vector.tensor_tensor(other[:, :, :], numbers, wide(wheref[:, :, 1]), ALU.is_equal))
            done(nc.vector.tensor_tensor(share[:, :, :], share[:, :, :], wide(w1), ALU.mult))
            done(nc.vector.tensor_tensor(other[:, :, :], other[:, :, :], wide(w2), ALU.mult))
            done(nc.vector.tensor_tensor(share[:, :, :], share[:, :, :], other[:, :, :], ALU.add))
            steps["all"] = k
            for i in (1, 3):
                dve.wait_ge(turned, i + 1)
                nc.vector.tensor_copy(shareT[0:E, i * 512:(i + 1) * 512], t_ps[i][0:E, :])

        @block.scalar
        def _(act):
            act.wait_ge(stepped, steps_to_raise)
            if softmax_first:
                nc.scalar.activation(other[:, :, :], score[:, :, :], ACT.Exp).then_inc(raised, 1)
            else:
                nc.scalar.activation(c_, a, ACT.Exp).then_inc(raised, 1)
            for i in (0, 2):
                act.wait_ge(turned, i + 1)
                nc.scalar.activation(shareT[0:E, i * 512:(i + 1) * 512], t_ps[i][0:E, :], ACT.Copy)

        @block.tensor
        def _(pe):
            pe.wait_ge(loaded, 32)
            for i in range(TILES):
                last = nc.tensor.matmul(s_ps[:, i * E:(i + 1) * E], m["xnT"][:, i * P:(i + 1) * P], gate[:, :], start=True, stop=True)
            last.then_inc(scored, 1)
            pe.wait_ge(stepped, steps["all"])
            for i in range(4):
                for k in range(4):
                    last = nc.tensor.transpose(t_ps[i][0:E, k * P:(k + 1) * P], share[:, 4 * i + k, :], m["ident"][:, :])
                last.then_inc(turned, 1)


def experts(nc, t, m, layer, weights_in, arrived):
    shape = MIXTURES[layer]
    NC, tag = shape["chunks"], f"e{layer}"
    W = EXPERT_TOK
    GROUPS = TOK // W
    outer = ExitStack()
    with outer:
        ctx = outer
        shareT = outer.enter_context(nc.sbuf_tensor(f"{tag}_shareT", [E, TOK], F32))
        route(nc, t, m, layer, shareT)

        def sb(name, shape_, dt=F32):
            return ctx.enter_context(nc.sbuf_tensor(f"{tag}_{name}", shape_, dt))

        sems = []

        def sem(name):
            sems.append(ctx.enter_context(nc.semaphore(f"{tag}_{name}")))
            return sems[-1]

        def psum(name):
            return ctx.enter_context(nc.psum_tensor(f"{tag}_{name}", [P, W], F32))

        select = sb("select", [E, E, P])
        xc = [sb(f"xc{i}", [P, W]) for i in range(2)]
        gated = [sb(f"gated{i}", [P, W]) for i in range(2)]
        hid = [sb(f"hid{i}", [P, W]) for i in range(2)]
        ysb = sb("ysb", [P, W])
        share_ps, y_ps, t_ps = psum("share_ps"), psum("y_ps"), psum("t_ps")
        g_ps, l_ps = [psum(f"g_ps{i}") for i in range(2)], [psum(f"l_ps{i}") for i in range(2)]
        select_in, share_ready, xc_ready, gate_ready, linear_ready, silu_done, hid_ready, down_done = (
            sem(n) for n in ("select_in", "share_ready", "xc_ready", "gate_ready", "linear_ready", "silu_done", "hid_ready", "down_done"))
        y_taken, turned, x_added, share_turn = sem("y_taken"), sem("turned"), sem("x_added"), sem("share_turn")
        up = m["wffn"][:, shape["up_at"]:shape["up_at"] + E * shape["up"]].rearrange("p (e n) -> p e n", e=E)
        down = m["wffn"][:, shape["down_at"]:shape["down_at"] + E * NC * P].rearrange("p (e n) -> p e n", e=E)
        ctx.callback(clear, nc, sems)
        block = ctx.enter_context(nc.Block())

        @block.sync
        def _(sp):
            sp.dma_start(select[:, :, :], t["select"]).then_inc(select_in, 16)
            sp.wait_ge(select_in, 16)

        @block.tensor
        def _(pe):
            pe.wait_ge(select_in, 16)
            pe.wait_ge(weights_in, arrived)

            def group(r, first):
                tokens = bass.ds(r * W, W)
                w0 = r * E

                def shares(e):
                    if not (first and e == 0):
                        pe.wait_ge(xc_ready, w0 + e)
                    nc.tensor.sem_inc(share_turn, 1)
                    nc.tensor.matmul(share_ps[:, :], select[:, e, :], shareT[:, tokens], start=True, stop=True).then_inc(share_ready, 1)

                def product_down(v):
                    e, c = v // NC, v % NC
                    pe.wait_ge(hid_ready, w0 * NC + v + 1)
                    nc.tensor.matmul(y_ps[:, :], down[:, e, c * P:(c + 1) * P], hid[v % 2][:, :],
                                     start=v == 0, stop=v == E * NC - 1).then_inc(down_done, 1)

                shares(0)
                for e in range(E):
                    for c in range(NC):
                        v = e * NC + c
                        at = shape["gated"] + c * P
                        if not (first and v < 2):
                            pe.wait_ge(silu_done, w0 * NC + v - 1)
                        nc.tensor.matmul(g_ps[v % 2][:, :], up[:, e, at:at + P], m["xnT"][:, tokens], start=True, stop=True).then_inc(gate_ready, 1)
                        if c == 0:
                            pe.wait_ge(xc_ready, w0 + e + 1)
                        if not (first and v < 2):
                            pe.wait_ge(hid_ready, w0 * NC + v - 1)
                        at = shape["linear"] + c * P
                        nc.tensor.matmul(l_ps[v % 2][:, :], up[:, e, at:at + P], xc[e % 2][:, :], start=True, stop=True).then_inc(linear_ready, 1)
                        if c == 0 and e + 1 < E:
                            shares(e + 1)
                        if v == 1 and not first:
                            pe.wait_ge(y_taken, r)
                        if v >= 1:
                            product_down(v - 1)
                product_down(E * NC - 1)
                pe.wait_ge(y_taken, r + 1)
                if not first:
                    pe.wait_ge(x_added, r)
                for k in range(W // P):
                    last = nc.tensor.transpose(t_ps[:, k * P:(k + 1) * P], ysb[:, k * P:(k + 1) * P], m["ident"][:, :])
                last.then_inc(turned, 1)

            group(0, True)
            with pe.Fori(1, GROUPS) as r:
                group(r, False)

        @block.scalar
        def _(act):
            def group(r, first):
                for v in range(E * NC):
                    n = r * E * NC + v
                    act.wait_ge(gate_ready, n + 1)
                    if not (first and v < 2):
                        act.wait_ge(hid_ready, n - 1)
                    nc.scalar.activation(gated[v % 2][:, :], g_ps[v % 2][:, :], ACT.Silu).then_inc(silu_done, 1)
                act.wait_ge(down_done, (r + 1) * E * NC)
                if not first:
                    act.wait_ge(turned, r)
                nc.scalar.activation(ysb[:, :], y_ps[:, :], ACT.Copy).then_inc(y_taken, 1)

            group(0, True)
            with act.Fori(1, GROUPS) as r:
                group(r, False)

        @block.vector
        def _(dve):
            def group(r, first):
                tokens = bass.ds(r * W, W)
                w0 = r * E

                def scale_input(e):
                    dve.wait_ge(share_ready, w0 + e + 1)
                    if not (first and e < 2):
                        dve.wait_ge(linear_ready, (w0 + e - 1) * NC)
                    nc.vector.tensor_tensor(xc[e % 2][:, :], m["xnT"][:, tokens], share_ps[:, :], ALU.mult).then_inc(xc_ready, 1)

                scale_input(0)
                for e in range(E):
                    if e + 1 < E:
                        scale_input(e + 1)
                    for c in range(NC):
                        v = e * NC + c
                        n = w0 * NC + v
                        dve.wait_ge(silu_done, n + 1)
                        dve.wait_ge(linear_ready, n + 1)
                        if not (first and v < 2):
                            dve.wait_ge(down_done, n - 1)
                        nc.vector.tensor_tensor(hid[v % 2][:, :], gated[v % 2][:, :], l_ps[v % 2][:, :], ALU.mult).then_inc(hid_ready, 1)
                xs = m["x"][:, tokens]
                dve.wait_ge(turned, r + 1)
                nc.vector.tensor_tensor(xs, xs, t_ps[:, :], ALU.add).then_inc(x_added, 1)

            group(0, True)
            with dve.Fori(1, GROUPS) as r:
                group(r, False)


def local_attention(nc, t, m, weights_in):
    WINDOW, POWER, MASKED = 16.0, 128.0, 1e9
    with ExitStack() as ctx:
        def sb(name, shape, dt=F32):
            return ctx.enter_context(nc.sbuf_tensor(f"w_{name}", shape, dt))

        sems = []

        def sem(name):
            sems.append(ctx.enter_context(nc.semaphore(f"w_{name}")))
            return sems[-1]

        def psum(name, cols):
            return ctx.enter_context(nc.psum_tensor(f"w_{name}", [P, cols], F32))

        wa, wc = sb("wa", [P, D]), sb("wc", [P, 2, D])
        number = sb("number", [P, L])
        centre, length = sb("centre", [P, B]), sb("length", [P, B])
        length_int = sb("length_int", [P, B], I32)
        start, end, minus = sb("start", [P, B]), sb("end", [P, B]), sb("minus", [P, B])
        bounds = sb("bounds", [P, 2])
        ctxT, ctxn = sb("ctxT", [P, L]), sb("ctxn", [P, KC, D])
        valid, below, gauss, dist = sb("valid", [P, L]), sb("below", [P, L]), sb("gauss", [P, L]), sb("dist", [P, L])
        aT = sb("aT", [P, S])
        masked = [sb(f"masked{i}", [P, L]) for i in range(2)]
        alT = sb("alT", [P, KC, S])
        stat = [sb(f"stat{i}", [P, 3]) for i in range(2)]
        cT, hT = sb("cT", [P, S]), sb("hT", [P, S])
        s_ps = psum("s_ps", 2048)
        t_ps = [psum(f"t_ps{i}", 512) for i in range(2)]
        c_ps, o_ps = psum("c_ps", 512), psum("o_ps", 512)
        w_in, ctx_in, ctxn_in = sem("w_in"), sem("ctx_in"), sem("ctxn_in")
        bounds_ready, mask_turn = sem("bounds_ready"), sem("mask_turn")
        stepped, valid_ready, below_ready, gauss_ready, dist_ready = (
            sem(n) for n in ("stepped", "valid_ready", "below_ready", "gauss_ready", "dist_ready"))
        a_ready, a_taken, scored, masked_ready, mask_step, exped, aligned, turned = (
            sem(n) for n in ("a_ready", "a_taken", "scored", "masked_ready", "mask_step", "exped", "aligned", "turned"))
        alT_ready = [sem(f"alT_ready_{engine}") for engine in ("scalar", "vector")]
        c_ready, cT_ready, o_ready, hT_ready, o_turned, x_added = (
            sem(n) for n in ("c_ready", "cT_ready", "o_ready", "hT_ready", "o_turned", "x_added"))
        N_IN = 6
        TURNS = -(-KC // 4)
        FIRST_STEPS = 6

        def take_turned(copy, q, i, **more):
            chunks = range(4 * i, min(4 * i + 4, KC))
            n = len(chunks) * P
            rows = P if i < TURNS - 1 else LAST
            return copy(alT[0:rows, 4 * i:4 * i + len(chunks), q * P:(q + 1) * P],
                        t_ps[i % 2][0:rows, 0:n].rearrange("p (c q) -> p c q", q=P), **more)

        ctx.callback(clear, nc, sems)
        block = ctx.enter_context(nc.Block())

        @block.sync
        def _(sp):
            sp.dma_start(wa[:, :], t["L2_xcond_W_a"]).then_inc(w_in, 16)
            sp.dma_start(wc[:, :, :], t["L2_WcT"].rearrange("(a p) o -> p a o", p=P)).then_inc(w_in, 16)
            sp.dma_start(number[:, :], t["numbers"][None, :].to_broadcast([P, L])).then_inc(w_in, 16)
            sp.dma_start(centre[:, :], t["condB_pt"][None, :].to_broadcast([P, B])).then_inc(w_in, 16)
            sp.dma_start(length_int[:, :], t["_lenS2"][None, :].to_broadcast([P, B])).then_inc(w_in, 16)
            sp.dma_start(hT[:, :], t["ctxT"][0, :, 0:S]).then_inc(w_in, 16)
            for layer in (2, 3):
                shape = MIXTURES[layer]
                up, down = E * shape["up"], E * shape["chunks"] * P
                sp.dma_start(m["wffn"][:, shape["up_at"]:shape["up_at"] + up].rearrange("p (e n) -> p e n", e=E), t[f"L{layer}_up"]).then_inc(weights_in, 16)
                sp.dma_start(m["wffn"][:, shape["down_at"]:shape["down_at"] + down].rearrange("p (e n) -> p e n", e=E), t[f"L{layer}_down"]).then_inc(weights_in, 16)

            def batch(b, first):
                if not first:
                    sp.wait_ge(scored, 2 * b)
                sp.dma_start(ctxT[:, :], t["ctxT"][bass.ds(b, 1), :, :].rearrange("o p l -> (o p) l")).then_inc(ctx_in, 16)
                if not first:
                    sp.wait_ge(c_ready, b)
                sp.dma_start(ctxn[:, 0:KC - 1, :], t["ctx_1024"][bass.ds(b, 1), 0:L - LAST, :].rearrange("o (c p) d -> (o p) c d", p=P)).then_inc(ctxn_in, 16)
                sp.dma_start(ctxn[0:LAST, KC - 1, :], t["ctx_1024"][bass.ds(b, 1), L - LAST:L, :].rearrange("o p d -> (o p) d")).then_inc(ctxn_in, 16)

            batch(0, True)
            with sp.Fori(1, B) as b:
                batch(b, False)
            sp.wait_ge(w_in, 16 * N_IN)
            sp.wait_ge(ctxn_in, 32 * B)

        @block.gpsimd
        def _(pool):
            pool.wait_ge(stepped, FIRST_STEPS)

            def batch(b, first):
                pool.wait_ge(bounds_ready, 2 * b + 2)
                nc.gpsimd.sem_inc(mask_turn, 1)
                nc.gpsimd.tensor_scalar(below[:, :], number[:, :], bounds[:, 0:1], None, ALU.is_ge).then_inc(below_ready, 1)
                pool.wait_ge(below_ready, 3 * b + 1)
                nc.gpsimd.sem_inc(mask_turn, 1)
                nc.gpsimd.tensor_scalar(valid[:, :], number[:, :], bounds[:, 1:2], None, ALU.is_le).then_inc(below_ready, 1)
                pool.wait_ge(below_ready, 3 * b + 2)
                nc.gpsimd.tensor_tensor(valid[:, :], valid[:, :], below[:, :], ALU.mult).then_inc(below_ready, 1)
                pool.wait_ge(below_ready, 3 * b + 3)
                nc.gpsimd.sem_inc(mask_turn, 1)
                nc.gpsimd.tensor_scalar(below[:, :], valid[:, :], -1.0, MASKED, ALU.add, ALU.mult).then_inc(valid_ready, 1)

            batch(0, True)
            with pool.Fori(1, B) as b:
                batch(b, False)

        @block.vector
        def _(dve):
            dve.wait_ge(w_in, 16 * N_IN)
            k = 0

            def done(instruction):
                nonlocal k
                k += 1
                instruction.then_inc(stepped, 1)
                dve.wait_ge(stepped, k)

            done(nc.vector.tensor_copy(length[:, :], length_int[:, :]))
            done(nc.vector.tensor_scalar(start[:, :], centre[:, :], WINDOW, 0.0, ALU.subtract, ALU.max))
            done(nc.vector.tensor_scalar(end[:, :], centre[:, :], WINDOW, None, ALU.add))
            done(nc.vector.tensor_tensor(end[:, :], end[:, :], length[:, :], ALU.min))
            done(nc.vector.tensor_scalar(minus[:, :], centre[:, :], -1.0, None, ALU.mult))
            done(nc.vector.memset(stat[0][:, :], 0.0))
            assert k == FIRST_STEPS

            def batch(b, first):
                dve.wait_ge(a_ready, b + 1)
                nc.vector.tensor_copy(aT[:, :], o_ps[:, 0:S]).then_inc(a_taken, 1)
                for bound, i in ((start, 0), (end, 1)):
                    nc.vector.tensor_copy(bounds[:, i:i + 1], bound[:, bass.ds(b, 1)]).then_inc(bounds_ready, 1)
                dve.wait_ge(valid_ready, b + 1)
                for q in range(QT):
                    n = 2 * b + q
                    dve.wait_ge(scored, n + 1)
                    if not first:
                        dve.wait_ge(turned, (n - 1) * TURNS)
                    nc.vector.tensor_tensor(masked[q][:, :], s_ps[:, 0:L], valid[:, :], ALU.mult).then_inc(mask_step, 1)
                    dve.wait_ge(mask_step, 2 * n + 1)
                    nc.vector.tensor_tensor(masked[q][:, :], masked[q][:, :], below[:, :], ALU.add).then_inc(mask_step, 1)
                    dve.wait_ge(mask_step, 2 * n + 2)
                    nc.vector.tensor_reduce(stat[q][:, 0:1], masked[q][:, :], axis=AX.X, op=ALU.max, negate=True).then_inc(masked_ready, 1)
                for q in range(QT):
                    n = 2 * b + q
                    dve.wait_ge(exped, n + 1)
                    nc.vector.reciprocal(stat[q][:, 2:3], stat[q][:, 1:2]).then_inc(aligned, 1)
                    dve.wait_ge(aligned, 2 * n + 1)
                    dve.wait_ge(gauss_ready, b + 1)
                    nc.vector.scalar_tensor_tensor(masked[q][:, :], masked[q][:, :], stat[q][:, 2:3], gauss[:, :], ALU.mult, ALU.mult).then_inc(aligned, 1)
                    for i in (1, 3):
                        dve.wait_ge(turned, n * TURNS + i + 1)
                        take_turned(nc.vector.tensor_copy, q, i).then_inc(alT_ready[1], 1)
                dve.wait_ge(c_ready, b + 1)
                nc.vector.tensor_copy(cT[:, :], c_ps[:, 0:S]).then_inc(cT_ready, 1)
                dve.wait_ge(o_turned, b + 1)
                xs = m["x"][:, bass.ds(b * S, S)]
                nc.vector.tensor_tensor(xs, xs, c_ps[:, 0:S], ALU.add).then_inc(x_added, 1)

            batch(0, True)
            with dve.Fori(1, B) as b:
                batch(b, False)

        @block.scalar
        def _(act):
            act.wait_ge(stepped, FIRST_STEPS)

            def batch(b, first):
                if not first:
                    act.wait_ge(aligned, 4 * b)
                nc.scalar.activation(dist[:, :], number[:, :], ACT.Square, bias=minus[:, bass.ds(b, 1)]).then_inc(dist_ready, 1)
                act.wait_ge(dist_ready, b + 1)
                nc.scalar.activation(gauss[:, :], dist[:, :], ACT.Exp, scale=-1.0 / POWER).then_inc(gauss_ready, 1)
                for q in range(QT):
                    n = 2 * b + q
                    act.wait_ge(masked_ready, n + 1)
                    nc.scalar.activation(masked[q][:, :], masked[q][:, :], ACT.Exp, bias=stat[q][:, 0:1],
                                         accum_out=stat[q][:, 1:2]).then_inc(exped, 1)
                for q in range(QT):
                    n = 2 * b + q
                    for i in (0, 2):
                        act.wait_ge(turned, n * TURNS + i + 1)
                        if not first:
                            act.wait_ge(c_ready, b)
                        take_turned(nc.scalar.activation, q, i, func=ACT.Copy).then_inc(alT_ready[0], 1)
                act.wait_ge(o_ready, b + 1)
                nc.scalar.activation(hT[:, :], o_ps[:, 0:S], ACT.Tanh).then_inc(hT_ready, 1)

            batch(0, True)
            with act.Fori(1, B) as b:
                batch(b, False)

        @block.tensor
        def _(pe):
            pe.wait_ge(w_in, 16 * N_IN)

            def batch(b, first):
                queries = bass.ds(b * S, S)
                if not first:
                    pe.wait_ge(hT_ready, b)
                nc.tensor.matmul(o_ps[:, 0:S], wa[:, :], m["xnT"][:, queries], start=True, stop=True).then_inc(a_ready, 1)
                pe.wait_ge(a_taken, b + 1)
                pe.wait_ge(ctx_in, 16 * b + 16)
                for q in range(QT):
                    n = 2 * b + q
                    if not (first and q == 0):
                        pe.wait_ge(mask_step, 2 * n - 1)
                    for i in range(TURNS):
                        width = min(512, L - 512 * i)
                        last = nc.tensor.matmul(s_ps[:, 512 * i:512 * i + width], aT[:, q * P:(q + 1) * P], ctxT[:, 512 * i:512 * i + width],
                                                start=True, stop=True)
                    last.then_inc(scored, 1)
                for q in range(QT):
                    n = 2 * b + q
                    pe.wait_ge(aligned, 2 * n + 2)
                    for i in range(TURNS):
                        if i >= 2 or not (first and q == 0):
                            pe.wait_ge(alT_ready[i % 2], 2 * n + i // 2)
                        for k, c in enumerate(range(4 * i, min(4 * i + 4, KC))):
                            rows = chunk_rows(c)
                            last = nc.tensor.transpose(t_ps[i % 2][0:rows, k * P:(k + 1) * P], masked[q][:, c * P:c * P + rows], m["ident"][:, :])
                        last.then_inc(turned, 1)
                for taken in alT_ready:
                    pe.wait_ge(taken, TURNS * (b + 1))
                pe.wait_ge(ctxn_in, 32 * b + 32)
                if not first:
                    pe.wait_ge(x_added, b)
                for c in range(KC):
                    rows = chunk_rows(c)
                    last = nc.tensor.matmul(c_ps[:, 0:S], ctxn[0:rows, c, :], alT[0:rows, c, :], start=c == 0, stop=c == KC - 1)
                last.then_inc(c_ready, 1)
                pe.wait_ge(cT_ready, b + 1)
                nc.tensor.matmul(o_ps[:, 0:S], wc[:, 0, :], cT[:, :], start=True, stop=False)
                nc.tensor.matmul(o_ps[:, 0:S], wc[:, 1, :], m["xnT"][:, queries], start=False, stop=True).then_inc(o_ready, 1)
                pe.wait_ge(hT_ready, b + 1)
                for q in range(QT):
                    last = nc.tensor.transpose(c_ps[:, q * P:(q + 1) * P], hT[:, q * P:(q + 1) * P], m["ident"][:, :])
                last.then_inc(o_turned, 1)

            batch(0, True)
            with pe.Fori(1, B) as b:
                batch(b, False)



def kernel(**inputs):
    import numpy as np
    import concourse.bacc as bacc
    from concourse.bass_utils import run_bass_kernel_spmd

    a = {name: np.asarray(value) for name, value in inputs.items()}
    arrays = {name: a[name] for name in ("x", "ctx_1024", "condB_tau", "fside_BxS2_0", "condB_pt", "_lenS2", "L2_xcond_W_a", "L3_ffn_norm_scale")}
    arrays["ctxT"] = a["ctx_1024"].transpose(0, 2, 1)
    for layer in (0, 1, 3):
        for w in ("Wq", "Wk", "Wv", "Wo"):
            arrays[f"L{layer}_{w}T"] = a[f"L{layer}_xcond_{w}"].T
        arrays[f"L{layer}_bq_rows"] = np.tile(a[f"L{layer}_xcond_bq"].reshape(G, ROWS).T, (3, 1))
        for v in ("bk", "bv", "bo"):
            arrays[f"L{layer}_xcond_{v}"] = a[f"L{layer}_xcond_{v}"]
    arrays["L0_w1T"], arrays["L0_w2T"] = a["L0_ffn_w1"].T, a["L0_ffn_w2"].T
    arrays["L2_WcT"] = a["L2_xcond_W_c"].T

    def by_chunk(w):
        e, h, d = w.shape
        return w.reshape(e, h // P, P, d).transpose(2, 0, 1, 3).reshape(P, e, h // P * d)

    arrays["L1_gateT"], arrays["L2_gateT"], arrays["L3_gateT"] = a["L1_ffn_gate_w"].T, a["L2_ffn_gate_w"].T, a["L3_ffn_w_router"].T
    arrays["L1_up"] = np.concatenate([a["L1_ffn_w1"], a["L1_ffn_w3"]], axis=1).transpose(2, 0, 1)
    arrays["L1_down"] = by_chunk(a["L1_ffn_w2"].transpose(0, 2, 1))
    arrays["L2_up"] = a["L2_ffn_gate_up_proj"].transpose(1, 0, 2)
    arrays["L2_down"] = by_chunk(a["L2_ffn_down_proj"])
    arrays["L3_up"] = a["L3_ffn_w_up"].transpose(2, 0, 1)
    arrays["L3_down"] = by_chunk(a["L3_ffn_w_down"].transpose(0, 2, 1))

    row = np.arange(P)
    arrays["ident"] = np.eye(P, dtype=np.float32)
    arrays["qmask"] = (row[:, None] % ROWS // DK == np.arange(J)).astype(np.float32)
    shift = np.zeros((P, J), np.float32)
    shift[96:96 + J] = -np.eye(J)
    shift[100:102] = 1.0
    arrays["shiftmask"] = shift
    rest = np.zeros((P, J), np.float32)
    rest[96:96 + J, 0] = 1.0
    rest[100:102, 1] = 1.0
    arrays["restmask"] = rest
    arrays["numbers"] = np.arange(L, dtype=np.float32)
    select = np.zeros((E, E, P), np.float32)
    select[np.arange(E), np.arange(E)] = 1.0
    arrays["select"] = select
    arrays = {name: np.ascontiguousarray(v) for name, v in arrays.items()}

    nc = bacc.Bacc("TRN2", target_bir_lowering=False, num_devices=1)
    t = {name: nc.dram_tensor(f"in_{name}", v.shape, mybir.dt.from_np(v.dtype), kind="ExternalInput").ap() for name, v in arrays.items()}
    out = nc.dram_tensor("out_x", (B, S, D), F32, kind="ExternalOutput").ap()
    build(nc, t, out)
    r = run_bass_kernel_spmd(nc, [{f"in_{name}": v for name, v in arrays.items()}], core_ids=[0])
    return r.results[0]["out_x"]
```

```python
from contextlib import ExitStack

import concourse.bass as bass
from concourse import mybir
from concourse.alu_op_type import AluOpType as ALU

F32 = mybir.dt.float32
F32R = mybir.dt.float32r
BF16 = mybir.dt.bfloat16
U32 = mybir.dt.uint32
I32 = mybir.dt.int32
ACT = mybir.ActivationFunctionType
AX = mybir.AxisListType

B, S, D = 8, 256, 128
L = 1601
H, DK = 16, 8
P = 128
TILES = B * S // P
TOK = B * S
QT = S // P
KC = -(-L // P)
LAST = L - (KC - 1) * P
G, J = 4, 4
ROWS = J * DK
E = 8
LN_EPS, RMS_EPS, L2_EPS, Q_EPS = 1e-5, 1e-6, 1e-9, 1e-5
ROUND = 1.5 * 2.0 ** 23
EXPERT_TOK = 512

UNITS = KC * 2
LAG = 3
GUARD_TILES = J * QT * 2
RUN = 2 * -(-L // 8)
RUNS = [i * (L - RUN) // 3 for i in range(4)]
assert all(b - a <= RUN for a, b in zip(RUNS, RUNS[1:])) and RUNS[-1] + RUN == L
GUARD_START = -7
MAX_AT = 18
GUARD_AT = {}
for _k in range(GUARD_TILES):
    _at = GUARD_START + _k * UNITS // GUARD_TILES
    GUARD_AT.setdefault(_at % UNITS, []).append((1 if _at >= 0 else 2, _k))
assert GUARD_START + (GUARD_TILES - 1) * UNITS // GUARD_TILES < MAX_AT
EARLY = [k for tiles in GUARD_AT.values() for ahead, k in tiles if ahead == 2]


def guard_tiles(unit, g, last):
    return [(ahead, k) for ahead, k in GUARD_AT.get(unit, []) if not (last and g + ahead >= G)]


SIDE = {
    0: [(2, "Q"), (6, "T"), (9, "AT"), (12, "WO"), (21, "R")],
    1: [(2, "Q"), (6, "T"), (8, "K0"), (10, "K1"), (12, "K2"), (14, "K3"), (21, "R")],
    2: [(2, "Q"), (6, "T"), (8, "V0"), (10, "V1"), (12, "V2"), (14, "V3"), (21, "R")],
    3: [(2, "Q"), (6, "T"), (21, "R")],
}


def side_items(first, last):
    out, n = [], 0
    for g in range(G):
        here = {}
        for unit, item in SIDE[g]:
            if first and g == 0 and item in ("T", "AT", "WO"):
                continue
            if last and (item[0] in "KV" or (item == "Q" and g >= 2) or (item == "R" and g == 3)):
                continue
            here[unit] = (item, n)
            n += 1
        out.append(here)
    return out, n


SIDE_START = 4 + 4 + 2 + 1
N_FIRST, N_MID = side_items(True, False)[1], side_items(False, False)[1]
N_LAST = side_items(False, True)[1]
AFTER_V3 = sum(item[0] != "V" for unit, item in SIDE[2] if unit > 14) + len(SIDE[3])


def side_base(b, first, last):
    if first:
        return SIDE_START
    if last:
        return SIDE_START + N_FIRST + N_MID * (B - 2)
    return SIDE_START + N_FIRST - N_MID + b * N_MID


def chunk_rows(c):
    return LAST if c == KC - 1 else P


def build(nc, t, out):
    top = ExitStack()

    def sb(name, shape, dt=F32, ctx=top):
        return ctx.enter_context(nc.sbuf_tensor(name, shape, dt))

    def psum(name, shape, ctx):
        return ctx.enter_context(nc.psum_tensor(name, shape, F32))

    def sem(name, ctx=top):
        return ctx.enter_context(nc.semaphore(name))

    with top:
        m = {
            "x": sb("x_sb", [P, TOK]),
            "xnT": sb("xnT", [P, TOK]),
            "ident": sb("ident", [P, P]),
            "qmask": sb("qmask", [P, J]),
            "shiftmask": sb("shiftmask", [P, J]),
            "restmask": sb("restmask", [P, J]),
            "tau": sb("tau_all", [P, B]),
            "wffn": sb("wffn", [P, 12288]),
            "nm": sb("nm", [P, QT, 32]),
        }
        split = nc.dram_tensor("delta_split", (2, B, L), F32, kind="Internal").ap()
        weights_in = sem("ffn_weights_in")
        setup(nc, t, m, split, sem, sb, weights_in)
        for layer in (0, 1):
            norm(nc, t, m, f"L{layer}a", False)
            attention(nc, t, m, split, layer)
            if layer == 0:
                quantised_ffn(nc, t, m)
            else:
                norm(nc, t, m, "L1f", False)
                experts(nc, t, m, 1, weights_in, 32)
        norm(nc, t, m, "L2a", False)
        local_attention(nc, t, m, weights_in)
        norm(nc, t, m, "L2f", False)
        experts(nc, t, m, 2, weights_in, 96)
        norm(nc, t, m, "L3a", False)
        attention(nc, t, m, split, 3)
        norm(nc, t, m, "L3f", True)
        experts(nc, t, m, 3, weights_in, 96)
        finish(nc, m, out, sem)


def setup(nc, t, m, split, sem, sb, weights_in):
    with ExitStack() as ctx:
        loaded, stepped, stored = sems = sem("setup_loaded", ctx), sem("setup_stepped", ctx), sem("setup_stored", ctx)
        delta = sb("delta", [B, L], F32, ctx)
        high = sb("delta_high", [B, L], F32R, ctx)
        low = sb("delta_low", [B, L], F32R, ctx)
        ctx.callback(clear, nc, sems)
        block = ctx.enter_context(nc.Block())

        @block.sync
        def _(sp):
            sp.dma_start(delta[:, :], t["fside_BxS2_0"]).then_inc(loaded, 16)
            sp.dma_start(m["x"][:, :].rearrange("p (n d) -> p n d", d=D),
                         t["x"].rearrange("b (n p) d -> p (b n) d", p=P)).then_inc(loaded, 16)
            for name in ("ident", "qmask", "shiftmask", "restmask"):
                sp.dma_start(m[name][:, :], t[name]).then_inc(loaded, 16)
            sp.dma_start(m["tau"][:, :], t["condB_tau"][None, :].to_broadcast([P, B])).then_inc(loaded, 16)
            sp.wait_ge(stepped, 2)
            sp.dma_start(split[0], high[:, :].bitcast(F32)).then_inc(stored, 16)
            sp.dma_start(split[1], low[:, :].bitcast(F32)).then_inc(stored, 16)
            sp.dma_start(m["wffn"][:, 0:E * 1024].rearrange("p (e n) -> p e n", e=E), t["L1_up"]).then_inc(weights_in, 16)
            sp.dma_start(m["wffn"][:, E * 1024:12288].rearrange("p (e n) -> p e n", e=E), t["L1_down"]).then_inc(weights_in, 16)
            sp.wait_ge(stored, 32)
            sp.wait_ge(loaded, 7 * 16)

        @block.vector
        def _(dve):
            dve.wait_ge(loaded, 7 * 16)
            nc.vector.tensor_copy(high[:, :], delta[:, :]).then_inc(stepped, 1)
            dve.wait_ge(stepped, 1)
            nc.vector.tensor_tensor(low[:, :], delta[:, :], high[:, :].bitcast(F32), ALU.subtract).then_inc(stepped, 1)
            nc.vector.memset(m["nm"][:, :, :], 0.0).then_inc(stepped, 1)
            dve.wait_ge(stepped, 3)
            nc.vector.memset(m["nm"][:, :, J:J + 2], 1.0).then_inc(stepped, 1)


def clear(nc, sems):
    with nc.Block() as block:
        @block.sync
        def _(sp):
            for s in sems:
                sp.sem_clear(s)


def finish(nc, m, out, sem):
    stored = sem("out_stored")
    with nc.Block() as block:
        @block.sync
        def _(sp):
            sp.dma_start(out.rearrange("b (n p) d -> p (b n) d", p=P),
                         m["x"][:, :].rearrange("p (n d) -> p n d", d=D)).then_inc(stored, 16)
            sp.wait_ge(stored, 16)


def norm(nc, t, m, tag, rms, xn=None):
    with ExitStack() as ctx:
        def sb(name, shape, dt=F32):
            return ctx.enter_context(nc.sbuf_tensor(f"{tag}_{name}", shape, dt))

        sems = []

        def sem(name):
            sems.append(ctx.enter_context(nc.semaphore(f"{tag}_{name}")))
            return sems[-1]

        turn = xn is None
        xn = sb("xn", [P, TOK]) if turn else xn
        square = sb("square", [P, TOK])
        stat = sb("stat", [P, 8, TILES])
        total, mean, power, spread, rstd = (stat[:, i, :] for i in range(5))
        gain = sb("gain", [P, D])
        banks = [ctx.enter_context(nc.psum_tensor(f"{tag}_ps{i}", [P, 4 * P], F32)) for i in range(4)]
        stepped, squared, rooted, turned, taken, gain_in = (sem(n) for n in ("stepped", "squared", "rooted", "turned", "taken", "gain_in"))
        x3 = m["x"][:, :].rearrange("p (n d) -> p n d", d=D)
        xn3 = xn[:, :].rearrange("p (n d) -> p n d", d=D)
        square3 = square[:, :].rearrange("p (n d) -> p n d", d=D)
        normalised = 11 if rms else 7
        ctx.callback(clear, nc, sems)
        block = ctx.enter_context(nc.Block())

        def per_token(a):
            return a[:, :, None].to_broadcast([P, TILES, D])

        if rms:
            @block.sync
            def _(sp):
                sp.dma_start(gain[:, :], t["L3_ffn_norm_scale"][None, :].to_broadcast([P, D])).then_inc(gain_in, 16)
                sp.wait_ge(gain_in, 16)

        @block.vector
        def _(dve):
            n = 0

            def done(instruction):
                nonlocal n
                n += 1
                instruction.then_inc(stepped, 1)
                dve.wait_ge(stepped, n)

            done(nc.vector.tensor_reduce(total, x3, axis=AX.X, op=ALU.add))
            done(nc.vector.tensor_scalar(mean, total, 1.0 / D, None, ALU.mult))
            done(nc.vector.tensor_tensor(xn3, x3, per_token(mean), ALU.subtract))
            dve.wait_ge(squared, 1)
            done(nc.vector.tensor_reduce(total, square3, axis=AX.X, op=ALU.add))
            done(nc.vector.tensor_scalar(power, total, 1.0 / D, LN_EPS, ALU.mult, ALU.add))
            dve.wait_ge(rooted, 1)
            done(nc.vector.reciprocal(rstd, spread))
            done(nc.vector.tensor_tensor(xn3, xn3, per_token(rstd), ALU.mult))
            if rms:
                dve.wait_ge(squared, 2)
                done(nc.vector.tensor_reduce(total, square3, axis=AX.X, op=ALU.add))
                done(nc.vector.tensor_scalar(power, total, 1.0 / D, RMS_EPS, ALU.mult, ALU.add))
                done(nc.vector.tensor_tensor(m["x"][:, :], m["x"][:, :], xn[:, :], ALU.add))
                dve.wait_ge(rooted, 2)
                nc.vector.reciprocal(rstd, spread).then_inc(taken, 1)
                dve.wait_ge(taken, 1)
                nc.vector.tensor_tensor(xn3, xn3, per_token(rstd), ALU.mult).then_inc(taken, 1)
                dve.wait_ge(taken, 2)
                dve.wait_ge(gain_in, 16)
                done(nc.vector.tensor_tensor(xn3, xn3, gain[:, None, :].to_broadcast([P, TILES, D]), ALU.mult))
            for i in (1, 3) if turn else ():
                dve.wait_ge(turned, i + 1)
                nc.vector.tensor_copy(m["xnT"][:, i * 512:(i + 1) * 512], banks[i][:, :])

        @block.scalar
        def _(act):
            act.wait_ge(stepped, 3)
            nc.scalar.activation(square[:, :], xn[:, :], ACT.Square).then_inc(squared, 1)
            act.wait_ge(stepped, 5)
            nc.scalar.activation(spread, power, ACT.Sqrt).then_inc(rooted, 1)
            if rms:
                act.wait_ge(stepped, 7)
                nc.scalar.activation(square[:, :], xn[:, :], ACT.Square).then_inc(squared, 1)
                act.wait_ge(stepped, 9)
                nc.scalar.activation(spread, power, ACT.Sqrt).then_inc(rooted, 1)
            for i in (0, 2) if turn else ():
                act.wait_ge(turned, i + 1)
                nc.scalar.activation(m["xnT"][:, i * 512:(i + 1) * 512], banks[i][:, :], ACT.Copy)

        @block.tensor
        def _(pe):
            pe.wait_ge(stepped, normalised)
            for i in range(4) if turn else ():
                for k in range(4):
                    tile = 4 * i + k
                    last = nc.tensor.transpose(banks[i][:, k * P:(k + 1) * P], xn[:, tile * P:(tile + 1) * P], m["ident"][:, :])
                last.then_inc(turned, 1)


def attention(nc, t, m, split, layer):
    tag = f"L{layer}"
    with ExitStack() as ctx:
        def sb(name, shape, dt=F32):
            return ctx.enter_context(nc.sbuf_tensor(f"{tag}_{name}", shape, dt))

        sems = []

        def sem(name):
            sems.append(ctx.enter_context(nc.semaphore(f"{tag}_{name}")))
            return sems[-1]

        def psum(name, shape):
            return ctx.enter_context(nc.psum_tensor(f"{tag}_{name}", shape, F32))

        ident = m["ident"]
        wq = sb("wq", [P, G, 3, ROWS])
        wk, wv, wo = sb("wk", [P, D]), sb("wv", [P, D]), sb("wo", [P, D])
        bq = sb("bq", [3 * ROWS, G])
        taubq = sb("taubq", [3 * ROWS, G, B])
        bk = sb("bk", [P, 1])
        bv, bo = sb("bv", [P, D]), sb("bo", [P, D])
        ctxT = sb("ctxT", [P, L])
        kfull = sb("kfull", [P, L])
        khigh, klow = sb("khigh", [P, L], F32R), sb("klow", [P, L], F32R)
        kst = [sb(f"kst{g}", [P, L], F32R) for g in range(G)]
        qst = [sb(f"qst{g}", [P, J, S], F32R) for g in range(G)]
        tq = [sb(f"tq{i}", [3 * ROWS, S]) for i in range(2)]
        tqh = sb("tqh", [3 * ROWS, S], F32R)
        vc = sb("vc", [P, KC, D])
        vx = sb("vx", [P, H, KC, 32])
        probs = [sb(f"probs{i}", [P, 2 * S]) for i in range(4)]
        partmax = sb("partmax", [P, QT, J, 2])
        nm = m["nm"]
        osb = sb("osb", [P, S])
        rcp = sb("rcp", [P, QT, J])
        att, attb = sb("att", [P, QT, D]), sb("attb", [P, QT, D])
        attT = sb("attT", [P, S])
        wotmp = sb("wotmp", [P, S])

        guard_ps = [psum(f"guard{i}", [P, 1024]) for i in range(2)]
        score_ps = [psum(f"score{i}", [P, 512]) for i in range(2)]
        o_ps = psum("o_ps", [P, 512])
        side = psum("side", [P, 512])

        w_in = sem("w_in")
        ctx_in = sem("ctx_in")
        kst_in = [sem(f"kst_in{g}") for g in range(G)]
        side_ready, side_taken = sem("side_ready"), sem("side_taken")
        guard_scored, guard_reduced = sem("guard_scored"), sem("guard_reduced")
        scores_ready, exp_done, pv_done = sem("scores_ready"), sem("exp_done"), sem("pv_done")
        o_taken = sem("o_taken")
        max_ready, shift_ready = sem("max_ready"), sem("shift_ready")
        kfull_ready, khigh_ready, klow_ready = sem("kfull_ready"), sem("khigh_ready"), sem("klow_ready")
        tq_ready, tq_high, tq_split = sem("tq_ready"), sem("tq_high"), sem("tq_split")
        qst_ready = sem("qst_ready")
        rcp_ready, att_done, attb_ready, attT_ready = sem("rcp_ready"), sem("att_done"), sem("attb_ready"), sem("attT_ready")
        wo_taken, x_added = sem("wo_taken"), sem("x_added")
        vx_ready, vx_cleared, spread_turn, split_turn = (
            sem("vx_ready"), sem("vx_cleared"), sem("spread_turn"), sem("split_turn"))
        taubq_ready, kst_cleared = sem("taubq_ready"), sem("kst_cleared")
        ctx.callback(clear, nc, sems)
        block = ctx.enter_context(nc.Block())

        LOADS = 3 * G + 3 + 1 + 1 + 2

        def step(b, g):
            return b * G + g

        def keys(c):
            return slice(c * P, c * P + chunk_rows(c))

        @block.sync
        def _(sp):
            for g in range(G):
                for r in range(3):
                    sp.dma_start(wq[:, g, r, :], t[f"{tag}_WqT"][:, g * ROWS:(g + 1) * ROWS]).then_inc(w_in, 16)
            for name, where in (("Wk", wk), ("Wv", wv), ("Wo", wo)):
                sp.dma_start(where[:, :], t[f"{tag}_{name}T"]).then_inc(w_in, 16)
            sp.dma_start(bq[:, :], t[f"{tag}_bq_rows"]).then_inc(w_in, 16)
            sp.dma_start(bk[:, :], t[f"{tag}_xcond_bk"][:, None]).then_inc(w_in, 16)
            sp.dma_start(bv[:, :], t[f"{tag}_xcond_bv"][None, :].to_broadcast([P, D])).then_inc(w_in, 16)
            sp.dma_start(bo[:, :], t[f"{tag}_xcond_bo"][None, :].to_broadcast([P, D])).then_inc(w_in, 16)

            def load_context(b):
                sp.dma_start(ctxT[:, :], t["ctxT"][bass.ds(b, 1), :, :].rearrange("o p l -> (o p) l")).then_inc(ctx_in, 16)

            def fill_stack(b, g):
                rows = slice(g * ROWS, (g + 1) * ROWS)
                for r, part in enumerate((khigh, klow, khigh)):
                    sp.dma_start(kst[g][r * ROWS:(r + 1) * ROWS, :].bitcast(F32), part[rows, :].bitcast(F32)).then_inc(kst_in[g], 16)
                sp.dma_start(kst[g][100:102, :].bitcast(F32), split[:, bass.ds(b, 1), :].rearrange("a o l -> (a o) l")).then_inc(kst_in[g], 16)

            load_context(0)
            sp.wait_ge(klow_ready, 1)
            sp.wait_ge(kst_cleared, G)
            for g in range(G):
                fill_stack(0, g)

            def batch(b, first, last):
                if not first:
                    sp.wait_ge(scores_ready, step(b, 0) * UNITS)
                    fill_stack(b, 3)
                if last:
                    return
                sp.wait_ge(side_ready, 8 if first else side_base(b, first, last) - AFTER_V3)
                load_context(b + 1)
                sp.wait_ge(klow_ready, b + 2)
                sp.wait_ge(scores_ready, step(b, 1) * UNITS)
                fill_stack(b + 1, 0)
                for g in (1, 2):
                    sp.wait_ge(scores_ready, step(b, g + 1) * UNITS)
                    fill_stack(b + 1, g)

            batch(0, True, False)
            with sp.Fori(1, B - 1) as b:
                batch(b, False, False)
            batch(B - 1, False, True)
            sp.wait_ge(w_in, LOADS * 16)

        @block.tensor
        def _(pe):
            def wait_side(n):
                pe.wait_ge(side_taken, n)

            def item(name, b, g, n):
                if not (name == "K0" and isinstance(n, int) and n == 0):
                    wait_side(n)
                if name[0] == "K":
                    c = int(name[1])
                    if c == 0:
                        pe.wait_ge(ctx_in, 16 * b + 32)
                    width = min(512, L - 512 * c)
                    last = nc.tensor.matmul(side[:, 0:width], wk[:, :], ctxT[:, 512 * c:512 * c + width], start=True, stop=True)
                elif name[0] == "V":
                    v = int(name[1])
                    for i, c in enumerate(range(4 * v, min(4 * v + 4, KC))):
                        last = nc.tensor.matmul(side[0:chunk_rows(c), i * P:(i + 1) * P], ctxT[:, keys(c)], wv[:, :], start=True, stop=True)
                elif name == "Q":
                    g2, b2 = (g + 2) % G, b + (g + 2) // G
                    last = nc.tensor.matmul(side[0:3 * ROWS, 0:S], wq[:, g2, :, :].rearrange("p r c -> p (r c)"),
                                            m["xnT"][:, bass.ds(b2 * S, S)], start=True, stop=True)
                elif name == "R":
                    pe.wait_ge(max_ready, step(b, g) + 2)
                    for q in range(QT):
                        last = nc.tensor.matmul(side[96:128, q * P:(q + 1) * P], nm[:, q, :], ident[:, :], start=True, stop=True)
                elif name == "T":
                    pe.wait_ge(o_taken, step(b, g))
                    for q in range(QT):
                        last = nc.tensor.transpose(side[:, q * P:(q + 1) * P], osb[:, q * P:(q + 1) * P], ident[:, :])
                elif name == "AT":
                    pe.wait_ge(attb_ready, b)
                    for q in range(QT):
                        last = nc.tensor.transpose(side[:, q * P:(q + 1) * P], attb[:, q, :], ident[:, :])
                elif name == "WO":
                    pe.wait_ge(attT_ready, b)
                    for q in range(QT):
                        last = nc.tensor.matmul(side[:, q * P:(q + 1) * P], attT[:, q * P:(q + 1) * P], wo[:, :], start=True, stop=True)
                last.then_inc(side_ready, 1)

            def guard(s, g, k):
                j, q, half = k // (2 * QT), k // 2 % QT, k % 2
                if k >= 2:
                    pe.wait_ge(guard_reduced, s * GUARD_TILES + k - 1)
                elif not (isinstance(s, int) and s == 0):
                    pe.wait_ge(guard_reduced, s * GUARD_TILES + k - 1)
                for i, start in enumerate(RUNS[2 * half:2 * half + 2]):
                    last = nc.tensor.matmul(guard_ps[half][:, i * 512:i * 512 + RUN], qst[g][:, j, q * P:(q + 1) * P],
                                            kst[g][:, start:start + RUN], start=True, stop=True)
                last.then_inc(guard_scored, 1)

            def values(s, g, c):
                pe.wait_ge(exp_done, s * UNITS + 2 * c + 2)
                n = chunk_rows(c)
                for j in range(J):
                    last = nc.tensor.matmul(o_ps[32 * j:32 * j + 32, 0:S], vx[0:n, g * J + j, c, :],
                                            probs[(2 * g + 2 * c + j // 2) % 4][0:n, j % 2 * S:(j % 2 + 1) * S],
                                            start=c == 0, stop=c == KC - 1)
                last.then_inc(pv_done, 2)

            pe.wait_ge(w_in, LOADS * 16)
            for n, name in enumerate(["K0", "K1", "K2", "K3", "V0", "V1", "V2", "V3"]):
                item(name, -1, 1, n)
            for n, s in ((8, 0), (9, 1)):
                item("Q", 0, s - 2, n)
            pe.wait_ge(kst_in[0], 64)
            pe.wait_ge(qst_ready, 2)
            for k in range(GUARD_TILES):
                guard(0, 0, k)
            item("R", 0, -1, 10)
            pe.wait_ge(kst_in[1], 64)
            pe.wait_ge(qst_ready, 4)
            for k in sorted(EARLY):
                guard(1, 1, k)

            def batch(b, first, last):
                items, _ = side_items(first, last)
                base = side_base(b, first, last)
                for g in range(G):
                    s = step(b, g)
                    for u in range(UNITS):
                        if u in items[g]:
                            name, n = items[g][u]
                            item(name, b, g, base + n)
                        for ahead, k in guard_tiles(u, g, last):
                            g1, b1 = (g + ahead) % G, b + (g + ahead) // G
                            if k == 0:
                                pe.wait_ge(kst_in[g1], 64 * b1 + 64)
                                pe.wait_ge(qst_ready, 2 * (s + ahead) + 2)
                            guard(s + ahead, g1, k)
                        if u == 0:
                            pe.wait_ge(shift_ready, s + 1)
                        if not (first and g == 0 and u < 2):
                            pe.wait_ge(exp_done, s * UNITS + u - 1)
                        c, pair = u // 2, u % 2
                        nc.tensor.matmul(score_ps[u % 2][0:chunk_rows(c), :], kst[g][:, keys(c)],
                                         qst[g][:, 2 * pair:2 * pair + 2, :].rearrange("p j q -> p (j q)"),
                                         start=True, stop=True).then_inc(scores_ready, 1)
                        if u >= LAG and u % 2:
                            if u == LAG:
                                pe.wait_ge(vx_ready, s + 1)
                                if not (first and g == 0):
                                    pe.wait_ge(o_taken, s)
                            values(s, g, (u - LAG) // 2)
                        elif u == 1 and not (first and g == 0):
                            values(s - 1, (g - 1) % G, KC - 1)

            batch(0, True, False)
            with pe.Fori(1, B - 1) as b:
                batch(b, False, False)
            batch(B - 1, False, True)
            values(B * G - 1, G - 1, KC - 1)
            n = SIDE_START + N_FIRST + N_MID * (B - 2) + N_LAST
            for i, name in enumerate(("T", "AT", "WO")):
                item(name, B, 0, n + i)

        @block.scalar
        def _(act):
            def item(name, b, g, n):
                if name[0] in "KVQ" or name == "AT":
                    act.wait_ge(side_ready, n + 1)
                if name[0] == "K":
                    c = int(name[1])
                    width = min(512, L - 512 * c)
                    if c == 0 and not (isinstance(b, int) and b == -1):
                        act.wait_ge(klow_ready, b + 1)
                    nc.scalar.activation(kfull[:, 512 * c:512 * c + width], side[:, 0:width], ACT.Identity,
                                         bias=bk[:, 0:1]).then_inc(kfull_ready, 1)
                    act.wait_ge(kfull_ready, 4 * b + 4 + c + 1)
                    nc.scalar.sem_inc(side_taken, 1)
                elif name[0] == "V":
                    v = int(name[1])
                    if v == 0:
                        act.wait_ge(vx_cleared, 2) if isinstance(b, int) and b == -1 else act.wait_ge(vx_ready, b * G + G)
                    if v < 3:
                        copied = nc.scalar.activation(vc[:, 4 * v:4 * v + 4, :].rearrange("p c d -> p (c d)"), side[:, :], ACT.Copy)
                    else:
                        copied = nc.scalar.activation(vc[0:LAST, KC - 1, :], side[0:LAST, 0:D], ACT.Copy)
                    copied.then_inc(side_taken, 1)
                elif name == "Q":
                    g2, b2 = (g + 2) % G, b + (g + 2) // G
                    s2 = step(b, g) + 2
                    if not (isinstance(s2, int) and s2 < 2):
                        act.wait_ge(qst_ready, 2 * (s2 - 1))
                    nc.scalar.activation(tq[g2 % 2][:, :], side[0:3 * ROWS, 0:S], ACT.Identity,
                                         scale=m["tau"][0:3 * ROWS, bass.ds(b2, 1)],
                                         bias=taubq[:, g2, bass.ds(b2, 1)]).then_inc(tq_ready, 1)
                    act.wait_ge(tq_ready, s2 + 1)
                    nc.scalar.sem_inc(side_taken, 1)
                elif name == "AT":
                    if not (isinstance(b, int) and b == 1):
                        act.wait_ge(wo_taken, b - 1)
                    nc.scalar.activation(attT[:, :], side[:, 0:S], ACT.Copy).then_inc(attT_ready, 1)
                    act.wait_ge(attT_ready, b)
                    nc.scalar.sem_inc(side_taken, 1)

            def take_output(s):
                act.wait_ge(pv_done, s * UNITS + UNITS)
                if not (isinstance(s, int) and s == 0):
                    act.wait_ge(att_done, s)
                nc.scalar.activation(osb[:, :], o_ps[:, 0:S], ACT.Copy).then_inc(o_taken, 1)

            act.wait_ge(w_in, LOADS * 16)
            act.wait_ge(taubq_ready, 1)
            for n, name in enumerate(["K0", "K1", "K2", "K3", "V0", "V1", "V2", "V3"]):
                item(name, -1, 1, n)
            for n, s in ((8, 0), (9, 1)):
                item("Q", 0, s - 2, n)

            def batch(b, first, last):
                items, _ = side_items(first, last)
                base = side_base(b, first, last)
                for g in range(G):
                    s = step(b, g)
                    for u in range(UNITS):
                        c = u // 2
                        act.wait_ge(scores_ready, s * UNITS + u + 1)
                        if not (first and g == 0 and u < 4):
                            act.wait_ge(pv_done, s * UNITS + u - 3 + (u % 2 == 0))
                        n = chunk_rows(c)
                        nc.scalar.activation(probs[(2 * g + u) % 4][0:n, :], score_ps[u % 2][0:n, :], ACT.Exp,
                                             scale=float(DK) ** -0.5).then_inc(exp_done, 1)
                        if u == 1 and not (first and g == 0):
                            take_output(s - 1)
                        if u in items[g]:
                            name, n = items[g][u]
                            item(name, b, g, base + n)

            batch(0, True, False)
            with act.Fori(1, B - 1) as b:
                batch(b, False, False)
            batch(B - 1, False, True)
            take_output(B * G - 1)
            item("AT", B, 0, SIDE_START + N_FIRST + N_MID * (B - 2) + N_LAST + 1)

        @block.vector
        def _(dve):
            def item(name, b, g, n):
                if name == "R":
                    g1 = (g + 1) % G
                    dve.wait_ge(side_ready, n + 1)
                    nc.vector.tensor_tensor(qst[g1][96:128, :, :], side[96:128, None, 0:S].to_broadcast([32, J, S]),
                                            m["shiftmask"][96:128, :, None].to_broadcast([32, J, S]), ALU.mult)\
                        .then_inc(shift_ready, 1)
                    dve.wait_ge(shift_ready, step(b, g) + 2)
                    nc.vector.sem_inc(side_taken, 1)
                elif name == "T":
                    g0 = (g - 1) % G
                    s0 = step(b, g) - 1
                    dve.wait_ge(side_ready, n + 1)
                    turned = side[:, 0:S].rearrange("p (q j r) -> p q j r", q=QT, r=32)
                    nc.vector.reciprocal(rcp[:, :, :], turned[:, :, :, DK]).then_inc(rcp_ready, 1)
                    dve.wait_ge(rcp_ready, s0 + 1)
                    if g0 == 0 and not (isinstance(b, int) and b == 0):
                        dve.wait_ge(attb_ready, b)
                    for q in range(QT):
                        last = nc.vector.tensor_tensor(att[:, q, g0 * ROWS:(g0 + 1) * ROWS].rearrange("p (j e) -> p j e", e=DK),
                                                       turned[:, q, :, 0:DK], rcp[:, q, :, None].to_broadcast([P, J, DK]), ALU.mult)
                    last.then_inc(att_done, 1)
                    dve.wait_ge(att_done, s0 + 1)
                    nc.vector.sem_inc(side_taken, 1)
                    if g0 == G - 1:
                        nc.vector.tensor_tensor(attb[:, :, :], att[:, :, :], bv[:, None, :].to_broadcast([P, QT, D]), ALU.add)\
                            .then_inc(attb_ready, 1)
                elif name == "WO":
                    dve.wait_ge(side_ready, n + 1)
                    nc.vector.tensor_tensor(wotmp[:, :].rearrange("p (q d) -> p q d", q=QT), side[:, 0:S].rearrange("p (q d) -> p q d", q=QT),
                                            bo[:, None, :].to_broadcast([P, QT, D]), ALU.add).then_inc(wo_taken, 1)
                    dve.wait_ge(wo_taken, b)
                    nc.vector.sem_inc(side_taken, 1)
                    xs = m["x"][:, bass.ds((b - 1) * S, S)]
                    nc.vector.tensor_tensor(xs, xs, wotmp[:, :], ALU.add).then_inc(x_added, 1)
                    dve.wait_ge(x_added, b)

            def reduce(s, k):
                j, q, half = k // (2 * QT), k // 2 % QT, k % 2
                if k == 0 and not (isinstance(s, int) and s == 0):
                    dve.wait_ge(max_ready, s)
                dve.wait_ge(guard_scored, s * GUARD_TILES + k + 1)
                nc.vector.tensor_reduce(partmax[:, q, j, half:half + 1], guard_ps[half][:, :].rearrange("p (i k) -> p i k", i=2)[:, :, 0:RUN], axis=AX.XY, op=ALU.max)\
                    .then_inc(guard_reduced, 1)

            def join(s):
                dve.wait_ge(guard_reduced, s * GUARD_TILES + GUARD_TILES)
                nc.vector.tensor_tensor(nm[:, :, 0:J], partmax[:, :, :, 0], partmax[:, :, :, 1], ALU.max).then_inc(max_ready, 1)

            dve.wait_ge(w_in, LOADS * 16)
            for g in range(G):
                last = nc.vector.tensor_scalar(taubq[:, g, :], m["tau"][0:3 * ROWS, :], bq[:, g:g + 1], None, ALU.mult)
            last.then_inc(taubq_ready, 1)
            for g in range(G):
                nc.vector.tensor_copy(kst[g][96:128, :], m["restmask"][96:128, 0:1].to_broadcast([32, L])).then_inc(kst_cleared, 1)
            for k in range(GUARD_TILES):
                reduce(0, k)
            join(0)
            item("R", 0, -1, 10)
            for k in sorted(EARLY):
                reduce(1, k)

            def batch(b, first, last):
                items, _ = side_items(first, last)
                base = side_base(b, first, last)
                for g in range(G):
                    s = step(b, g)
                    for u in range(UNITS):
                        for ahead, k in guard_tiles(u, g, last):
                            reduce(s + ahead, k)
                        if u == MAX_AT and not (last and g == G - 1):
                            join(s + 1)
                        if u in items[g]:
                            name, n = items[g][u]
                            item(name, b, g, base + n)

            batch(0, True, False)
            with dve.Fori(1, B - 1) as b:
                batch(b, False, False)
            batch(B - 1, False, True)
            n = SIDE_START + N_FIRST + N_MID * (B - 2) + N_LAST
            item("T", B, 0, n)
            item("WO", B, 0, n + 2)

        @block.gpsimd
        def _(pool):
            def spread(b, g, stacks):
                pool.wait_ge(qst_ready, 2 * stacks)
                if not (isinstance(b, int) and b == 0 and g == 0):
                    pool.wait_ge(vx_ready, step(b, g))
                nc.gpsimd.sem_inc(spread_turn, 1)
                nc.gpsimd.tensor_copy(vx[:, g * J:(g + 1) * J, :, 0:DK],
                                      vc[:, :, g * ROWS:(g + 1) * ROWS].rearrange("p c (j e) -> p j c e", e=DK)).then_inc(vx_ready, 1)

            def stack(b, g):
                g2, s2 = (g + 2) % G, step(b, g) + 2
                x, low = tq[g2 % 2], slice(2 * ROWS, 3 * ROWS)
                pool.wait_ge(tq_ready, s2 + 1)
                if not (isinstance(s2, int) and s2 < G):
                    pool.wait_ge(scores_ready, (s2 - 3) * UNITS)
                if not (isinstance(s2, int) and s2 == 0):
                    pool.wait_ge(qst_ready, 2 * s2)
                if g >= 0:
                    pool.wait_ge(vx_ready, G * b + G)
                    pool.wait_ge(klow_ready, b + 1 + (g >= 2))
                nc.gpsimd.sem_inc(split_turn, 1)
                nc.gpsimd.tensor_copy(tqh[low, :], x[low, :]).then_inc(tq_high, 1)
                pool.wait_ge(tq_high, s2 + 1)
                nc.gpsimd.tensor_tensor(x[low, :], x[low, :], tqh[low, :].bitcast(F32), ALU.subtract).then_inc(tq_split, 1)
                pool.wait_ge(tq_split, s2 + 1)
                nc.gpsimd.tensor_tensor(qst[g2][96:128, :, :], m["ident"][96:128, None, 0:1].to_broadcast([32, J, S]),
                                        m["restmask"][96:128, 1:2, None].to_broadcast([32, J, S]), ALU.add).then_inc(qst_ready, 1)
                pool.wait_ge(qst_ready, 2 * s2 + 1)
                nc.gpsimd.tensor_tensor(qst[g2][0:3 * ROWS, :, :], tq[g2 % 2][:, None, :].to_broadcast([3 * ROWS, J, S]),
                                        m["qmask"][0:3 * ROWS, :, None].to_broadcast([3 * ROWS, J, S]), ALU.mult).then_inc(qst_ready, 1)

            def split_keys(b, stacks):
                pool.wait_ge(kfull_ready, 4 * b + 8)
                if not (isinstance(b, int) and b == -1):
                    for filled in kst_in:
                        pool.wait_ge(filled, 64 * b + 64)
                    pool.wait_ge(qst_ready, 2 * stacks)
                nc.gpsimd.sem_inc(split_turn, 1)
                nc.gpsimd.tensor_copy(khigh[:, :], kfull[:, :]).then_inc(khigh_ready, 1)
                pool.wait_ge(khigh_ready, b + 2)
                nc.gpsimd.tensor_tensor(klow[:, :], kfull[:, :], khigh[:, :].bitcast(F32), ALU.subtract).then_inc(klow_ready, 1)

            nc.gpsimd.memset(vx[:, :, :, :], 1.0).then_inc(vx_cleared, 1)
            pool.wait_ge(vx_cleared, 1)
            nc.gpsimd.memset(vc[:, :, :], 0.0).then_inc(vx_cleared, 1)
            pool.wait_ge(vx_cleared, 2)
            split_keys(-1, 0)
            pool.wait_ge(klow_ready, 1)
            stack(0, -2)
            stack(0, -1)
            pool.wait_ge(side_taken, 8)
            for g in range(G):
                spread(0, g, 2)

            def batch(b, first, last):
                items, _ = side_items(first, last)
                base = side_base(b, first, last)
                for g in range(G):
                    if g == 0 and not first:
                        pool.wait_ge(pv_done, step(b, 0) * UNITS)
                        spread(b, 3, G * b + 2)
                    if not (last and g >= 2):
                        stack(b, g)
                    if g == 1 and not last:
                        split_keys(b, G * b + 4)
                    if g == 3 and not last:
                        n = [n for here in items for name, n in here.values() if name == "V3"][0]
                        pool.wait_ge(side_taken, base + n + 1)
                        for i in range(3):
                            pool.wait_ge(pv_done, step(b, i + 1) * UNITS)
                            spread(b + 1, i, G * b + 6)

            batch(0, True, False)
            with pool.Fori(1, B - 1) as b:
                batch(b, False, False)
            batch(B - 1, False, True)


def quantised_ffn(nc, t, m):
    HID, HC = 512, 4
    N_W = HID * D
    outer = ExitStack()
    with outer:
        xn = outer.enter_context(nc.sbuf_tensor("q_xn", [P, TOK], F32))
        norm(nc, t, m, "L0f", False, xn)
        ctx = outer

        def sb(name, shape, dt=F32):
            return ctx.enter_context(nc.sbuf_tensor(f"q_{name}", shape, dt))

        sems = []

        def sem(name):
            sems.append(ctx.enter_context(nc.semaphore(f"q_{name}")))
            return sems[-1]

        def psum(name, shape, dt=F32):
            return ctx.enter_context(nc.psum_tensor(f"q_{name}", shape, dt))

        w = sb("w", [P, 2, HID])
        scratch = sb("scratch", [P, TOK])
        wq = sb("wq", [P, 2, HID], BF16)
        identb = sb("identb", [P, P], BF16)
        ones = sb("ones", [P, P])
        wsum, ws, wr = sb("wsum", [P, 2]), sb("ws", [P, 2]), sb("wr", [P, 2])
        amax, xr, xs = sb("amax", [P, TILES]), sb("xr", [P, TILES]), sb("xs", [P, TILES])
        hscale = sb("hscale", [P, TILES])
        xq, xqT = sb("xq", [P, TOK], BF16), sb("xqT", [P, TOK], BF16)
        h = [sb(f"h{i}", [P, HID]) for i in range(2)]
        hr = [sb(f"hr{i}", [P, HID]) for i in range(2)]
        hq = [sb(f"hq{i}", [P, HID], BF16) for i in range(2)]
        hqT = [sb(f"hqT{i}", [P, HID], BF16) for i in range(2)]
        hmax = [sb(f"hmax{i}", [P, 4]) for i in range(2)]
        xT_ps = psum("xT_ps", [P, TOK], BF16)
        h_ps = [psum(f"h_ps{i}", [P, HID]) for i in range(2)]
        t_ps = [psum(f"t_ps{i}", [P, 1024], BF16) for i in range(2)]
        y_ps = [psum(f"y_ps{i}", [P, 512]) for i in range(2)]
        w_in, stepped, summed, totals, absolute, turned_x, xqT_ready = (
            sem(n) for n in ("w_in", "stepped", "summed", "totals", "absolute", "turned_x", "xqT_ready"))
        clip_turn = sem("clip_turn")
        h_ready, gelu_done, hstep, clipped, hq_ready, turned, hqT_ready, y_ready, x_added = (
            sem(n) for n in ("h_ready", "gelu_done", "hstep", "clipped", "hq_ready", "turned", "hqT_ready", "y_ready", "x_added"))
        FINAL_STEP = 14
        HSTEPS = 4
        xn3 = xn[:, :].rearrange("p (n d) -> p n d", d=D)
        sc3 = scratch[:, :].rearrange("p (n d) -> p n d", d=D)
        ctx.callback(clear, nc, sems)
        block = ctx.enter_context(nc.Block())

        @block.sync
        def _(sp):
            sp.dma_start(w[:, 0, :], t["L0_w1T"]).then_inc(w_in, 16)
            sp.dma_start(w[:, 1, :].rearrange("p (c d) -> p c d", c=HC), t["L0_w2T"].rearrange("(c p) d -> p c d", p=P)).then_inc(w_in, 16)
            sp.wait_ge(w_in, 32)

        @block.scalar
        def _(act):
            nc.scalar.activation(scratch[:, :], xn[:, :], ACT.Abs).then_inc(absolute, 1)
            act.wait_ge(w_in, 32)
            for i in range(2):
                nc.scalar.activation(h[i][:, :], w[:, i, :], ACT.Abs, accum_out=wsum[:, i:i + 1]).then_inc(summed, 1)
            act.wait_ge(turned_x, 1)
            nc.scalar.activation(xqT[:, :], xT_ps[:, :], ACT.Copy).then_inc(xqT_ready, 1)
            act.wait_ge(stepped, FINAL_STEP)

            def pair(b, first):
                for i in range(2):
                    n = 2 * b + i
                    act.wait_ge(h_ready, n + 1)
                    if not first:
                        act.wait_ge(hstep, HSTEPS * (n - 1))
                    nc.scalar.activation(h[i][:, :], h_ps[i][:, :], ACT.Gelu, scale=hscale[:, bass.ds(n, 1)]).then_inc(gelu_done, 1)
                for i in range(2):
                    n = 2 * b + i
                    act.wait_ge(turned, n + 1)
                    nc.scalar.activation(hqT[i][:, :], t_ps[i][:, 0:HID], ACT.Copy).then_inc(hqT_ready, 1)

            pair(0, True)
            with act.Fori(1, B) as b:
                pair(b, False)

        @block.vector
        def _(dve):
            k = 0

            def done(instruction):
                nonlocal k
                k += 1
                instruction.then_inc(stepped, 1)
                dve.wait_ge(stepped, k)

            done(nc.vector.memset(ones[:, :], 1.0))
            done(nc.vector.tensor_copy(identb[:, :], m["ident"][:, :]))
            dve.wait_ge(absolute, 1)
            done(nc.vector.tensor_reduce(amax[:, :], sc3, axis=AX.X, op=ALU.max))
            done(nc.vector.tensor_scalar(amax[:, :], amax[:, :], Q_EPS, None, ALU.max))
            done(nc.vector.reciprocal(xr[:, :], amax[:, :]))
            done(nc.vector.tensor_scalar(xs[:, :], xr[:, :], 127.0, None, ALU.mult))
            done(nc.vector.tensor_tensor(sc3, xn3, xs[:, :, None].to_broadcast([P, TILES, D]), ALU.mult))
            done(nc.vector.tensor_scalar(scratch[:, :], scratch[:, :], ROUND, ROUND, ALU.add, ALU.subtract))
            done(nc.vector.tensor_scalar(xq[:, :], scratch[:, :], 127.0, -128.0, ALU.min, ALU.max))
            dve.wait_ge(totals, 1)
            done(nc.vector.tensor_scalar(ws[:, :], y_ps[0][:, 0:2], 1.0 / N_W, Q_EPS, ALU.mult, ALU.max))
            done(nc.vector.reciprocal(wr[:, :], ws[:, :]))
            for i in range(2):
                nc.vector.tensor_scalar(w[:, i, :], w[:, i, :], wr[:, i:i + 1], ROUND, ALU.mult, ALU.add).then_inc(totals, 1)
                dve.wait_ge(totals, 2 + 2 * i)
                nc.vector.tensor_scalar(w[:, i, :], w[:, i, :], ROUND, -1.0, ALU.subtract, ALU.max).then_inc(totals, 1)
                dve.wait_ge(totals, 3 + 2 * i)
                last = nc.vector.tensor_scalar(wq[:, i, :], w[:, i, :], 1.0, None, ALU.min)
            done(last)
            done(nc.vector.tensor_scalar(hscale[:, :], amax[:, :], ws[:, 0:1], 1.0 / 127.0, ALU.mult, ALU.mult))
            done(nc.vector.tensor_scalar(ws[:, :], ws[:, :], 1.0 / 127.0, None, ALU.mult))
            assert k == FINAL_STEP

            def pair(b, first):
                for i in range(2):
                    n = 2 * b + i
                    q = hmax[i]
                    dve.wait_ge(gelu_done, n + 1)
                    nc.vector.tensor_reduce(q[:, 0:1], h[i][:, :], axis=AX.X, op=ALU.max, apply_absolute_value=True).then_inc(hstep, 1)
                    dve.wait_ge(hstep, HSTEPS * n + 1)
                    nc.vector.tensor_scalar(q[:, 1:2], q[:, 0:1], Q_EPS, None, ALU.max).then_inc(hstep, 1)
                    dve.wait_ge(hstep, HSTEPS * n + 2)
                    nc.vector.reciprocal(q[:, 2:3], q[:, 1:2]).then_inc(hstep, 1)
                    dve.wait_ge(hstep, HSTEPS * n + 3)
                    nc.vector.tensor_scalar(hr[i][:, :], h[i][:, :], q[:, 2:3], 127.0, ALU.mult, ALU.mult).then_inc(hstep, 1)
                    dve.wait_ge(hstep, HSTEPS * n + 4)
                    nc.vector.tensor_scalar(hr[i][:, :], hr[i][:, :], ROUND, ROUND, ALU.add, ALU.subtract).then_inc(clipped, 1)
                    nc.vector.tensor_scalar(q[:, 3:4], q[:, 1:2], ws[:, 1:2], None, ALU.mult).then_inc(clipped, 1)
                for i in range(2):
                    n = 2 * b + i
                    xt = m["x"][:, bass.ds(n * P, P)]
                    dve.wait_ge(y_ready, n + 1)
                    dve.wait_ge(clipped, 2 * n + 2)
                    nc.vector.scalar_tensor_tensor(xt, y_ps[i][:, 0:D], hmax[i][:, 3:4], xt, ALU.mult, ALU.add).then_inc(x_added, 1)
                dve.wait_ge(x_added, 2 * b + 2)

            pair(0, True)
            with dve.Fori(1, B) as b:
                pair(b, False)

        @block.gpsimd
        def _(pool):
            def pair(b, first):
                for i in range(2):
                    n = 2 * b + i
                    pool.wait_ge(clipped, 2 * n + 1)
                    if not first:
                        pool.wait_ge(turned, n - 1)
                    nc.gpsimd.sem_inc(clip_turn, 1)
                    nc.gpsimd.tensor_scalar(hq[i][:, :], hr[i][:, :], 127.0, -128.0, ALU.min, ALU.max).then_inc(hq_ready, 1)

            pair(0, True)
            with pool.Fori(1, B) as b:
                pair(b, False)

        @block.tensor
        def _(pe):
            pe.wait_ge(stepped, 9)
            for i in range(TILES):
                last = nc.tensor.transpose(xT_ps[:, i * P:(i + 1) * P], xq[:, i * P:(i + 1) * P], identb[:, :])
            last.then_inc(turned_x, 1)
            pe.wait_ge(summed, 2)
            nc.tensor.matmul(y_ps[0][:, 0:2], ones[:, :], wsum[:, :], start=True, stop=True).then_inc(totals, 1)
            pe.wait_ge(stepped, FINAL_STEP)
            pe.wait_ge(xqT_ready, 1)

            def pair(b, first):
                for i in range(2):
                    n = 2 * b + i
                    if not first:
                        pe.wait_ge(gelu_done, n - 1)
                    nc.tensor.matmul(h_ps[i][:, :], xqT[:, bass.ds(n * P, P)], wq[:, 0, :], start=True, stop=True).then_inc(h_ready, 1)
                for i in range(2):
                    n = 2 * b + i
                    pe.wait_ge(hq_ready, n + 1)
                    if not first:
                        pe.wait_ge(hqT_ready, n - 1)
                    for c in range(HC):
                        last = nc.tensor.transpose(t_ps[i][:, c * P:(c + 1) * P], hq[i][:, c * P:(c + 1) * P], identb[:, :])
                    last.then_inc(turned, 1)
                for i in range(2):
                    n = 2 * b + i
                    pe.wait_ge(hqT_ready, n + 1)
                    if not first:
                        pe.wait_ge(x_added, n - 1)
                    for c in range(HC):
                        last = nc.tensor.matmul(y_ps[i][:, 0:D], hqT[i][:, c * P:(c + 1) * P], wq[:, 1, c * P:(c + 1) * P],
                                                start=c == 0, stop=c == HC - 1)
                    last.then_inc(y_ready, 1)

            pair(0, True)
            with pe.Fori(1, B) as b:
                pair(b, False)


MIXTURES = {
    1: dict(chunks=4, up=1024, gated=0, linear=512, up_at=0, down_at=E * 1024),
    2: dict(chunks=1, up=256, gated=0, linear=128, up_at=0, down_at=E * 256),
    3: dict(chunks=2, up=512, gated=256, linear=0, up_at=E * 384, down_at=E * 896),
}


def route(nc, t, m, layer, shareT):
    tag = f"r{layer}"
    with ExitStack() as ctx:
        def sb(name, shape, dt=F32):
            return ctx.enter_context(nc.sbuf_tensor(f"{tag}_{name}", shape, dt))

        sems = []

        def sem(name):
            sems.append(ctx.enter_context(nc.semaphore(f"{tag}_{name}")))
            return sems[-1]

        gate = sb("gate", [P, E])
        number = sb("number", [P, E])
        score, share, other = (sb(n, [P, TILES, E]) for n in ("score", "share", "other"))
        best, where = sb("best", [P, TILES, 8]), sb("where", [P, TILES, 8], U32)
        wheref = sb("wheref", [P, TILES, 2])
        small = sb("small", [P, 6, TILES])
        a, b_, c_, w1, w2, d_ = (small[:, i, :] for i in range(6))
        s_ps = ctx.enter_context(nc.psum_tensor(f"{tag}_s_ps", [P, TILES * E], F32))
        t_ps = [ctx.enter_context(nc.psum_tensor(f"{tag}_t_ps{i}", [P, 512], F32)) for i in range(4)]
        loaded, scored, stepped, raised, turned = (sem(n) for n in ("loaded", "scored", "stepped", "raised", "turned"))
        softmax_first = layer == 2
        ctx.callback(clear, nc, sems)
        block = ctx.enter_context(nc.Block())

        @block.sync
        def _(sp):
            sp.dma_start(gate[:, :], t[f"L{layer}_gateT"]).then_inc(loaded, 16)
            sp.dma_start(number[:, :], t["numbers"][None, 0:E].to_broadcast([P, E])).then_inc(loaded, 16)
            sp.wait_ge(loaded, 32)

        steps_to_raise = 3 if softmax_first else 2 + 2
        steps = {}

        @block.vector
        def _(dve):
            k = 0

            def done(instruction):
                nonlocal k
                k += 1
                instruction.then_inc(stepped, 1)
                dve.wait_ge(stepped, k)

            def wide(v):
                return v[:, :, None].to_broadcast([P, TILES, E])

            dve.wait_ge(scored, 1)
            done(nc.vector.tensor_copy(score[:, :, :], s_ps[:, :].rearrange("p (n e) -> p n e", e=E)))
            if softmax_first:
                done(nc.vector.tensor_reduce(a, score[:, :, :], axis=AX.X, op=ALU.max))
                done(nc.vector.tensor_tensor(score[:, :, :], score[:, :, :], wide(a), ALU.subtract))
                dve.wait_ge(raised, 1)
                done(nc.vector.tensor_reduce(a, other[:, :, :], axis=AX.X, op=ALU.add))
                done(nc.vector.reciprocal(b_, a))
                done(nc.vector.tensor_tensor(score[:, :, :], other[:, :, :], wide(b_), ALU.mult))
            for i in range(TILES):
                last = nc.vector.max(best[:, i, :], score[:, i, :])
            done(last)
            for i in range(TILES):
                last = nc.vector.max_index(where[:, i, :], best[:, i, :], score[:, i, :])
            first, second = best[:, :, 0], best[:, :, 1]
            if softmax_first:
                done(last)
                done(nc.vector.tensor_copy(wheref[:, :, :], where[:, :, 0:2]))
                done(nc.vector.tensor_tensor(a, first, second, ALU.add))
                done(nc.vector.tensor_scalar(a, a, L2_EPS, None, ALU.add))
                done(nc.vector.reciprocal(b_, a))
                done(nc.vector.tensor_tensor(w1, first, b_, ALU.mult))
                done(nc.vector.tensor_tensor(w2, second, b_, ALU.mult))
                done(nc.vector.tensor_tensor(a, w1, w2, ALU.add))
                done(nc.vector.tensor_scalar(a, a, L2_EPS, None, ALU.add))
                done(nc.vector.reciprocal(b_, a))
                done(nc.vector.tensor_tensor(w1, w1, b_, ALU.mult))
                done(nc.vector.tensor_tensor(w2, w2, b_, ALU.mult))
            else:
                done(last)
                done(nc.vector.tensor_tensor(a, second, first, ALU.subtract))
                done(nc.vector.tensor_copy(wheref[:, :, :], where[:, :, 0:2]))
                dve.wait_ge(raised, 1)
                done(nc.vector.tensor_scalar(b_, c_, 1.0, None, ALU.add))
                done(nc.vector.reciprocal(w1, b_))
                done(nc.vector.tensor_tensor(w2, c_, w1, ALU.mult))
            numbers = number[:, None, :].to_broadcast([P, TILES, E])
            done(nc.vector.tensor_tensor(share[:, :, :], numbers, wide(wheref[:, :, 0]), ALU.is_equal))
            done(nc.vector.tensor_tensor(other[:, :, :], numbers, wide(wheref[:, :, 1]), ALU.is_equal))
            done(nc.vector.tensor_tensor(share[:, :, :], share[:, :, :], wide(w1), ALU.mult))
            done(nc.vector.tensor_tensor(other[:, :, :], other[:, :, :], wide(w2), ALU.mult))
            done(nc.vector.tensor_tensor(share[:, :, :], share[:, :, :], other[:, :, :], ALU.add))
            steps["all"] = k
            for i in (1, 3):
                dve.wait_ge(turned, i + 1)
                nc.vector.tensor_copy(shareT[0:E, i * 512:(i + 1) * 512], t_ps[i][0:E, :])

        @block.scalar
        def _(act):
            act.wait_ge(stepped, steps_to_raise)
            if softmax_first:
                nc.scalar.activation(other[:, :, :], score[:, :, :], ACT.Exp).then_inc(raised, 1)
            else:
                nc.scalar.activation(c_, a, ACT.Exp).then_inc(raised, 1)
            for i in (0, 2):
                act.wait_ge(turned, i + 1)
                nc.scalar.activation(shareT[0:E, i * 512:(i + 1) * 512], t_ps[i][0:E, :], ACT.Copy)

        @block.tensor
        def _(pe):
            pe.wait_ge(loaded, 32)
            for i in range(TILES):
                last = nc.tensor.matmul(s_ps[:, i * E:(i + 1) * E], m["xnT"][:, i * P:(i + 1) * P], gate[:, :], start=True, stop=True)
            last.then_inc(scored, 1)
            pe.wait_ge(stepped, steps["all"])
            for i in range(4):
                for k in range(4):
                    last = nc.tensor.transpose(t_ps[i][0:E, k * P:(k + 1) * P], share[:, 4 * i + k, :], m["ident"][:, :])
                last.then_inc(turned, 1)


def experts(nc, t, m, layer, weights_in, arrived):
    shape = MIXTURES[layer]
    NC, tag = shape["chunks"], f"e{layer}"
    W = EXPERT_TOK
    GROUPS = TOK // W
    outer = ExitStack()
    with outer:
        ctx = outer
        shareT = outer.enter_context(nc.sbuf_tensor(f"{tag}_shareT", [E, TOK], F32))
        route(nc, t, m, layer, shareT)

        def sb(name, shape_, dt=F32):
            return ctx.enter_context(nc.sbuf_tensor(f"{tag}_{name}", shape_, dt))

        sems = []

        def sem(name):
            sems.append(ctx.enter_context(nc.semaphore(f"{tag}_{name}")))
            return sems[-1]

        def psum(name):
            return ctx.enter_context(nc.psum_tensor(f"{tag}_{name}", [P, W], F32))

        select = sb("select", [E, E, P])
        xc = [sb(f"xc{i}", [P, W]) for i in range(2)]
        gated = [sb(f"gated{i}", [P, W]) for i in range(2)]
        hid = [sb(f"hid{i}", [P, W]) for i in range(2)]
        ysb = sb("ysb", [P, W])
        share_ps, y_ps, t_ps = psum("share_ps"), psum("y_ps"), psum("t_ps")
        g_ps, l_ps = [psum(f"g_ps{i}") for i in range(2)], [psum(f"l_ps{i}") for i in range(2)]
        select_in, share_ready, xc_ready, gate_ready, linear_ready, silu_done, hid_ready, down_done = (
            sem(n) for n in ("select_in", "share_ready", "xc_ready", "gate_ready", "linear_ready", "silu_done", "hid_ready", "down_done"))
        y_taken, turned, x_added, share_turn = sem("y_taken"), sem("turned"), sem("x_added"), sem("share_turn")
        up = m["wffn"][:, shape["up_at"]:shape["up_at"] + E * shape["up"]].rearrange("p (e n) -> p e n", e=E)
        down = m["wffn"][:, shape["down_at"]:shape["down_at"] + E * NC * P].rearrange("p (e n) -> p e n", e=E)
        ctx.callback(clear, nc, sems)
        block = ctx.enter_context(nc.Block())

        @block.sync
        def _(sp):
            sp.dma_start(select[:, :, :], t["select"]).then_inc(select_in, 16)
            sp.wait_ge(select_in, 16)

        @block.tensor
        def _(pe):
            pe.wait_ge(select_in, 16)
            pe.wait_ge(weights_in, arrived)

            def group(r, first):
                tokens = bass.ds(r * W, W)
                w0 = r * E

                def shares(e):
                    if not (first and e == 0):
                        pe.wait_ge(xc_ready, w0 + e)
                    nc.tensor.sem_inc(share_turn, 1)
                    nc.tensor.matmul(share_ps[:, :], select[:, e, :], shareT[:, tokens], start=True, stop=True).then_inc(share_ready, 1)

                def product_down(v):
                    e, c = v // NC, v % NC
                    pe.wait_ge(hid_ready, w0 * NC + v + 1)
                    nc.tensor.matmul(y_ps[:, :], down[:, e, c * P:(c + 1) * P], hid[v % 2][:, :],
                                     start=v == 0, stop=v == E * NC - 1).then_inc(down_done, 1)

                shares(0)
                for e in range(E):
                    for c in range(NC):
                        v = e * NC + c
                        at = shape["gated"] + c * P
                        if not (first and v < 2):
                            pe.wait_ge(silu_done, w0 * NC + v - 1)
                        nc.tensor.matmul(g_ps[v % 2][:, :], up[:, e, at:at + P], m["xnT"][:, tokens], start=True, stop=True).then_inc(gate_ready, 1)
                        if c == 0:
                            pe.wait_ge(xc_ready, w0 + e + 1)
                        if not (first and v < 2):
                            pe.wait_ge(hid_ready, w0 * NC + v - 1)
                        at = shape["linear"] + c * P
                        nc.tensor.matmul(l_ps[v % 2][:, :], up[:, e, at:at + P], xc[e % 2][:, :], start=True, stop=True).then_inc(linear_ready, 1)
                        if c == 0 and e + 1 < E:
                            shares(e + 1)
                        if v == 1 and not first:
                            pe.wait_ge(y_taken, r)
                        if v >= 1:
                            product_down(v - 1)
                product_down(E * NC - 1)
                pe.wait_ge(y_taken, r + 1)
                if not first:
                    pe.wait_ge(x_added, r)
                for k in range(W // P):
                    last = nc.tensor.transpose(t_ps[:, k * P:(k + 1) * P], ysb[:, k * P:(k + 1) * P], m["ident"][:, :])
                last.then_inc(turned, 1)

            group(0, True)
            with pe.Fori(1, GROUPS) as r:
                group(r, False)

        @block.scalar
        def _(act):
            def group(r, first):
                for v in range(E * NC):
                    n = r * E * NC + v
                    act.wait_ge(gate_ready, n + 1)
                    if not (first and v < 2):
                        act.wait_ge(hid_ready, n - 1)
                    nc.scalar.activation(gated[v % 2][:, :], g_ps[v % 2][:, :], ACT.Silu).then_inc(silu_done, 1)
                act.wait_ge(down_done, (r + 1) * E * NC)
                if not first:
                    act.wait_ge(turned, r)
                nc.scalar.activation(ysb[:, :], y_ps[:, :], ACT.Copy).then_inc(y_taken, 1)

            group(0, True)
            with act.Fori(1, GROUPS) as r:
                group(r, False)

        @block.vector
        def _(dve):
            def group(r, first):
                tokens = bass.ds(r * W, W)
                w0 = r * E

                def scale_input(e):
                    dve.wait_ge(share_ready, w0 + e + 1)
                    if not (first and e < 2):
                        dve.wait_ge(linear_ready, (w0 + e - 1) * NC)
                    nc.vector.tensor_tensor(xc[e % 2][:, :], m["xnT"][:, tokens], share_ps[:, :], ALU.mult).then_inc(xc_ready, 1)

                scale_input(0)
                for e in range(E):
                    if e + 1 < E:
                        scale_input(e + 1)
                    for c in range(NC):
                        v = e * NC + c
                        n = w0 * NC + v
                        dve.wait_ge(silu_done, n + 1)
                        dve.wait_ge(linear_ready, n + 1)
                        if not (first and v < 2):
                            dve.wait_ge(down_done, n - 1)
                        nc.vector.tensor_tensor(hid[v % 2][:, :], gated[v % 2][:, :], l_ps[v % 2][:, :], ALU.mult).then_inc(hid_ready, 1)
                xs = m["x"][:, tokens]
                dve.wait_ge(turned, r + 1)
                nc.vector.tensor_tensor(xs, xs, t_ps[:, :], ALU.add).then_inc(x_added, 1)

            group(0, True)
            with dve.Fori(1, GROUPS) as r:
                group(r, False)


def local_attention(nc, t, m, weights_in):
    WINDOW, POWER, MASKED = 16.0, 128.0, 1e9
    with ExitStack() as ctx:
        sems = []

        def sem(name):
            sems.append(ctx.enter_context(nc.semaphore(f"w_{name}")))
            return sems[-1]

        def sb(name, shape, dt=F32):
            return ctx.enter_context(nc.sbuf_tensor(f"w_{name}", shape, dt))

        def psum(name, cols):
            return ctx.enter_context(nc.psum_tensor(f"w_{name}", [P, cols], F32))

        wa, wc = sb("wa", [P, D]), sb("wc", [P, 2, D])
        number = sb("number", [P, L])
        keyno = sb("keyno", [P, KC])
        centre, length = sb("centre", [P, B]), sb("length", [P, B])
        length_int = sb("length_int", [P, B], I32)
        start, end = sb("start", [P, B]), sb("end", [P, B])
        bounds = sb("bounds", [P, 2])
        gauss = sb("gauss", [P, B, KC])
        gauss_now = sb("gauss_now", [P, KC])
        ctxT, ctxv = sb("ctxT", [P, L]), sb("ctxv", [P, L])
        ctxn, ctxg = sb("ctxn", [P, KC, D]), sb("ctxg", [P, KC, D])
        after, valid, below = sb("after", [P, L]), sb("valid", [P, L]), sb("below", [P, L])
        aT = sb("aT", [P, S])
        masked = [sb(f"masked{i}", [P, L]) for i in range(QT)]
        alT = sb("alT", [P, KC, S])
        stat = [sb(f"stat{i}", [P, 4]) for i in range(QT)]
        cT, hT = sb("cT", [P, S]), sb("hT", [P, S])
        s_ps = psum("s_ps", 2048)
        t_ps = [psum(f"t_ps{i}", 512) for i in range(2)]
        c_ps, o_ps = psum("c_ps", 512), psum("o_ps", 512)
        w_in, ctx_in, ctxn_in, stepped, gauss_ready, gauss_now_ready, bounds_ready, after_ready, valid_ready = (
            sem(n) for n in ("w_in", "ctx_in", "ctxn_in", "stepped", "gauss_ready", "gauss_now_ready", "bounds_ready", "after_ready", "valid_ready"))
        keys_ready, below_ready, values_step, values_ready, score_turn = (
            sem(n) for n in ("keys_ready", "below_ready", "values_step", "values_ready", "score_turn"))
        a_ready, a_taken, scored, masked_ready, minus_ready, exped, inverse_ready, aligned, turned = (
            sem(n) for n in ("a_ready", "a_taken", "scored", "masked_ready", "minus_ready", "exped", "inverse_ready", "aligned", "turned"))
        alT_ready = [sem(f"alT_ready_{engine}") for engine in ("scalar", "vector")]
        c_ready, cT_ready, o_ready, hT_ready, o_turned, x_added = (
            sem(n) for n in ("c_ready", "cT_ready", "o_ready", "hT_ready", "o_turned", "x_added"))
        N_IN = 6
        TURNS = -(-KC // 4)
        FIRST_STEPS = 6

        def take_turned(copy, q, i, **more):
            chunks = range(4 * i, min(4 * i + 4, KC))
            n = len(chunks) * P
            rows = P if i < TURNS - 1 else LAST
            return copy(alT[0:rows, 4 * i:4 * i + len(chunks), q * P:(q + 1) * P],
                        t_ps[i % 2][0:rows, 0:n].rearrange("p (c q) -> p c q", q=P), **more)

        ctx.callback(clear, nc, sems)
        block = ctx.enter_context(nc.Block())

        @block.sync
        def _(sp):
            sp.dma_start(wa[:, :], t["L2_xcond_W_a"]).then_inc(w_in, 16)
            sp.dma_start(wc[:, :, :], t["L2_WcT"].rearrange("(a p) o -> p a o", p=P)).then_inc(w_in, 16)
            sp.dma_start(number[:, :], t["numbers"][None, :].to_broadcast([P, L])).then_inc(w_in, 16)
            sp.dma_start(keyno[:, :], t["key_numbers"]).then_inc(w_in, 16)
            sp.dma_start(centre[:, :], t["condB_pt"][None, :].to_broadcast([P, B])).then_inc(w_in, 16)
            sp.dma_start(length_int[:, :], t["_lenS2"][None, :].to_broadcast([P, B])).then_inc(w_in, 16)

            def load_keys(n):
                sp.dma_start(ctxT[:, :], t["ctxT"][bass.ds(n, 1), :, :].rearrange("o p l -> (o p) l")).then_inc(ctx_in, 16)

            def load_values(n):
                sp.dma_start(ctxn[:, 0:KC - 1, :], t["ctx_1024"][bass.ds(n, 1), 0:L - LAST, :].rearrange("o (c p) d -> (o p) c d", p=P)).then_inc(ctxn_in, 16)
                sp.dma_start(ctxn[0:LAST, KC - 1, :], t["ctx_1024"][bass.ds(n, 1), L - LAST:L, :].rearrange("o p d -> (o p) d")).then_inc(ctxn_in, 16)

            load_keys(0)
            load_values(0)
            sp.wait_ge(keys_ready, 1)
            load_keys(1)
            for layer in (2, 3):
                shape = MIXTURES[layer]
                up, down = E * shape["up"], E * shape["chunks"] * P
                sp.dma_start(m["wffn"][:, shape["up_at"]:shape["up_at"] + up].rearrange("p (e n) -> p e n", e=E), t[f"L{layer}_up"]).then_inc(weights_in, 16)
                sp.dma_start(m["wffn"][:, shape["down_at"]:shape["down_at"] + down].rearrange("p (e n) -> p e n", e=E), t[f"L{layer}_down"]).then_inc(weights_in, 16)
            with sp.Fori(1, B - 1) as n:
                sp.wait_ge(values_ready, n)
                load_values(n)
                sp.wait_ge(keys_ready, n + 1)
                load_keys(n + 1)
            sp.wait_ge(values_ready, B - 1)
            load_values(B - 1)
            sp.wait_ge(w_in, 16 * N_IN)
            sp.wait_ge(ctxn_in, 32 * B)

        @block.gpsimd
        def _(pool):
            def keys(n, first):
                pool.wait_ge(ctx_in, 16 * n + 16)
                pool.wait_ge(valid_ready, n + 1)
                if not first:
                    pool.wait_ge(scored, 2 * n)
                nc.gpsimd.tensor_tensor(ctxv[:, :], ctxT[:, :], valid[:, :], ALU.mult).then_inc(keys_ready, 1)
                pool.wait_ge(keys_ready, n + 1)

            def values(n, first):
                pool.wait_ge(ctxn_in, 32 * n + 32)
                pool.wait_ge(gauss_now_ready, n + 1)
                if not first:
                    pool.wait_ge(c_ready, n)
                nc.gpsimd.tensor_tensor(ctxg[:, 0:KC - 1, :], ctxn[:, 0:KC - 1, :],
                                        gauss_now[:, 0:KC - 1, None].to_broadcast([P, KC - 1, D]), ALU.mult).then_inc(values_step, 1)
                pool.wait_ge(values_step, n + 1)
                nc.gpsimd.tensor_tensor(ctxg[0:LAST, KC - 1, :], ctxn[0:LAST, KC - 1, :],
                                        gauss_now[0:LAST, KC - 1:KC].to_broadcast([LAST, D]), ALU.mult).then_inc(values_ready, 1)
                pool.wait_ge(values_ready, n + 1)

            keys(0, True)
            values(0, True)
            with pool.Fori(1, B) as n:
                keys(n, False)
                values(n, False)

        @block.vector
        def _(dve):
            dve.wait_ge(w_in, 16 * N_IN)
            k = 0

            def done(instruction):
                nonlocal k
                k += 1
                instruction.then_inc(stepped, 1)
                dve.wait_ge(stepped, k)

            done(nc.vector.tensor_copy(length[:, :], length_int[:, :]))
            done(nc.vector.tensor_scalar(start[:, :], centre[:, :], WINDOW, 0.0, ALU.subtract, ALU.max))
            done(nc.vector.tensor_scalar(end[:, :], centre[:, :], WINDOW, None, ALU.add))
            done(nc.vector.tensor_tensor(end[:, :], end[:, :], length[:, :], ALU.min))
            keyno3, centre3 = keyno[:, None, :].to_broadcast([P, B, KC]), centre[:, :, None].to_broadcast([P, B, KC])
            done(nc.vector.tensor_tensor(gauss[:, :, :], keyno3, centre3, ALU.subtract))
            done(nc.vector.tensor_tensor(gauss[:, :, :], gauss[:, :, :], gauss[:, :, :], ALU.mult))
            assert k == FIRST_STEPS
            dve.wait_ge(gauss_ready, 1)

            def window(n, first):
                for i, column in enumerate((start, end)):
                    if not first:
                        dve.wait_ge(valid_ready, n)
                    nc.vector.tensor_copy(bounds[:, i:i + 1], column[:, bass.ds(n, 1)]).then_inc(bounds_ready, 1)
                dve.wait_ge(bounds_ready, 2 * n + 2)
                nc.vector.tensor_scalar(after[:, :], number[:, :], bounds[:, 0:1], None, ALU.is_ge).then_inc(after_ready, 1)
                dve.wait_ge(after_ready, n + 1)
                if not first:
                    dve.wait_ge(keys_ready, n)
                    dve.wait_ge(below_ready, n)
                nc.vector.scalar_tensor_tensor(valid[:, :], number[:, :], bounds[:, 1:2], after[:, :], ALU.is_le, ALU.mult).then_inc(valid_ready, 1)

            def addend(n, first):
                dve.wait_ge(valid_ready, n + 1)
                if not first:
                    dve.wait_ge(masked_ready, 2 * n)
                nc.vector.tensor_scalar(below[:, :], valid[:, :], -1.0, MASKED, ALU.add, ALU.mult).then_inc(below_ready, 1)

            def factors(n, first):
                if not first:
                    dve.wait_ge(values_ready, n)
                nc.vector.tensor_copy(gauss_now[:, :], gauss[:, bass.ds(n, 1), :].rearrange("p o c -> p (o c)")).then_inc(gauss_now_ready, 1)

            def mask(n, q, first):
                i = 2 * n + q
                dve.wait_ge(scored, i + 1)
                dve.wait_ge(below_ready, n + 1)
                if not first:
                    dve.wait_ge(turned, (i - 1) * TURNS)
                nc.vector.sem_inc(score_turn, 1)
                nc.vector.tensor_tensor_reduce(masked[q][:, :], s_ps[:, 0:L], below[:, :], 1.0, -3.4e38, ALU.add, ALU.max,
                                               stat[q][:, 0:1]).then_inc(masked_ready, 1)
                dve.wait_ge(masked_ready, i + 1)
                nc.vector.tensor_scalar(stat[q][:, 1:2], stat[q][:, 0:1], -1.0, None, ALU.mult).then_inc(minus_ready, 1)

            def divide(n, q):
                i = 2 * n + q
                dve.wait_ge(exped, i + 1)
                nc.vector.reciprocal(stat[q][:, 3:4], stat[q][:, 2:3]).then_inc(inverse_ready, 1)
                dve.wait_ge(inverse_ready, i + 1)
                nc.vector.tensor_scalar(masked[q][:, :], masked[q][:, :], stat[q][:, 3:4], None, ALU.mult).then_inc(aligned, 1)

            def take(b, q):
                for i in (1, 3):
                    dve.wait_ge(turned, (2 * b + q) * TURNS + i + 1)
                    take_turned(nc.vector.tensor_copy, q, i).then_inc(alT_ready[1], 1)

            def batch(b, last, before_last):
                take(b, 0)
                if not last:
                    mask(b + 1, 0, False)
                take(b, 1)
                if not last:
                    mask(b + 1, 1, False)
                if not (last or before_last):
                    window(b + 2, False)
                if not last:
                    divide(b + 1, 0)
                if not (last or before_last):
                    addend(b + 2, False)
                if not last:
                    divide(b + 1, 1)
                dve.wait_ge(c_ready, b + 1)
                nc.vector.tensor_copy(cT[:, :], c_ps[:, 0:S]).then_inc(cT_ready, 1)
                if not last:
                    factors(b + 1, False)
                dve.wait_ge(o_turned, b + 1)
                xs = m["x"][:, bass.ds(b * S, S)]
                nc.vector.tensor_tensor(xs, xs, c_ps[:, 0:S], ALU.add).then_inc(x_added, 1)

            window(0, True)
            addend(0, True)
            factors(0, True)
            for q in range(QT):
                mask(0, q, True)
            for q in range(QT):
                divide(0, q)
            window(1, False)
            addend(1, False)
            batch(0, False, False)
            with dve.Fori(1, B - 2) as b:
                batch(b, False, False)
            batch(B - 2, False, True)
            batch(B - 1, True, False)

        @block.scalar
        def _(act):
            act.wait_ge(stepped, FIRST_STEPS)
            nc.scalar.activation(gauss[:, :, :], gauss[:, :, :], ACT.Exp, scale=-1.0 / POWER).then_inc(gauss_ready, 1)

            def take_a(n):
                act.wait_ge(a_ready, n + 1)
                nc.scalar.activation(aT[:, :], o_ps[:, 0:S], ACT.Copy).then_inc(a_taken, 1)

            def exp(n, q):
                act.wait_ge(minus_ready, 2 * n + q + 1)
                nc.scalar.activation(masked[q][:, :], masked[q][:, :], ACT.Exp, bias=stat[q][:, 1:2],
                                     accum_out=stat[q][:, 2:3]).then_inc(exped, 1)

            def take(b, q, first):
                for i in (0, 2):
                    act.wait_ge(turned, (2 * b + q) * TURNS + i + 1)
                    if not first:
                        act.wait_ge(c_ready, b)
                    take_turned(nc.scalar.activation, q, i, func=ACT.Copy).then_inc(alT_ready[0], 1)

            def batch(b, first, last):
                take(b, 0, first)
                take(b, 1, first)
                if not last:
                    exp(b + 1, 0)
                    exp(b + 1, 1)
                act.wait_ge(o_ready, b + 1)
                nc.scalar.activation(hT[:, :], o_ps[:, 0:S], ACT.Tanh).then_inc(hT_ready, 1)
                if not (isinstance(b, int) and b >= B - 2):
                    take_a(b + 2)

            take_a(0)
            exp(0, 0)
            exp(0, 1)
            take_a(1)
            batch(0, True, False)
            with act.Fori(1, B - 2) as b:
                batch(b, False, False)
            batch(B - 2, False, False)
            batch(B - 1, False, True)

        @block.tensor
        def _(pe):
            pe.wait_ge(w_in, 16 * N_IN)

            def queries(b):
                return m["xnT"][:, bass.ds(b * S, S)]

            def product_a(n):
                nc.tensor.matmul(o_ps[:, 0:S], wa[:, :], queries(n), start=True, stop=True).then_inc(a_ready, 1)

            def scores(n, q, first):
                if q == 0:
                    pe.wait_ge(a_taken, n + 1)
                    pe.wait_ge(keys_ready, n + 1)
                if not first:
                    pe.wait_ge(masked_ready, 2 * n + q)
                for i in range(TURNS):
                    width = min(512, L - 512 * i)
                    last = nc.tensor.matmul(s_ps[:, 512 * i:512 * i + width], aT[:, q * P:(q + 1) * P], ctxv[:, 512 * i:512 * i + width],
                                            start=True, stop=True)
                last.then_inc(scored, 1)

            def turn(b, q, first):
                n = 2 * b + q
                pe.wait_ge(aligned, n + 1)
                for i in range(TURNS):
                    if i >= 2 or not first:
                        pe.wait_ge(alT_ready[i % 2], 2 * n + i // 2)
                    for k, c in enumerate(range(4 * i, min(4 * i + 4, KC))):
                        rows = chunk_rows(c)
                        last = nc.tensor.transpose(t_ps[i % 2][0:rows, k * P:(k + 1) * P], masked[q][:, c * P:c * P + rows], m["ident"][:, :])
                    last.then_inc(turned, 1)

            def batch(b, first, last):
                if not last:
                    scores(b + 1, 0, False)
                for q in range(QT):
                    turn(b, q, first and q == 0)
                if not last:
                    scores(b + 1, 1, False)
                for taken in alT_ready:
                    pe.wait_ge(taken, TURNS * (b + 1))
                pe.wait_ge(values_ready, b + 1)
                if not first:
                    pe.wait_ge(x_added, b)
                for c in range(KC):
                    rows = chunk_rows(c)
                    final = nc.tensor.matmul(c_ps[:, 0:S], ctxg[0:rows, c, :], alT[0:rows, c, :], start=c == 0, stop=c == KC - 1)
                final.then_inc(c_ready, 1)
                pe.wait_ge(cT_ready, b + 1)
                nc.tensor.matmul(o_ps[:, 0:S], wc[:, 0, :], cT[:, :], start=True, stop=False)
                nc.tensor.matmul(o_ps[:, 0:S], wc[:, 1, :], queries(b), start=False, stop=True).then_inc(o_ready, 1)
                pe.wait_ge(hT_ready, b + 1)
                for q in range(QT):
                    final = nc.tensor.transpose(c_ps[:, q * P:(q + 1) * P], hT[:, q * P:(q + 1) * P], m["ident"][:, :])
                final.then_inc(o_turned, 1)
                if not (isinstance(b, int) and b >= B - 2):
                    product_a(b + 2)

            product_a(0)
            scores(0, 0, True)
            scores(0, 1, False)
            product_a(1)
            batch(0, True, False)
            with pe.Fori(1, B - 2) as b:
                batch(b, False, False)
            batch(B - 2, False, False)
            batch(B - 1, False, True)



def kernel(**inputs):
    import numpy as np
    import concourse.bacc as bacc
    from concourse.bass_utils import run_bass_kernel_spmd

    a = {name: np.asarray(value) for name, value in inputs.items()}
    arrays = {name: a[name] for name in ("x", "ctx_1024", "condB_tau", "fside_BxS2_0", "condB_pt", "_lenS2", "L2_xcond_W_a", "L3_ffn_norm_scale")}
    arrays["ctxT"] = a["ctx_1024"].transpose(0, 2, 1)
    for layer in (0, 1, 3):
        for w in ("Wq", "Wk", "Wv", "Wo"):
            arrays[f"L{layer}_{w}T"] = a[f"L{layer}_xcond_{w}"].T
        arrays[f"L{layer}_bq_rows"] = np.tile(a[f"L{layer}_xcond_bq"].reshape(G, ROWS).T, (3, 1))
        for v in ("bk", "bv", "bo"):
            arrays[f"L{layer}_xcond_{v}"] = a[f"L{layer}_xcond_{v}"]
    arrays["L0_w1T"], arrays["L0_w2T"] = a["L0_ffn_w1"].T, a["L0_ffn_w2"].T
    arrays["L2_WcT"] = a["L2_xcond_W_c"].T

    def by_chunk(w):
        e, h, d = w.shape
        return w.reshape(e, h // P, P, d).transpose(2, 0, 1, 3).reshape(P, e, h // P * d)

    arrays["L1_gateT"], arrays["L2_gateT"], arrays["L3_gateT"] = a["L1_ffn_gate_w"].T, a["L2_ffn_gate_w"].T, a["L3_ffn_w_router"].T
    arrays["L1_up"] = np.concatenate([a["L1_ffn_w1"], a["L1_ffn_w3"]], axis=1).transpose(2, 0, 1)
    arrays["L1_down"] = by_chunk(a["L1_ffn_w2"].transpose(0, 2, 1))
    arrays["L2_up"] = a["L2_ffn_gate_up_proj"].transpose(1, 0, 2)
    arrays["L2_down"] = by_chunk(a["L2_ffn_down_proj"])
    arrays["L3_up"] = a["L3_ffn_w_up"].transpose(2, 0, 1)
    arrays["L3_down"] = by_chunk(a["L3_ffn_w_down"].transpose(0, 2, 1))

    row = np.arange(P)
    arrays["ident"] = np.eye(P, dtype=np.float32)
    arrays["qmask"] = (row[:, None] % ROWS // DK == np.arange(J)).astype(np.float32)
    shift = np.zeros((P, J), np.float32)
    shift[96:96 + J] = -np.eye(J)
    shift[100:102] = 1.0
    arrays["shiftmask"] = shift
    rest = np.zeros((P, J), np.float32)
    rest[96:96 + J, 0] = 1.0
    rest[100:102, 1] = 1.0
    arrays["restmask"] = rest
    arrays["numbers"] = np.arange(L, dtype=np.float32)
    arrays["key_numbers"] = (np.arange(KC) * P + row[:, None]).astype(np.float32)
    select = np.zeros((E, E, P), np.float32)
    select[np.arange(E), np.arange(E)] = 1.0
    arrays["select"] = select
    arrays = {name: np.ascontiguousarray(v) for name, v in arrays.items()}

    nc = bacc.Bacc("TRN2", target_bir_lowering=False, num_devices=1)
    t = {name: nc.dram_tensor(f"in_{name}", v.shape, mybir.dt.from_np(v.dtype), kind="ExternalInput").ap() for name, v in arrays.items()}
    out = nc.dram_tensor("out_x", (B, S, D), F32, kind="ExternalOutput").ap()
    build(nc, t, out)
    r = run_bass_kernel_spmd(nc, [{f"in_{name}": v for name, v in arrays.items()}], core_ids=[0])
    return r.results[0]["out_x"]
```

```python
from contextlib import ExitStack

import concourse.bass as bass
from concourse import mybir
from concourse.alu_op_type import AluOpType as ALU

F32 = mybir.dt.float32
F32R = mybir.dt.float32r
BF16 = mybir.dt.bfloat16
U32 = mybir.dt.uint32
I32 = mybir.dt.int32
ACT = mybir.ActivationFunctionType
AX = mybir.AxisListType

B, S, D = 8, 256, 128
L = 1601
H, DK = 16, 8
P = 128
TILES = B * S // P
TOK = B * S
QT = S // P
KC = -(-L // P)
LAST = L - (KC - 1) * P
G, J = 4, 4
ROWS = J * DK
E = 8
BY_SCALAR = 10
LN_EPS, RMS_EPS, L2_EPS, Q_EPS = 1e-5, 1e-6, 1e-9, 1e-5
ROUND = 1.5 * 2.0 ** 23
EXPERT_TOK = 512

UNITS = KC * 2
LAG = 5
PROBS = 8
BANKS = 3
RUN = 2 * -(-L // 8)
RUNS = [i * (L - RUN) // 3 for i in range(4)]
GUARD_TILES = J * QT * len(RUNS)
assert G * UNITS % PROBS == 0 and UNITS % PROBS == 2
assert all(b - a <= RUN for a, b in zip(RUNS, RUNS[1:])) and RUNS[-1] + RUN == L
GUARD_START = -8
MAX_AT = 18
GUARD_AT = {}
for _k in range(GUARD_TILES):
    _at = GUARD_START + _k * UNITS // GUARD_TILES
    GUARD_AT.setdefault(_at % UNITS, []).append((1 if _at >= 0 else 2, _k))
assert GUARD_START + (GUARD_TILES - 1) * UNITS // GUARD_TILES < MAX_AT
EARLY = [k for tiles in GUARD_AT.values() for ahead, k in tiles if ahead == 2]


def guard_tiles(unit, g, last):
    return [(ahead, k) for ahead, k in GUARD_AT.get(unit, []) if not (last and g + ahead >= G)]


SIDE = {
    0: [(2, "Q"), (7, "T"), (10, "AT"), (13, "WO"), (21, "R")],
    1: [(2, "Q"), (7, "T"), (9, "K0"), (12, "K1"), (15, "K2"), (18, "K3"), (21, "R")],
    2: [(2, "Q"), (7, "T"), (9, "V0"), (12, "V1"), (15, "V2"), (18, "V3"), (21, "R")],
    3: [(2, "Q"), (7, "T"), (21, "R")],
}


def side_items(first, last):
    out, n = [], 0
    for g in range(G):
        here = {}
        for unit, item in SIDE[g]:
            if first and g == 0 and item in ("T", "AT", "WO"):
                continue
            if last and (item[0] in "KV" or (item == "Q" and g >= 2) or (item == "R" and g == 3)):
                continue
            here[unit] = (item, n)
            n += 1
        out.append(here)
    return out, n


SIDE_START = 4 + 4 + 2 + 1
N_FIRST, N_MID = side_items(True, False)[1], side_items(False, False)[1]
N_LAST = side_items(False, True)[1]
AFTER_V3 = len(SIDE[2]) - 1 - [item for _, item in SIDE[2]].index("V3") + len(SIDE[3])


def side_base(b, first, last):
    if first:
        return SIDE_START
    if last:
        return SIDE_START + N_FIRST + N_MID * (B - 2)
    return SIDE_START + N_FIRST - N_MID + b * N_MID


def freed(number, place, per_batch):
    if place >= BANKS:
        return number - BANKS + 1
    before = max(i for i in range(per_batch) if i % BANKS == place)
    return number - place - per_batch + before + 1


def chunk_rows(c):
    return LAST if c == KC - 1 else P


def build(nc, t, out):
    top = ExitStack()

    def sb(name, shape, dt=F32, ctx=top):
        return ctx.enter_context(nc.sbuf_tensor(name, shape, dt))

    def psum(name, shape, ctx):
        return ctx.enter_context(nc.psum_tensor(name, shape, F32))

    def sem(name, ctx=top):
        return ctx.enter_context(nc.semaphore(name))

    with top:
        m = {
            "x": sb("x_sb", [P, TOK]),
            "xnT": sb("xnT", [P, TOK]),
            "ident": sb("ident", [P, P]),
            "qmask": sb("qmask", [P, J]),
            "shiftmask": sb("shiftmask", [P, J]),
            "restmask": sb("restmask", [P, J]),
            "tau": sb("tau_all", [P, B]),
            "nm": sb("nm", [P, QT, 32]),
        }
        split = nc.dram_tensor("delta_split", (2, B, L), F32, kind="Internal").ap()
        setup(nc, t, m, split, sem, sb)
        for layer in (0, 1):
            norm(nc, t, m, f"L{layer}a", False)
            attention(nc, t, m, split, layer)
            if layer == 0:
                quantised_ffn(nc, t, m)
            else:
                norm(nc, t, m, "L1f", False)
                experts(nc, t, m, 1)
        norm(nc, t, m, "L2a", False)
        local_attention(nc, t, m)
        norm(nc, t, m, "L2f", False)
        experts(nc, t, m, 2)
        norm(nc, t, m, "L3a", False)
        attention(nc, t, m, split, 3)
        norm(nc, t, m, "L3f", True)
        experts(nc, t, m, 3)
        finish(nc, m, out, sem)


def setup(nc, t, m, split, sem, sb):
    with ExitStack() as ctx:
        loaded, stepped, stored = sems = sem("setup_loaded", ctx), sem("setup_stepped", ctx), sem("setup_stored", ctx)
        delta = sb("delta", [B, L], F32, ctx)
        high = sb("delta_high", [B, L], F32R, ctx)
        low = sb("delta_low", [B, L], F32R, ctx)
        ctx.callback(clear, nc, sems)
        block = ctx.enter_context(nc.Block())

        @block.sync
        def _(sp):
            sp.dma_start(delta[:, :], t["fside_BxS2_0"]).then_inc(loaded, 16)
            sp.dma_start(m["x"][:, :].rearrange("p (n d) -> p n d", d=D),
                         t["x"].rearrange("b (n p) d -> p (b n) d", p=P)).then_inc(loaded, 16)
            for name in ("ident", "qmask", "shiftmask", "restmask"):
                sp.dma_start(m[name][:, :], t[name]).then_inc(loaded, 16)
            sp.dma_start(m["tau"][:, :], t["condB_tau"][None, :].to_broadcast([P, B])).then_inc(loaded, 16)
            sp.wait_ge(stepped, 2)
            sp.dma_start(split[0], high[:, :].bitcast(F32)).then_inc(stored, 16)
            sp.dma_start(split[1], low[:, :].bitcast(F32)).then_inc(stored, 16)
            sp.wait_ge(stored, 32)
            sp.wait_ge(loaded, 7 * 16)

        @block.vector
        def _(dve):
            dve.wait_ge(loaded, 7 * 16)
            nc.vector.tensor_copy(high[:, :], delta[:, :]).then_inc(stepped, 1)
            dve.wait_ge(stepped, 1)
            nc.vector.tensor_tensor(low[:, :], delta[:, :], high[:, :].bitcast(F32), ALU.subtract).then_inc(stepped, 1)
            nc.vector.memset(m["nm"][:, :, :], 0.0).then_inc(stepped, 1)
            dve.wait_ge(stepped, 3)
            nc.vector.memset(m["nm"][:, :, J:J + 2], 1.0).then_inc(stepped, 1)


def clear(nc, sems):
    with nc.Block() as block:
        @block.sync
        def _(sp):
            for s in sems:
                sp.sem_clear(s)


def finish(nc, m, out, sem):
    stored = sem("out_stored")
    with nc.Block() as block:
        @block.sync
        def _(sp):
            sp.dma_start(out.rearrange("b (n p) d -> p (b n) d", p=P),
                         m["x"][:, :].rearrange("p (n d) -> p n d", d=D)).then_inc(stored, 16)
            sp.wait_ge(stored, 16)


def norm(nc, t, m, tag, rms, xn=None):
    with ExitStack() as ctx:
        def sb(name, shape, dt=F32):
            return ctx.enter_context(nc.sbuf_tensor(f"{tag}_{name}", shape, dt))

        sems = []

        def sem(name):
            sems.append(ctx.enter_context(nc.semaphore(f"{tag}_{name}")))
            return sems[-1]

        turn = xn is None
        xn = sb("xn", [P, TOK]) if turn else xn
        square = sb("square", [P, TOK])
        stat = sb("stat", [P, 8, TILES])
        total, minus_mean, squares, power, spread, rstd = (stat[:, i, :] for i in range(6))
        gain = sb("gain", [P, D])
        banks = [ctx.enter_context(nc.psum_tensor(f"{tag}_ps{i}", [P, 4 * P], F32)) for i in range(4)]
        stepped, squared, rooted, turned, taken, gain_in, first_normalised = (
            sem(n) for n in ("stepped", "squared", "rooted", "turned", "taken", "gain_in", "first_normalised"))
        x3 = m["x"][:, :].rearrange("p (n d) -> p n d", d=D)
        xn3 = xn[:, :].rearrange("p (n d) -> p n d", d=D)
        square3 = square[:, :].rearrange("p (n d) -> p n d", d=D)
        first, rest = slice(0, BY_SCALAR), slice(BY_SCALAR, TILES)
        steps = {}
        ctx.callback(clear, nc, sems)
        block = ctx.enter_context(nc.Block())

        def per_token(a, tiles):
            return a[:, tiles, None].to_broadcast([P, tiles.stop - tiles.start, D])

        if rms:
            @block.sync
            def _(sp):
                sp.dma_start(gain[:, :], t["L3_ffn_norm_scale"][None, :].to_broadcast([P, D])).then_inc(gain_in, 16)
                sp.wait_ge(gain_in, 16)

        @block.vector
        def _(dve):
            n = 0

            def done(instruction):
                nonlocal n
                n += 1
                instruction.then_inc(stepped, 1)
                dve.wait_ge(stepped, n)

            for part in (first, rest):
                done(nc.vector.tensor_reduce(total[:, part], x3[:, part, :], axis=AX.X, op=ALU.add))
                done(nc.vector.tensor_scalar(minus_mean[:, part], total[:, part], -1.0 / D, None, ALU.mult))
                steps.setdefault("mean", n)
            done(nc.vector.tensor_tensor(xn3[:, rest, :], x3[:, rest, :], per_token(minus_mean, rest), ALU.add))
            done(nc.vector.tensor_tensor(square3[:, rest, :], xn3[:, rest, :], xn3[:, rest, :], ALU.mult))
            done(nc.vector.tensor_reduce(squares[:, rest], square3[:, rest, :], axis=AX.X, op=ALU.add))
            dve.wait_ge(squared, 1)
            done(nc.vector.tensor_scalar(power, squares, 1.0 / D, LN_EPS, ALU.mult, ALU.add))
            steps["power"] = n
            dve.wait_ge(rooted, 1)
            done(nc.vector.reciprocal(rstd, spread))
            for i in range(BY_SCALAR):
                last = nc.vector.tensor_scalar(xn3[:, i, :], x3[:, i, :], minus_mean[:, i:i + 1], rstd[:, i:i + 1], ALU.add, ALU.mult)
                last.then_inc(first_normalised, 1)
            dve.wait_ge(first_normalised, BY_SCALAR)
            done(nc.vector.tensor_tensor(xn3[:, rest, :], xn3[:, rest, :], per_token(rstd, rest), ALU.mult))
            steps["normalised"] = n
            if rms:
                dve.wait_ge(squared, 2)
                done(nc.vector.tensor_reduce(total, square3, axis=AX.X, op=ALU.add))
                done(nc.vector.tensor_scalar(power, total, 1.0 / D, RMS_EPS, ALU.mult, ALU.add))
                steps["mean_square"] = n
                done(nc.vector.tensor_tensor(m["x"][:, :], m["x"][:, :], xn[:, :], ALU.add))
                dve.wait_ge(rooted, 2)
                nc.vector.reciprocal(rstd, spread).then_inc(taken, 1)
                dve.wait_ge(taken, 1)
                nc.vector.tensor_tensor(xn3, xn3, per_token(rstd, slice(0, TILES)), ALU.mult).then_inc(taken, 1)
                dve.wait_ge(taken, 2)
                dve.wait_ge(gain_in, 16)
                done(nc.vector.tensor_tensor(xn3, xn3, gain[:, None, :].to_broadcast([P, TILES, D]), ALU.mult))
                steps["scaled"] = n
            for i in (1, 3) if turn else ():
                dve.wait_ge(turned, i + 1)
                nc.vector.tensor_copy(m["xnT"][:, i * 512:(i + 1) * 512], banks[i][:, :])

        @block.scalar
        def _(act):
            act.wait_ge(stepped, steps["mean"])
            for i in range(BY_SCALAR):
                last = nc.scalar.activation(square3[:, i, :], x3[:, i, :], ACT.Square, bias=minus_mean[:, i:i + 1], accum_out=squares[:, i:i + 1])
            last.then_inc(squared, 1)
            act.wait_ge(stepped, steps["power"])
            nc.scalar.activation(spread, power, ACT.Sqrt).then_inc(rooted, 1)
            if rms:
                act.wait_ge(stepped, steps["normalised"])
                nc.scalar.activation(square[:, :], xn[:, :], ACT.Square).then_inc(squared, 1)
                act.wait_ge(stepped, steps["mean_square"])
                nc.scalar.activation(spread, power, ACT.Sqrt).then_inc(rooted, 1)
            for i in (0, 2) if turn else ():
                act.wait_ge(turned, i + 1)
                nc.scalar.activation(m["xnT"][:, i * 512:(i + 1) * 512], banks[i][:, :], ACT.Copy)

        @block.tensor
        def _(pe):
            if rms:
                pe.wait_ge(stepped, steps["scaled"])
            for i in range(4) if turn else ():
                for k in range(4):
                    tile = 4 * i + k
                    if not rms and tile < BY_SCALAR:
                        pe.wait_ge(first_normalised, tile + 1)
                    elif tile == BY_SCALAR:
                        pe.wait_ge(stepped, steps["normalised"])
                    last = nc.tensor.transpose(banks[i][:, k * P:(k + 1) * P], xn[:, tile * P:(tile + 1) * P], m["ident"][:, :])
                last.then_inc(turned, 1)


def attention(nc, t, m, split, layer):
    tag = f"L{layer}"
    with ExitStack() as ctx:
        def sb(name, shape, dt=F32):
            return ctx.enter_context(nc.sbuf_tensor(f"{tag}_{name}", shape, dt))

        sems = []

        def sem(name):
            sems.append(ctx.enter_context(nc.semaphore(f"{tag}_{name}")))
            return sems[-1]

        def psum(name, shape):
            return ctx.enter_context(nc.psum_tensor(f"{tag}_{name}", shape, F32))

        ident = m["ident"]
        wq = sb("wq", [P, G, 3, ROWS])
        wk, wv, wo = sb("wk", [P, D]), sb("wv", [P, D]), sb("wo", [P, D])
        bq = sb("bq", [3 * ROWS, G])
        taubq = sb("taubq", [3 * ROWS, G, B])
        bk = sb("bk", [P, 1])
        bv, bo = sb("bv", [P, D]), sb("bo", [P, D])
        ctxT = sb("ctxT", [P, L])
        kfull = sb("kfull", [P, L])
        khigh, klow = sb("khigh", [P, L], F32R), sb("klow", [P, L], F32R)
        kst = [sb(f"kst{g}", [P, L], F32R) for g in range(G)]
        qst = [sb(f"qst{g}", [P, J, S], F32R) for g in range(G)]
        tq = [sb(f"tq{i}", [3 * ROWS, S]) for i in range(2)]
        tqh = sb("tqh", [3 * ROWS, S], F32R)
        vc = sb("vc", [P, KC, D])
        vx = sb("vx", [P, H, KC, 32])
        probs = [sb(f"probs{i}", [P, 2 * S]) for i in range(PROBS)]
        partmax = sb("partmax", [P, QT, J, len(RUNS)])
        nm = m["nm"]
        osb = sb("osb", [P, S])
        rcp = sb("rcp", [P, QT, J])
        att, attb = sb("att", [P, QT, D]), sb("attb", [P, QT, D])
        attT = sb("attT", [P, S])
        wotmp = sb("wotmp", [P, S])

        guard_ps = [psum(f"guard{i}", [P, 512]) for i in range(BANKS)]
        score_ps = [psum(f"score{i}", [P, 512]) for i in range(BANKS)]
        o_ps = psum("o_ps", [P, 512])
        side = psum("side", [P, 512])

        w_in = sem("w_in")
        ctx_in = sem("ctx_in")
        kst_in = [sem(f"kst_in{g}") for g in range(G)]
        side_ready, side_taken = sem("side_ready"), sem("side_taken")
        guard_scored, guard_reduced = sem("guard_scored"), sem("guard_reduced")
        scores_ready, exp_done, pv_done = sem("scores_ready"), sem("exp_done"), sem("pv_done")
        o_taken = sem("o_taken")
        max_ready, shift_ready = sem("max_ready"), sem("shift_ready")
        kfull_ready, khigh_ready, klow_ready = sem("kfull_ready"), sem("khigh_ready"), sem("klow_ready")
        tq_ready, tq_high, tq_split = sem("tq_ready"), sem("tq_high"), sem("tq_split")
        qst_ready = sem("qst_ready")
        rcp_ready, att_done, attb_ready, attT_ready = sem("rcp_ready"), sem("att_done"), sem("attb_ready"), sem("attT_ready")
        wo_taken, x_added = sem("wo_taken"), sem("x_added")
        vx_ready, vx_cleared, spread_turn, split_turn = (
            sem("vx_ready"), sem("vx_cleared"), sem("spread_turn"), sem("split_turn"))
        taubq_ready, kst_cleared = sem("taubq_ready"), sem("kst_cleared")
        ctx.callback(clear, nc, sems)
        block = ctx.enter_context(nc.Block())

        LOADS = 1 + 3 + 1 + 1 + 2

        PROLOGUE = [("K0", guard_ps[0], 0), ("K1", guard_ps[1], 0), ("K2", guard_ps[2], 0), ("K3", score_ps[0], 0),
                    ("Q", side, 0), ("Q", o_ps, 0),
                    ("V0", score_ps[1], 0), ("V1", score_ps[2], 0), ("V2", score_ps[0], 4), ("V3", score_ps[1], 7)]
        R_FIRST = len(PROLOGUE)

        def prologue_step(name, n):
            return (0, n - 6) if name == "Q" else (-1, 1)

        def step(b, g):
            return b * G + g

        def keys(c):
            return slice(c * P, c * P + chunk_rows(c))

        @block.sync
        def _(sp):
            def load_context(b):
                sp.dma_start(ctxT[:, :], t["ctxT"][bass.ds(b, 1), :, :].rearrange("o p l -> (o p) l")).then_inc(ctx_in, 16)

            def fill_stack(b, g):
                rows = slice(g * ROWS, (g + 1) * ROWS)
                for r, part in enumerate((khigh, klow, khigh)):
                    sp.dma_start(kst[g][r * ROWS:(r + 1) * ROWS, :].bitcast(F32), part[rows, :].bitcast(F32)).then_inc(kst_in[g], 16)
                sp.dma_start(kst[g][100:102, :].bitcast(F32), split[:, bass.ds(b, 1), :].rearrange("a o l -> (a o) l")).then_inc(kst_in[g], 16)

            sp.dma_start(wk[:, :], t[f"{tag}_WkT"]).then_inc(w_in, 16)
            sp.dma_start(bk[:, :], t[f"{tag}_xcond_bk"][:, None]).then_inc(w_in, 16)
            load_context(0)
            sp.dma_start(wq[:, :, :, :], t[f"{tag}_Wq_groups"]).then_inc(w_in, 16)
            sp.dma_start(bq[:, :], t[f"{tag}_bq_rows"]).then_inc(w_in, 16)
            for name, where in (("Wv", wv), ("Wo", wo)):
                sp.dma_start(where[:, :], t[f"{tag}_{name}T"]).then_inc(w_in, 16)
            sp.dma_start(bv[:, :], t[f"{tag}_xcond_bv"][None, :].to_broadcast([P, D])).then_inc(w_in, 16)
            sp.dma_start(bo[:, :], t[f"{tag}_xcond_bo"][None, :].to_broadcast([P, D])).then_inc(w_in, 16)
            sp.wait_ge(klow_ready, 1)
            sp.wait_ge(kst_cleared, G)
            for g in range(G):
                fill_stack(0, g)

            def batch(b, first, last):
                if not first:
                    sp.wait_ge(scores_ready, step(b, 0) * UNITS)
                    fill_stack(b, 3)
                if last:
                    return
                sp.wait_ge(side_ready, len(PROLOGUE) if first else side_base(b, first, last) - AFTER_V3)
                load_context(b + 1)
                sp.wait_ge(klow_ready, b + 2)
                sp.wait_ge(scores_ready, step(b, 1) * UNITS)
                fill_stack(b + 1, 0)
                for g in (1, 2):
                    sp.wait_ge(scores_ready, step(b, g + 1) * UNITS)
                    fill_stack(b + 1, g)

            batch(0, True, False)
            with sp.Fori(1, B - 1) as b:
                batch(b, False, False)
            batch(B - 1, False, True)
            sp.wait_ge(w_in, LOADS * 16)

        @block.tensor
        def _(pe):
            def wait_side(n):
                pe.wait_ge(side_taken, n)

            def item(name, b, g, n, side=side, before=None):
                if before is None:
                    wait_side(n)
                elif before:
                    pe.wait_ge(side_taken, before)
                if name[0] == "K":
                    c = int(name[1])
                    if c == 0:
                        pe.wait_ge(ctx_in, 16 * b + 32)
                    width = min(512, L - 512 * c)
                    last = nc.tensor.matmul(side[:, 0:width], wk[:, :], ctxT[:, 512 * c:512 * c + width], start=True, stop=True)
                elif name[0] == "V":
                    v = int(name[1])
                    for i, c in enumerate(range(4 * v, min(4 * v + 4, KC))):
                        last = nc.tensor.matmul(side[0:chunk_rows(c), i * P:(i + 1) * P], ctxT[:, keys(c)], wv[:, :], start=True, stop=True)
                elif name == "Q":
                    g2, b2 = (g + 2) % G, b + (g + 2) // G
                    last = nc.tensor.matmul(side[0:3 * ROWS, 0:S], wq[:, g2, :, :].rearrange("p r c -> p (r c)"),
                                            m["xnT"][:, bass.ds(b2 * S, S)], start=True, stop=True)
                elif name == "R":
                    pe.wait_ge(max_ready, step(b, g) + 2)
                    for q in range(QT):
                        last = nc.tensor.matmul(side[96:128, q * P:(q + 1) * P], nm[:, q, :], ident[:, :], start=True, stop=True)
                elif name == "T":
                    pe.wait_ge(o_taken, step(b, g))
                    for q in range(QT):
                        last = nc.tensor.transpose(side[:, q * P:(q + 1) * P], osb[:, q * P:(q + 1) * P], ident[:, :])
                elif name == "AT":
                    pe.wait_ge(attb_ready, b)
                    for q in range(QT):
                        last = nc.tensor.transpose(side[:, q * P:(q + 1) * P], attb[:, q, :], ident[:, :])
                elif name == "WO":
                    pe.wait_ge(attT_ready, b)
                    for q in range(QT):
                        last = nc.tensor.matmul(side[:, q * P:(q + 1) * P], attT[:, q * P:(q + 1) * P], wo[:, :], start=True, stop=True)
                last.then_inc(side_ready, 1)

            def guard(s, g, k):
                j, q, run = k // (len(RUNS) * QT), k // len(RUNS) % QT, k % len(RUNS)
                place = g * GUARD_TILES + k
                if not (isinstance(s, int) and s == 0 and place < BANKS):
                    pe.wait_ge(guard_reduced, freed(s * GUARD_TILES + k, place, G * GUARD_TILES))
                nc.tensor.matmul(guard_ps[place % BANKS][:, 0:RUN], qst[g][:, j, q * P:(q + 1) * P],
                                 kst[g][:, RUNS[run]:RUNS[run] + RUN], start=True, stop=True).then_inc(guard_scored, 1)

            def values(s, g, c):
                pe.wait_ge(exp_done, s * UNITS + 2 * c + 2)
                n = chunk_rows(c)
                for j in range(J):
                    last = nc.tensor.matmul(o_ps[32 * j:32 * j + 32, 0:S], vx[0:n, g * J + j, c, :],
                                            probs[(2 * g + 2 * c + j // 2) % PROBS][0:n, j % 2 * S:(j % 2 + 1) * S],
                                            start=c == 0, stop=c == KC - 1)
                last.then_inc(pv_done, 2)

            pe.wait_ge(w_in, LOADS * 16)
            for n, (name, bank, before) in enumerate(PROLOGUE):
                item(name, *prologue_step(name, n), n, bank, before)
            pe.wait_ge(kst_in[0], 64)
            pe.wait_ge(qst_ready, 2)
            for k in range(GUARD_TILES):
                guard(0, 0, k)
            item("R", 0, -1, R_FIRST)
            pe.wait_ge(kst_in[1], 64)
            pe.wait_ge(qst_ready, 4)
            for k in sorted(EARLY):
                guard(1, 1, k)

            def batch(b, first, last):
                items, _ = side_items(first, last)
                base = side_base(b, first, last)
                for g in range(G):
                    s = step(b, g)
                    for u in range(UNITS):
                        if u in items[g]:
                            name, n = items[g][u]
                            item(name, b, g, base + n)
                        for ahead, k in guard_tiles(u, g, last):
                            g1, b1 = (g + ahead) % G, b + (g + ahead) // G
                            if k == 0:
                                pe.wait_ge(kst_in[g1], 64 * b1 + 64)
                                pe.wait_ge(qst_ready, 2 * (s + ahead) + 2)
                            guard(s + ahead, g1, k)
                        if u == 0:
                            pe.wait_ge(shift_ready, 2 * s + 2)
                        place = g * UNITS + u
                        if not (first and place < BANKS):
                            pe.wait_ge(exp_done, freed(s * UNITS + u, place, G * UNITS))
                        c, pair = u // 2, u % 2
                        nc.tensor.matmul(score_ps[place % BANKS][0:chunk_rows(c), :], kst[g][:, keys(c)],
                                         qst[g][:, 2 * pair:2 * pair + 2, :].rearrange("p j q -> p (j q)"),
                                         start=True, stop=True).then_inc(scores_ready, 1)
                        if u > LAG and u % 2:
                            if u == LAG + 2:
                                pe.wait_ge(vx_ready, s + 1)
                                if not (first and g == 0):
                                    pe.wait_ge(o_taken, s)
                                values(s, g, 0)
                            values(s, g, (u - LAG) // 2)
                        elif u in (1, 3) and not (first and g == 0):
                            values(s - 1, (g - 1) % G, KC - (LAG - u) // 2)

            batch(0, True, False)
            with pe.Fori(1, B - 1) as b:
                batch(b, False, False)
            batch(B - 1, False, True)
            for c in (KC - 2, KC - 1):
                values(B * G - 1, G - 1, c)
            n = SIDE_START + N_FIRST + N_MID * (B - 2) + N_LAST
            for i, name in enumerate(("T", "AT", "WO")):
                item(name, B, 0, n + i)

        @block.scalar
        def _(act):
            def shift(b, g, half):
                for j in range(J // 2 * half, J // 2 * (half + 1)):
                    last = nc.scalar.activation(qst[(g + 1) % G][96:128, j, :], side[96:128, 0:S], ACT.Identity, scale=m["shiftmask"][96:128, j:j + 1])
                last.then_inc(shift_ready, 1)

            def item(name, b, g, n, side=side):
                if name == "R":
                    act.wait_ge(side_ready, n + 1)
                    shift(b, g, 0)
                elif name == "R2":
                    shift(b, g, 1)
                    act.wait_ge(shift_ready, 2 * step(b, g) + 4)
                    nc.scalar.sem_inc(side_taken, 1)
                if name[0] in "KVQ" or name == "AT":
                    act.wait_ge(side_ready, n + 1)
                if name[0] == "K":
                    c = int(name[1])
                    width = min(512, L - 512 * c)
                    if c == 0 and not (isinstance(b, int) and b == -1):
                        act.wait_ge(klow_ready, b + 1)
                    nc.scalar.activation(kfull[:, 512 * c:512 * c + width], side[:, 0:width], ACT.Identity,
                                         bias=bk[:, 0:1]).then_inc(kfull_ready, 1)
                    act.wait_ge(kfull_ready, 4 * b + 4 + c + 1)
                    nc.scalar.sem_inc(side_taken, 1)
                elif name[0] == "V":
                    v = int(name[1])
                    if v == 0:
                        act.wait_ge(vx_cleared, 2) if isinstance(b, int) and b == -1 else act.wait_ge(vx_ready, b * G + G)
                    if v < 3:
                        copied = nc.scalar.activation(vc[:, 4 * v:4 * v + 4, :].rearrange("p c d -> p (c d)"), side[:, :], ACT.Copy)
                    else:
                        copied = nc.scalar.activation(vc[0:LAST, KC - 1, :], side[0:LAST, 0:D], ACT.Copy)
                    copied.then_inc(side_taken, 1)
                elif name == "Q":
                    g2, b2 = (g + 2) % G, b + (g + 2) // G
                    s2 = step(b, g) + 2
                    if not (isinstance(s2, int) and s2 < 2):
                        act.wait_ge(qst_ready, 2 * (s2 - 1))
                    nc.scalar.activation(tq[g2 % 2][:, :], side[0:3 * ROWS, 0:S], ACT.Identity,
                                         scale=m["tau"][0:3 * ROWS, bass.ds(b2, 1)],
                                         bias=taubq[:, g2, bass.ds(b2, 1)]).then_inc(tq_ready, 1)
                    act.wait_ge(tq_ready, s2 + 1)
                    nc.scalar.sem_inc(side_taken, 1)
                elif name == "AT":
                    if not (isinstance(b, int) and b == 1):
                        act.wait_ge(wo_taken, b - 1)
                    nc.scalar.activation(attT[:, :], side[:, 0:S], ACT.Copy).then_inc(attT_ready, 1)
                    act.wait_ge(attT_ready, b)
                    nc.scalar.sem_inc(side_taken, 1)

            def take_output(s):
                act.wait_ge(pv_done, s * UNITS + UNITS)
                if not (isinstance(s, int) and s == 0):
                    act.wait_ge(att_done, s)
                nc.scalar.activation(osb[:, :], o_ps[:, 0:S], ACT.Copy).then_inc(o_taken, 1)

            act.wait_ge(w_in, LOADS * 16)
            act.wait_ge(taubq_ready, 1)
            for n, (name, bank, _) in enumerate(PROLOGUE):
                item(name, *prologue_step(name, n), n, bank)
            for name in ("R", "R2"):
                item(name, 0, -1, R_FIRST)

            def batch(b, first, last):
                items, _ = side_items(first, last)
                base = side_base(b, first, last)
                for g in range(G):
                    s = step(b, g)
                    for u in range(UNITS):
                        c = u // 2
                        act.wait_ge(scores_ready, s * UNITS + u + 1)
                        if not (first and g == 0 and u < PROBS):
                            act.wait_ge(pv_done, s * UNITS + u - PROBS + 1 + (u % 2 == 0))
                        n = chunk_rows(c)
                        nc.scalar.activation(probs[(2 * g + u) % PROBS][0:n, :], score_ps[(g * UNITS + u) % BANKS][0:n, :], ACT.Exp,
                                             scale=float(DK) ** -0.5).then_inc(exp_done, 1)
                        if u == LAG - 2 and not (first and g == 0):
                            take_output(s - 1)
                        if items[g].get(u - 1, (None,))[0] == "R":
                            item("R2", b, g, 0)
                        if u in items[g]:
                            name, n = items[g][u]
                            item(name, b, g, base + n)

            batch(0, True, False)
            with act.Fori(1, B - 1) as b:
                batch(b, False, False)
            batch(B - 1, False, True)
            take_output(B * G - 1)
            item("AT", B, 0, SIDE_START + N_FIRST + N_MID * (B - 2) + N_LAST + 1)

        @block.vector
        def _(dve):
            def item(name, b, g, n):
                if name == "T":
                    g0 = (g - 1) % G
                    s0 = step(b, g) - 1
                    dve.wait_ge(side_ready, n + 1)
                    turned = side[:, 0:S].rearrange("p (q j r) -> p q j r", q=QT, r=32)
                    nc.vector.reciprocal(rcp[:, :, :], turned[:, :, :, DK]).then_inc(rcp_ready, 1)
                    dve.wait_ge(rcp_ready, s0 + 1)
                    if g0 == 0 and not (isinstance(b, int) and b == 0):
                        dve.wait_ge(attb_ready, b)
                    for q in range(QT):
                        last = nc.vector.tensor_tensor(att[:, q, g0 * ROWS:(g0 + 1) * ROWS].rearrange("p (j e) -> p j e", e=DK),
                                                       turned[:, q, :, 0:DK], rcp[:, q, :, None].to_broadcast([P, J, DK]), ALU.mult)
                    last.then_inc(att_done, 1)
                    dve.wait_ge(att_done, s0 + 1)
                    nc.vector.sem_inc(side_taken, 1)
                    if g0 == G - 1:
                        nc.vector.tensor_tensor(attb[:, :, :], att[:, :, :], bv[:, None, :].to_broadcast([P, QT, D]), ALU.add)\
                            .then_inc(attb_ready, 1)
                elif name == "WO":
                    dve.wait_ge(side_ready, n + 1)
                    nc.vector.tensor_tensor(wotmp[:, :].rearrange("p (q d) -> p q d", q=QT), side[:, 0:S].rearrange("p (q d) -> p q d", q=QT),
                                            bo[:, None, :].to_broadcast([P, QT, D]), ALU.add).then_inc(wo_taken, 1)
                    dve.wait_ge(wo_taken, b)
                    nc.vector.sem_inc(side_taken, 1)
                    xs = m["x"][:, bass.ds((b - 1) * S, S)]
                    nc.vector.tensor_tensor(xs, xs, wotmp[:, :], ALU.add).then_inc(x_added, 1)
                    dve.wait_ge(x_added, b)

            def reduce(s, g, k):
                j, q, run = k // (len(RUNS) * QT), k // len(RUNS) % QT, k % len(RUNS)
                if k == 0 and not (isinstance(s, int) and s == 0):
                    dve.wait_ge(max_ready, s)
                dve.wait_ge(guard_scored, s * GUARD_TILES + k + 1)
                nc.vector.tensor_reduce(partmax[:, q, j, run:run + 1], guard_ps[(g * GUARD_TILES + k) % BANKS][:, 0:RUN], axis=AX.X, op=ALU.max)\
                    .then_inc(guard_reduced, 1)

            def join(s):
                dve.wait_ge(guard_reduced, s * GUARD_TILES + GUARD_TILES)
                nc.vector.tensor_reduce(nm[:, :, 0:J], partmax[:, :, :, :], axis=AX.X, op=ALU.max).then_inc(max_ready, 1)

            for g in range(G):
                nc.vector.tensor_copy(kst[g][96:128, :], m["restmask"][96:128, 0:1].to_broadcast([32, L])).then_inc(kst_cleared, 1)
            dve.wait_ge(w_in, LOADS * 16)
            for g in range(G):
                last = nc.vector.tensor_scalar(taubq[:, g, :], m["tau"][0:3 * ROWS, :], bq[:, g:g + 1], None, ALU.mult)
            last.then_inc(taubq_ready, 1)
            dve.wait_ge(kfull_ready, 4)
            nc.vector.tensor_copy(khigh[:, :], kfull[:, :]).then_inc(khigh_ready, 1)
            dve.wait_ge(khigh_ready, 1)
            nc.vector.tensor_tensor(klow[:, :], kfull[:, :], khigh[:, :].bitcast(F32), ALU.subtract).then_inc(klow_ready, 1)
            low = slice(2 * ROWS, 3 * ROWS)
            nc.vector.tensor_tensor(qst[0][96:128, :, :], m["ident"][96:128, None, 0:1].to_broadcast([32, J, S]),
                                    m["restmask"][96:128, 1:2, None].to_broadcast([32, J, S]), ALU.add).then_inc(qst_ready, 1)
            dve.wait_ge(tq_ready, 1)
            nc.vector.tensor_copy(tqh[low, :], tq[0][low, :]).then_inc(tq_high, 1)
            dve.wait_ge(tq_high, 1)
            nc.vector.tensor_tensor(tq[0][low, :], tq[0][low, :], tqh[low, :].bitcast(F32), ALU.subtract).then_inc(tq_split, 1)
            dve.wait_ge(tq_split, 1)
            nc.vector.tensor_tensor(qst[0][0:3 * ROWS, :, :], tq[0][:, None, :].to_broadcast([3 * ROWS, J, S]),
                                    m["qmask"][0:3 * ROWS, :, None].to_broadcast([3 * ROWS, J, S]), ALU.mult).then_inc(qst_ready, 1)
            for k in range(GUARD_TILES):
                reduce(0, 0, k)
            join(0)
            for k in sorted(EARLY):
                reduce(1, 1, k)

            def batch(b, first, last):
                items, _ = side_items(first, last)
                base = side_base(b, first, last)
                for g in range(G):
                    s = step(b, g)
                    for u in range(UNITS):
                        if u == MAX_AT and not (last and g == G - 1):
                            join(s + 1)
                        for ahead, k in guard_tiles(u, g, last):
                            reduce(s + ahead, (g + ahead) % G, k)
                        if u in items[g]:
                            name, n = items[g][u]
                            item(name, b, g, base + n)

            batch(0, True, False)
            with dve.Fori(1, B - 1) as b:
                batch(b, False, False)
            batch(B - 1, False, True)
            n = SIDE_START + N_FIRST + N_MID * (B - 2) + N_LAST
            item("T", B, 0, n)
            item("WO", B, 0, n + 2)

        @block.gpsimd
        def _(pool):
            def spread(b, g, stacks):
                pool.wait_ge(qst_ready, 2 * stacks)
                if not (isinstance(b, int) and b == 0 and g == 0):
                    pool.wait_ge(vx_ready, step(b, g))
                nc.gpsimd.sem_inc(spread_turn, 1)
                nc.gpsimd.tensor_copy(vx[:, g * J:(g + 1) * J, :, 0:DK],
                                      vc[:, :, g * ROWS:(g + 1) * ROWS].rearrange("p c (j e) -> p j c e", e=DK)).then_inc(vx_ready, 1)

            def stack(b, g):
                g2, s2 = (g + 2) % G, step(b, g) + 2
                x, low = tq[g2 % 2], slice(2 * ROWS, 3 * ROWS)
                pool.wait_ge(tq_ready, s2 + 1)
                if not (isinstance(s2, int) and s2 < G):
                    pool.wait_ge(scores_ready, (s2 - 3) * UNITS)
                if not (isinstance(s2, int) and s2 == 0):
                    pool.wait_ge(qst_ready, 2 * s2)
                if g >= 0:
                    pool.wait_ge(vx_ready, G * b + G)
                    pool.wait_ge(klow_ready, b + 1 + (g >= 2))
                nc.gpsimd.sem_inc(split_turn, 1)
                nc.gpsimd.tensor_copy(tqh[low, :], x[low, :]).then_inc(tq_high, 1)
                pool.wait_ge(tq_high, s2 + 1)
                nc.gpsimd.tensor_tensor(x[low, :], x[low, :], tqh[low, :].bitcast(F32), ALU.subtract).then_inc(tq_split, 1)
                pool.wait_ge(tq_split, s2 + 1)
                nc.gpsimd.tensor_tensor(qst[g2][96:128, :, :], m["ident"][96:128, None, 0:1].to_broadcast([32, J, S]),
                                        m["restmask"][96:128, 1:2, None].to_broadcast([32, J, S]), ALU.add).then_inc(qst_ready, 1)
                pool.wait_ge(qst_ready, 2 * s2 + 1)
                nc.gpsimd.tensor_tensor(qst[g2][0:3 * ROWS, :, :], tq[g2 % 2][:, None, :].to_broadcast([3 * ROWS, J, S]),
                                        m["qmask"][0:3 * ROWS, :, None].to_broadcast([3 * ROWS, J, S]), ALU.mult).then_inc(qst_ready, 1)

            def split_keys(b, stacks):
                pool.wait_ge(kfull_ready, 4 * b + 8)
                for filled in kst_in:
                    pool.wait_ge(filled, 64 * b + 64)
                pool.wait_ge(qst_ready, 2 * stacks)
                nc.gpsimd.sem_inc(split_turn, 1)
                nc.gpsimd.tensor_copy(khigh[:, :], kfull[:, :]).then_inc(khigh_ready, 1)
                pool.wait_ge(khigh_ready, b + 2)
                nc.gpsimd.tensor_tensor(klow[:, :], kfull[:, :], khigh[:, :].bitcast(F32), ALU.subtract).then_inc(klow_ready, 1)

            nc.gpsimd.memset(vx[:, :, :, :], 1.0).then_inc(vx_cleared, 1)
            pool.wait_ge(vx_cleared, 1)
            nc.gpsimd.memset(vc[:, :, :], 0.0).then_inc(vx_cleared, 1)
            pool.wait_ge(vx_cleared, 2)
            stack(0, -1)
            pool.wait_ge(side_taken, len(PROLOGUE))
            for g in range(G):
                spread(0, g, 2)

            def batch(b, first, last):
                items, _ = side_items(first, last)
                base = side_base(b, first, last)
                for g in range(G):
                    if g == 0 and not first:
                        pool.wait_ge(pv_done, step(b, 0) * UNITS)
                        spread(b, 3, G * b + 2)
                    if not (last and g >= 2):
                        stack(b, g)
                    if g == 1 and not last:
                        split_keys(b, G * b + 4)
                    if g == 3 and not last:
                        n = [n for here in items for name, n in here.values() if name == "V3"][0]
                        pool.wait_ge(side_taken, base + n + 1)
                        for i in range(3):
                            pool.wait_ge(pv_done, step(b, i + 1) * UNITS)
                            spread(b + 1, i, G * b + 6)

            batch(0, True, False)
            with pool.Fori(1, B - 1) as b:
                batch(b, False, False)
            batch(B - 1, False, True)


def quantised_ffn(nc, t, m):
    QUAD, TURN_LAG, ADD_LAG = 4, 2, 3
    HID, HC = 512, 4
    N_W = HID * D
    outer = ExitStack()
    with outer:
        xn = outer.enter_context(nc.sbuf_tensor("q_xn", [P, TOK], F32))
        norm(nc, t, m, "L0f", False, xn)
        ctx = outer

        def sb(name, shape, dt=F32):
            return ctx.enter_context(nc.sbuf_tensor(f"q_{name}", shape, dt))

        sems = []

        def sem(name):
            sems.append(ctx.enter_context(nc.semaphore(f"q_{name}")))
            return sems[-1]

        def psum(name, shape, dt=F32):
            return ctx.enter_context(nc.psum_tensor(f"q_{name}", shape, dt))

        w = sb("w", [P, 2, HID])
        scratch = sb("scratch", [P, TOK])
        wq = sb("wq", [P, 2, HID], BF16)
        identb = sb("identb", [P, P], BF16)
        ones = sb("ones", [P, P])
        wsum, ws, wr = sb("wsum", [P, 2]), sb("ws", [P, 2]), sb("wr", [P, 2])
        amax, xr, xs = sb("amax", [P, TILES]), sb("xr", [P, TILES]), sb("xs", [P, TILES])
        hscale = sb("hscale", [P, TILES])
        xq, xqT = sb("xq", [P, TOK], BF16), sb("xqT", [P, TOK], BF16)
        h = [sb(f"h{i}", [P, HID]) for i in range(2)]
        hr = [sb(f"hr{i}", [P, HID]) for i in range(2)]
        hq = [sb(f"hq{i}", [P, HID], BF16) for i in range(2)]
        hqT = [sb(f"hqT{i}", [P, HID], BF16) for i in range(2)]
        hmax = [sb(f"hmax{i}", [P, 4]) for i in range(QUAD)]
        xT_ps = psum("xT_ps", [P, TOK], BF16)
        h_ps = [psum(f"h_ps{i}", [P, HID]) for i in range(2)]
        t_ps = [psum(f"t_ps{i}", [P, 1024], BF16) for i in range(2)]
        y_ps = [psum(f"y_ps{i}", [P, 512]) for i in range(2)]
        w_in, stepped, summed, totals, absolute, turned_x, xqT_ready = (
            sem(n) for n in ("w_in", "stepped", "summed", "totals", "absolute", "turned_x", "xqT_ready"))
        clip_turn = sem("clip_turn")
        h_ready, gelu_done, hstep, clipped, hq_ready, turned, hqT_ready, y_ready, x_added = (
            sem(n) for n in ("h_ready", "gelu_done", "hstep", "clipped", "hq_ready", "turned", "hqT_ready", "y_ready", "x_added"))
        FINAL_STEP = 14
        HSTEPS = 4
        xn3 = xn[:, :].rearrange("p (n d) -> p n d", d=D)
        sc3 = scratch[:, :].rearrange("p (n d) -> p n d", d=D)
        ctx.callback(clear, nc, sems)
        block = ctx.enter_context(nc.Block())

        def tiles(engine, stages):
            def quad(r, start, stop):
                for i in range(start, stop):
                    for lag, stage in stages:
                        n = r * QUAD + i - lag
                        if not isinstance(n, int) or 0 <= n < TILES:
                            stage(n, (i - lag) % QUAD)

            for r in (0, 1):
                quad(r, 0, QUAD)
            with engine.Fori(2, TILES // QUAD) as r:
                quad(r, 0, QUAD)
            quad(TILES // QUAD, 0, ADD_LAG)

        def later(n, tiles):
            return not (isinstance(n, int) and n < tiles)

        @block.sync
        def _(sp):
            sp.dma_start(w[:, 0, :], t["L0_w1T"]).then_inc(w_in, 16)
            sp.dma_start(w[:, 1, :].rearrange("p (c d) -> p c d", c=HC), t["L0_w2T"].rearrange("(c p) d -> p c d", p=P)).then_inc(w_in, 16)
            sp.wait_ge(w_in, 32)

        @block.scalar
        def _(act):
            nc.scalar.activation(scratch[:, :], xn[:, :], ACT.Abs).then_inc(absolute, 1)
            act.wait_ge(w_in, 32)
            for i in range(2):
                nc.scalar.activation(h[i][:, :], w[:, i, :], ACT.Abs, accum_out=wsum[:, i:i + 1]).then_inc(summed, 1)
            act.wait_ge(turned_x, 1)
            nc.scalar.activation(xqT[:, :], xT_ps[:, :], ACT.Copy).then_inc(xqT_ready, 1)
            act.wait_ge(stepped, FINAL_STEP)

            def gelu(n, i):
                act.wait_ge(h_ready, n + 1)
                if later(n, 2):
                    act.wait_ge(hstep, HSTEPS * (n - 1))
                nc.scalar.activation(h[i % 2][:, :], h_ps[i % 2][:, :], ACT.Gelu, scale=hscale[:, bass.ds(n, 1)]).then_inc(gelu_done, 1)

            def take_turned(n, i):
                act.wait_ge(turned, n + 1)
                nc.scalar.activation(hqT[i % 2][:, :], t_ps[i % 2][:, 0:HID], ACT.Copy).then_inc(hqT_ready, 1)

            tiles(act, ((0, gelu), (TURN_LAG, take_turned)))

        @block.vector
        def _(dve):
            k = 0

            def done(instruction):
                nonlocal k
                k += 1
                instruction.then_inc(stepped, 1)
                dve.wait_ge(stepped, k)

            done(nc.vector.memset(ones[:, :], 1.0))
            done(nc.vector.tensor_copy(identb[:, :], m["ident"][:, :]))
            dve.wait_ge(absolute, 1)
            done(nc.vector.tensor_reduce(amax[:, :], sc3, axis=AX.X, op=ALU.max))
            done(nc.vector.tensor_scalar(amax[:, :], amax[:, :], Q_EPS, None, ALU.max))
            done(nc.vector.reciprocal(xr[:, :], amax[:, :]))
            done(nc.vector.tensor_scalar(xs[:, :], xr[:, :], 127.0, None, ALU.mult))
            done(nc.vector.tensor_tensor(sc3, xn3, xs[:, :, None].to_broadcast([P, TILES, D]), ALU.mult))
            done(nc.vector.tensor_scalar(scratch[:, :], scratch[:, :], ROUND, ROUND, ALU.add, ALU.subtract))
            done(nc.vector.tensor_scalar(xq[:, :], scratch[:, :], 127.0, -128.0, ALU.min, ALU.max))
            dve.wait_ge(totals, 1)
            done(nc.vector.tensor_scalar(ws[:, :], y_ps[0][:, 0:2], 1.0 / N_W, Q_EPS, ALU.mult, ALU.max))
            done(nc.vector.reciprocal(wr[:, :], ws[:, :]))
            for i in range(2):
                nc.vector.tensor_scalar(w[:, i, :], w[:, i, :], wr[:, i:i + 1], ROUND, ALU.mult, ALU.add).then_inc(totals, 1)
                dve.wait_ge(totals, 2 + 2 * i)
                nc.vector.tensor_scalar(w[:, i, :], w[:, i, :], ROUND, -1.0, ALU.subtract, ALU.max).then_inc(totals, 1)
                dve.wait_ge(totals, 3 + 2 * i)
                last = nc.vector.tensor_scalar(wq[:, i, :], w[:, i, :], 1.0, None, ALU.min)
            done(last)
            done(nc.vector.tensor_scalar(hscale[:, :], amax[:, :], ws[:, 0:1], 1.0 / 127.0, ALU.mult, ALU.mult))
            done(nc.vector.tensor_scalar(ws[:, :], ws[:, :], 1.0 / 127.0, None, ALU.mult))
            assert k == FINAL_STEP

            def quantise(n, i):
                q = hmax[i]
                dve.wait_ge(gelu_done, n + 1)
                nc.vector.tensor_reduce(q[:, 0:1], h[i % 2][:, :], axis=AX.X, op=ALU.max, apply_absolute_value=True).then_inc(hstep, 1)
                dve.wait_ge(hstep, HSTEPS * n + 1)
                nc.vector.tensor_scalar(q[:, 1:2], q[:, 0:1], Q_EPS, None, ALU.max).then_inc(hstep, 1)
                dve.wait_ge(hstep, HSTEPS * n + 2)
                nc.vector.reciprocal(q[:, 2:3], q[:, 1:2]).then_inc(hstep, 1)
                dve.wait_ge(hstep, HSTEPS * n + 3)
                if later(n, 2):
                    dve.wait_ge(hq_ready, n - 1)
                nc.vector.tensor_scalar(hr[i % 2][:, :], h[i % 2][:, :], q[:, 2:3], 127.0, ALU.mult, ALU.mult).then_inc(hstep, 1)
                dve.wait_ge(hstep, HSTEPS * n + 4)
                nc.vector.tensor_scalar(hr[i % 2][:, :], hr[i % 2][:, :], ROUND, ROUND, ALU.add, ALU.subtract).then_inc(clipped, 1)
                nc.vector.tensor_scalar(q[:, 3:4], q[:, 1:2], ws[:, 1:2], None, ALU.mult).then_inc(clipped, 1)

            def add(n, i):
                xt = m["x"][:, bass.ds(n * P, P)]
                dve.wait_ge(clipped, 2 * n + 2)
                dve.wait_ge(y_ready, n + 1)
                nc.vector.scalar_tensor_tensor(xt, y_ps[i % 2][:, 0:D], hmax[i][:, 3:4], xt, ALU.mult, ALU.add).then_inc(x_added, 1)

            tiles(dve, ((0, quantise), (ADD_LAG, add)))

        @block.gpsimd
        def _(pool):
            def clip(n, i):
                pool.wait_ge(clipped, 2 * n + 1)
                if later(n, 2):
                    pool.wait_ge(turned, n - 1)
                if later(n, 1):
                    pool.wait_ge(hq_ready, n)
                nc.gpsimd.sem_inc(clip_turn, 1)
                nc.gpsimd.tensor_scalar(hq[i % 2][:, :], hr[i % 2][:, :], 127.0, -128.0, ALU.min, ALU.max).then_inc(hq_ready, 1)

            tiles(pool, ((0, clip),))

        @block.tensor
        def _(pe):
            pe.wait_ge(stepped, 9)
            for i in range(TILES):
                last = nc.tensor.transpose(xT_ps[:, i * P:(i + 1) * P], xq[:, i * P:(i + 1) * P], identb[:, :])
            last.then_inc(turned_x, 1)
            pe.wait_ge(summed, 2)
            nc.tensor.matmul(y_ps[0][:, 0:2], ones[:, :], wsum[:, :], start=True, stop=True).then_inc(totals, 1)
            pe.wait_ge(stepped, FINAL_STEP)
            pe.wait_ge(xqT_ready, 1)

            def up(n, i):
                if later(n, 2):
                    pe.wait_ge(gelu_done, n - 1)
                nc.tensor.matmul(h_ps[i % 2][:, :], xqT[:, bass.ds(n * P, P)], wq[:, 0, :], start=True, stop=True).then_inc(h_ready, 1)

            def turn(n, i):
                pe.wait_ge(hq_ready, n + 1)
                if later(n, 2):
                    pe.wait_ge(hqT_ready, n - 1)
                for c in range(HC):
                    last = nc.tensor.transpose(t_ps[i % 2][:, c * P:(c + 1) * P], hq[i % 2][:, c * P:(c + 1) * P], identb[:, :])
                last.then_inc(turned, 1)

            def down(n, i):
                pe.wait_ge(hqT_ready, n + 1)
                if later(n, 2):
                    pe.wait_ge(x_added, n - 1)
                for c in range(HC):
                    last = nc.tensor.matmul(y_ps[i % 2][:, 0:D], hqT[i % 2][:, c * P:(c + 1) * P], wq[:, 1, c * P:(c + 1) * P],
                                            start=c == 0, stop=c == HC - 1)
                last.then_inc(y_ready, 1)

            tiles(pe, ((0, up), (TURN_LAG, turn), (ADD_LAG, down)))


MIXTURES = {
    1: dict(chunks=4, gated=0, linear=512, down=1024, early=1),
    2: dict(chunks=1, gated=0, linear=128, down=256, early=E),
    3: dict(chunks=2, gated=256, linear=0, down=512, early=4),
}


def route(nc, t, m, layer, shares, x_high, x_low, early, stages, load, split_high, split_low):
    tag = f"r{layer}"
    with ExitStack() as ctx:
        def sb(name, shape, dt=F32):
            return ctx.enter_context(nc.sbuf_tensor(f"{tag}_{name}", shape, dt))

        sems = []

        def sem(name):
            sems.append(ctx.enter_context(nc.semaphore(f"{tag}_{name}")))
            return sems[-1]

        gate = sb("gate", [P, E])
        number = sb("number", [P, E])
        score, share, other = (sb(n, [P, TILES, E]) for n in ("score", "share", "other"))
        pair = sb("pair", [P, TILES, 2 * E], F32R)
        best, where = sb("best", [P, TILES, 8]), sb("where", [P, TILES, 8], U32)
        wheref = sb("wheref", [P, TILES, 2])
        small = sb("small", [P, 6, TILES])
        a, b_, c_, w1, w2, d_ = (small[:, i, :] for i in range(6))
        s_ps = ctx.enter_context(nc.psum_tensor(f"{tag}_s_ps", [P, TILES * E], F32))
        t_ps = [ctx.enter_context(nc.psum_tensor(f"{tag}_t_ps{i}", [P, 512], F32)) for i in range(4)]
        loaded, scored, stepped, raised, turned, x_high_ready, x_low_ready, w_high_ready, w_low_ready = (
            sem(n) for n in ("loaded", "scored", "stepped", "raised", "turned", "x_high_ready", "x_low_ready", "w_high_ready", "w_low_ready"))
        w_in = [sem(f"w_in{i}") for i in range(stages)]
        softmax_first = layer == 2
        ctx.callback(clear, nc, sems)
        block = ctx.enter_context(nc.Block())

        @block.sync
        def _(sp):
            sp.dma_start(gate[:, :], t[f"L{layer}_gateT"]).then_inc(loaded, 16)
            sp.dma_start(number[:, :], t["numbers"][None, 0:E].to_broadcast([P, E])).then_inc(loaded, 16)
            load(sp, 0, early, w_in, w_low_ready)
            sp.wait_ge(loaded, 32)

        steps_to_raise = 3 if softmax_first else 2 + 2
        steps = {}

        @block.vector
        def _(dve):
            k = 0

            def done(instruction):
                nonlocal k
                k += 1
                instruction.then_inc(stepped, 1)
                dve.wait_ge(stepped, k)

            def wide(v):
                return v[:, :, None].to_broadcast([P, TILES, E])

            dve.wait_ge(x_high_ready, 1)
            nc.vector.tensor_tensor(x_low[:, :], m["xnT"][:, :], x_high[:, :].bitcast(F32), ALU.subtract).then_inc(x_low_ready, 1)
            dve.wait_ge(scored, 1)
            done(nc.vector.tensor_copy(score[:, :, :], s_ps[:, :].rearrange("p (n e) -> p n e", e=E)))
            if softmax_first:
                done(nc.vector.tensor_reduce(a, score[:, :, :], axis=AX.X, op=ALU.max))
                done(nc.vector.tensor_tensor(score[:, :, :], score[:, :, :], wide(a), ALU.subtract))
                dve.wait_ge(raised, 1)
                done(nc.vector.tensor_reduce(a, other[:, :, :], axis=AX.X, op=ALU.add))
                done(nc.vector.reciprocal(b_, a))
                done(nc.vector.tensor_tensor(score[:, :, :], other[:, :, :], wide(b_), ALU.mult))
            for i in range(TILES):
                last = nc.vector.max(best[:, i, :], score[:, i, :])
            done(last)
            for i in range(TILES):
                last = nc.vector.max_index(where[:, i, :], best[:, i, :], score[:, i, :])
            first, second = best[:, :, 0], best[:, :, 1]
            if softmax_first:
                done(last)
                done(nc.vector.tensor_copy(wheref[:, :, :], where[:, :, 0:2]))
                done(nc.vector.tensor_tensor(a, first, second, ALU.add))
                done(nc.vector.tensor_scalar(a, a, L2_EPS, None, ALU.add))
                done(nc.vector.reciprocal(b_, a))
                done(nc.vector.tensor_tensor(w1, first, b_, ALU.mult))
                done(nc.vector.tensor_tensor(w2, second, b_, ALU.mult))
                done(nc.vector.tensor_tensor(a, w1, w2, ALU.add))
                done(nc.vector.tensor_scalar(a, a, L2_EPS, None, ALU.add))
                done(nc.vector.reciprocal(b_, a))
                done(nc.vector.tensor_tensor(w1, w1, b_, ALU.mult))
                done(nc.vector.tensor_tensor(w2, w2, b_, ALU.mult))
            else:
                done(last)
                done(nc.vector.tensor_tensor(a, second, first, ALU.subtract))
                done(nc.vector.tensor_copy(wheref[:, :, :], where[:, :, 0:2]))
                dve.wait_ge(raised, 1)
                done(nc.vector.tensor_scalar(b_, c_, 1.0, None, ALU.add))
                done(nc.vector.reciprocal(w1, b_))
                done(nc.vector.tensor_tensor(w2, c_, w1, ALU.mult))
            numbers = number[:, None, :].to_broadcast([P, TILES, E])
            done(nc.vector.tensor_tensor(share[:, :, :], numbers, wide(wheref[:, :, 0]), ALU.is_equal))
            done(nc.vector.tensor_tensor(other[:, :, :], numbers, wide(wheref[:, :, 1]), ALU.is_equal))
            done(nc.vector.tensor_tensor(share[:, :, :], share[:, :, :], wide(w1), ALU.mult))
            done(nc.vector.tensor_tensor(other[:, :, :], other[:, :, :], wide(w2), ALU.mult))
            done(nc.vector.tensor_tensor(share[:, :, :], share[:, :, :], other[:, :, :], ALU.add))
            done(nc.vector.tensor_copy(pair[:, :, 0:E], share[:, :, :]))
            done(nc.vector.tensor_tensor(pair[:, :, E:2 * E], share[:, :, :], pair[:, :, 0:E].bitcast(F32), ALU.subtract))
            steps["all"] = k
            for i in (1, 3):
                dve.wait_ge(turned, i + 1)
                nc.vector.tensor_copy(shares[:, i * 512:(i + 1) * 512], t_ps[i][0:2 * E, :])

        @block.gpsimd
        def _(pool):
            for e in range(early):
                pool.wait_ge(w_high_ready, e + 1)
                split_low(e, w_low_ready)
                pool.wait_ge(w_low_ready, e + 1)

        @block.scalar
        def _(act):
            nc.scalar.activation(x_high[:, :], m["xnT"][:, :], ACT.Copy).then_inc(x_high_ready, 1)
            act.wait_ge(stepped, steps_to_raise)
            if softmax_first:
                nc.scalar.activation(other[:, :, :], score[:, :, :], ACT.Exp).then_inc(raised, 1)
            else:
                nc.scalar.activation(c_, a, ACT.Exp).then_inc(raised, 1)
            for e in range(early):
                split_high(e, 0, w_in, w_high_ready)
            for i in (0, 2):
                act.wait_ge(turned, i + 1)
                nc.scalar.activation(shares[:, i * 512:(i + 1) * 512], t_ps[i][0:2 * E, :], ACT.Copy)

        @block.tensor
        def _(pe):
            pe.wait_ge(loaded, 32)
            for i in range(TILES):
                last = nc.tensor.matmul(s_ps[:, i * E:(i + 1) * E], m["xnT"][:, i * P:(i + 1) * P], gate[:, :], start=True, stop=True)
            last.then_inc(scored, 1)
            pe.wait_ge(stepped, steps["all"])
            for i in range(4):
                for k in range(4):
                    last = nc.tensor.transpose(t_ps[i][0:2 * E, k * P:(k + 1) * P], pair[:, 4 * i + k, :].bitcast(F32), m["ident"][:, :])
                last.then_inc(turned, 1)


def experts(nc, t, m, layer):
    shape = MIXTURES[layer]
    NC, tag = shape["chunks"], f"e{layer}"
    W = EXPERT_TOK
    GROUPS = TOK // W
    V = E * NC
    COLS = NC * 3 * P
    STAGES = E // NC
    AHEAD = 2
    BUFS = 4
    assert V % BUFS == 0 and E % BUFS == 0 and V >= 8 and GROUPS >= 3
    outer = ExitStack()
    with outer:
        ctx = outer

        def sb(name, shape_, dt=F32):
            return ctx.enter_context(nc.sbuf_tensor(f"{tag}_{name}", shape_, dt))

        shares = sb("shares", [2 * E, TOK], F32R)
        x_high, x_low = sb("x_high", [P, TOK], F32R), sb("x_low", [P, TOK], F32R)
        w_stage = sb("w_stage", [P, STAGES, COLS])
        w_high, w_low = sb("w_high", [P, E, COLS], F32R), sb("w_low", [P, E, COLS], F32R)

        def load(sp, start, end, w_in, w_low_ready):
            for e in range(start, end):
                if e - STAGES >= start:
                    sp.wait_ge(w_low_ready, e - STAGES - start + 1)
                sp.dma_start(w_stage[:, e % STAGES, :], t[f"L{layer}_experts"][:, e, :]).then_inc(w_in[e % STAGES], 16)

        def split_high(e, start, w_in, ready):
            loads = sum(i % STAGES == e % STAGES for i in range(start, e + 1))
            nc.scalar.wait_ge(w_in[e % STAGES], 16 * loads)
            nc.scalar.activation(w_high[:, e, :], w_stage[:, e % STAGES, :], ACT.Copy).then_inc(ready, 1)

        def split_low(e, ready):
            nc.gpsimd.tensor_tensor(w_low[:, e, :], w_stage[:, e % STAGES, :], w_high[:, e, :].bitcast(F32), ALU.subtract).then_inc(ready, 1)

        def weights(e, at):
            return w_high[:, e, at:at + P], w_low[:, e, at:at + P]

        early = shape["early"]
        route(nc, t, m, layer, shares, x_high, x_low, early, STAGES, load, split_high, split_low)

        sems = []

        def sem(name):
            sems.append(ctx.enter_context(nc.semaphore(f"{tag}_{name}")))
            return sems[-1]

        def psum(name):
            return ctx.enter_context(nc.psum_tensor(f"{tag}_{name}", [P, W], F32))

        select, select_rounded = sb("select", [2 * E, E, P]), sb("select_rounded", [2 * E, E, P], F32R)
        xc = [sb(f"xc{i}", [P, W]) for i in range(2)]
        xc_high, xc_low = ([sb(f"xc_{part}{i}", [P, W], F32R) for i in range(BUFS)] for part in ("high", "low"))
        gated = [sb(f"gated{i}", [P, W]) for i in range(2)]
        hid = [sb(f"hid{i}", [P, W]) for i in range(2)]
        hid_high, hid_low = ([sb(f"hid_{part}{i}", [P, W], F32R) for i in range(BUFS)] for part in ("high", "low"))
        ysb = sb("ysb", [P, W])
        y_ps, t_ps = psum("y_ps"), psum("t_ps")
        share_ps, g_ps, l_ps = ([psum(f"{n}{i}") for i in range(2)] for n in ("share_ps", "g_ps", "l_ps"))
        select_in, share_ready, xc_ready, xc_high_ready, xc_low_ready, gate_ready, linear_ready, silu_done = (
            sem(n) for n in ("select_in", "share_ready", "xc_ready", "xc_high_ready", "xc_low_ready", "gate_ready", "linear_ready", "silu_done"))
        hid_ready, hid_high_ready, hid_low_ready, down_done, y_taken, turned, x_added = (
            sem(n) for n in ("hid_ready", "hid_high_ready", "hid_low_ready", "down_done", "y_taken", "turned", "x_added"))
        w_high_ready, w_low_ready, select_ready = sem("w_high_ready"), sem("w_low_ready"), sem("select_ready")
        w_in = [sem(f"w_in{i}") for i in range(STAGES)]
        ctx.callback(clear, nc, sems)
        block = ctx.enter_context(nc.Block())

        def groups(engine, group):
            group(0, True, False)
            with engine.Fori(1, GROUPS - 1) as r:
                group(r, False, False)
            group(GROUPS - 1, False, True)

        def tokens(r, e):
            return bass.ds((r + (e >= E)) * W, W)

        @block.sync
        def _(sp):
            sp.dma_start(select[:, :, :], t["select"]).then_inc(select_in, 16)
            load(sp, early, E, w_in, w_low_ready)
            sp.wait_ge(select_in, 16)

        @block.tensor
        def _(pe):
            pe.wait_ge(select_ready, 1)

            def product(out, w, x, start, stop):
                nc.tensor.matmul(out, w[0], x[0], start=start, stop=False)
                nc.tensor.matmul(out, w[0], x[1], start=False, stop=False)
                return nc.tensor.matmul(out, w[1], x[0], start=False, stop=stop)

            def share(r, e):
                if not (isinstance(r, int) and r == 0 and e < 2):
                    pe.wait_ge(xc_ready, r * E + e - 1)
                nc.tensor.matmul(share_ps[e % 2][:, :], select_rounded[:, e % E, :], shares[:, tokens(r, e)], start=True, stop=True).then_inc(share_ready, 1)

            def product_down(v, n):
                e, c = v // NC, v % NC
                pe.wait_ge(hid_low_ready, n + 1)
                product(y_ps[:, :], weights(e, shape["down"] + c * P), (hid_high[v % BUFS][:, :], hid_low[v % BUFS][:, :]),
                        v == 0, v == V - 1).then_inc(down_done, 1)

            def turn(r, first):
                pe.wait_ge(y_taken, r + 1)
                if not first:
                    pe.wait_ge(x_added, r)
                for k in range(W // P):
                    last = nc.tensor.transpose(t_ps[:, k * P:(k + 1) * P], ysb[:, k * P:(k + 1) * P], m["ident"][:, :])
                last.then_inc(turned, 1)

            def group(r, first, last):
                x = x_high[:, tokens(r, 0)], x_low[:, tokens(r, 0)]
                for v in range(V):
                    e, c, n = v // NC, v % NC, r * V + v
                    if first and c == 0 and e >= early:
                        pe.wait_ge(w_low_ready, e - early + 1)
                    if not (first and v < 2):
                        pe.wait_ge(silu_done, n - 1)
                    at = shape["gated"] + c * P
                    product(g_ps[v % 2][:, :], weights(e, at), x, True, True).then_inc(gate_ready, 1)
                    if c == 0:
                        pe.wait_ge(xc_low_ready, r * E + e + 1)
                    if not (first and v < 2):
                        pe.wait_ge(hid_ready, n - 1)
                    at = shape["linear"] + c * P
                    product(l_ps[v % 2][:, :], weights(e, at), (xc_high[e % BUFS][:, :], xc_low[e % BUFS][:, :]),
                            True, True).then_inc(linear_ready, 1)
                    if c == 0 and not (last and e + AHEAD >= E):
                        share(r, e + AHEAD)
                    if v == 2 and not first:
                        pe.wait_ge(y_taken, r)
                    if not (first and v < 2):
                        product_down((v - 2) % V, n - 2)
                    if v == 3 and not first:
                        turn(r - 1, isinstance(r, int) and r == 1)

            for e in range(AHEAD):
                share(0, e)
            group(0, True, False)
            group(1, False, False)
            with pe.Fori(2, GROUPS - 1) as r:
                group(r, False, False)
            group(GROUPS - 1, False, True)
            for v in (V - 2, V - 1):
                product_down(v, (GROUPS - 1) * V + v)
            turn(GROUPS - 1, False)

        @block.scalar
        def _(act):
            def input_high(r, e):
                f = r * E + e
                act.wait_ge(xc_ready, f + 1)
                if not (isinstance(r, int) and r == 0 and e < BUFS):
                    act.wait_ge(linear_ready, (f - BUFS + 1) * NC)
                nc.scalar.activation(xc_high[e % BUFS][:, :], xc[e % 2][:, :], ACT.Copy).then_inc(xc_high_ready, 1)

            def hidden_high(v, n, counted):
                act.wait_ge(hid_ready, n + 1)
                if counted:
                    act.wait_ge(down_done, n - BUFS + 1)
                nc.scalar.activation(hid_high[v % BUFS][:, :], hid[v % 2][:, :], ACT.Copy).then_inc(hid_high_ready, 1)

            def take_y(r, first):
                act.wait_ge(down_done, (r + 1) * V)
                if not first:
                    act.wait_ge(turned, r)
                nc.scalar.activation(ysb[:, :], y_ps[:, :], ACT.Copy).then_inc(y_taken, 1)

            def group(r, first, last):
                for v in range(V):
                    n = r * V + v
                    act.wait_ge(gate_ready, n + 1)
                    if not (first and v < 2):
                        act.wait_ge(hid_ready, n - 1)
                    nc.scalar.activation(gated[v % 2][:, :], g_ps[v % 2][:, :], ACT.Silu).then_inc(silu_done, 1)
                    if first and v % NC == 0 and early + v // NC < E:
                        split_high(early + v // NC, early, w_in, w_high_ready)
                    e = (v - 1) // NC + AHEAD
                    if (v - 1) % NC == 0 and not (first and v == 0) and not (last and e >= E):
                        input_high(r, e)
                    if not (first and v == 0):
                        hidden_high((v - 1) % V, n - 1, not (first and v - 1 < BUFS))
                    if v == 1 and not first:
                        take_y(r - 1, isinstance(r, int) and r == 1)

            for e in range(AHEAD):
                input_high(0, e)
            group(0, True, False)
            group(1, False, False)
            with act.Fori(2, GROUPS - 1) as r:
                group(r, False, False)
            group(GROUPS - 1, False, True)
            hidden_high(V - 1, GROUPS * V - 1, True)
            take_y(GROUPS - 1, False)

        @block.gpsimd
        def _(pool):
            def input_low(r, e):
                f = r * E + e
                pool.wait_ge(xc_high_ready, f + 1)
                nc.gpsimd.tensor_tensor(xc_low[e % BUFS][:, :], xc[e % 2][:, :], xc_high[e % BUFS][:, :].bitcast(F32), ALU.subtract).then_inc(xc_low_ready, 1)
                pool.wait_ge(xc_low_ready, f + 1)

            def group(r, first, last):
                for e in range(E):
                    if first and early + e < E:
                        pool.wait_ge(w_high_ready, e + 1)
                        split_low(early + e, w_low_ready)
                        pool.wait_ge(w_low_ready, e + 1)
                    if not (last and e + AHEAD >= E):
                        input_low(r, e + AHEAD)

            for e in range(AHEAD):
                input_low(0, e)
            groups(pool, group)

        @block.vector
        def _(dve):
            def scale_input(r, e):
                f = r * E + e
                dve.wait_ge(share_ready, f + 1)
                if not (isinstance(r, int) and r == 0 and e < 2):
                    dve.wait_ge(xc_low_ready, f - 1)
                nc.vector.tensor_tensor(xc[e % 2][:, :], m["xnT"][:, tokens(r, e)], share_ps[e % 2][:, :], ALU.mult).then_inc(xc_ready, 1)

            def hidden_low(v, n):
                dve.wait_ge(hid_high_ready, n + 1)
                nc.vector.tensor_tensor(hid_low[v % BUFS][:, :], hid[v % 2][:, :], hid_high[v % BUFS][:, :].bitcast(F32), ALU.subtract).then_inc(hid_low_ready, 1)

            def add(r):
                xs = m["x"][:, bass.ds(r * W, W)]
                dve.wait_ge(turned, r + 1)
                nc.vector.tensor_tensor(xs, xs, t_ps[:, :], ALU.add).then_inc(x_added, 1)

            def group(r, first, last):
                for v in range(V):
                    e, c, n = v // NC, v % NC, r * V + v
                    dve.wait_ge(silu_done, n + 1)
                    dve.wait_ge(linear_ready, n + 1)
                    if not (first and v < 2):
                        dve.wait_ge(hid_low_ready, n - 1)
                    nc.vector.tensor_tensor(hid[v % 2][:, :], gated[v % 2][:, :], l_ps[v % 2][:, :], ALU.mult).then_inc(hid_ready, 1)
                    if c == 0 and not (last and e + AHEAD >= E):
                        scale_input(r, e + AHEAD)
                    if not (first and v == 0):
                        hidden_low((v - 1) % V, n - 1)
                    if v == 4 and not first:
                        add(r - 1)

            dve.wait_ge(select_in, 16)
            nc.vector.tensor_copy(select_rounded[:, :, :], select[:, :, :]).then_inc(select_ready, 1)
            for e in range(AHEAD):
                scale_input(0, e)
            groups(dve, group)
            hidden_low(V - 1, GROUPS * V - 1)
            add(GROUPS - 1)


def local_attention(nc, t, m):
    WINDOW, POWER, MASKED = 16.0, 128.0, 1e9
    with ExitStack() as ctx:
        sems = []

        def sem(name):
            sems.append(ctx.enter_context(nc.semaphore(f"w_{name}")))
            return sems[-1]

        def sb(name, shape, dt=F32):
            return ctx.enter_context(nc.sbuf_tensor(f"w_{name}", shape, dt))

        def psum(name, cols):
            return ctx.enter_context(nc.psum_tensor(f"w_{name}", [P, cols], F32))

        wa, wc = sb("wa", [P, D]), sb("wc", [P, 2, D])
        number = sb("number", [P, L])
        keyno = sb("keyno", [P, KC])
        centre, length = sb("centre", [P, B]), sb("length", [P, B])
        length_int = sb("length_int", [P, B], I32)
        start, end = sb("start", [P, B]), sb("end", [P, B])
        bounds = sb("bounds", [P, 2])
        gauss = sb("gauss", [P, B, KC])
        gauss_now = sb("gauss_now", [P, KC])
        ctxT, ctxv = sb("ctxT", [P, L]), sb("ctxv", [P, L])
        ctxn, ctxg = sb("ctxn", [P, KC, D]), sb("ctxg", [P, KC, D])
        after, valid, below = sb("after", [P, L]), sb("valid", [P, L]), sb("below", [P, L])
        aT = sb("aT", [P, S])
        masked = [sb(f"masked{i}", [P, L]) for i in range(QT)]
        alT = sb("alT", [P, KC, S])
        stat = [sb(f"stat{i}", [P, 4]) for i in range(QT)]
        cT, hT = sb("cT", [P, S]), sb("hT", [P, S])
        s_ps = psum("s_ps", 2048)
        t_ps = [psum(f"t_ps{i}", 512) for i in range(2)]
        c_ps, o_ps = psum("c_ps", 512), psum("o_ps", 512)
        w_in, ctx_in, ctxn_in, stepped, gauss_ready, gauss_now_ready, bounds_ready, after_ready, valid_ready = (
            sem(n) for n in ("w_in", "ctx_in", "ctxn_in", "stepped", "gauss_ready", "gauss_now_ready", "bounds_ready", "after_ready", "valid_ready"))
        keys_ready, below_ready, values_step, values_ready, score_turn = (
            sem(n) for n in ("keys_ready", "below_ready", "values_step", "values_ready", "score_turn"))
        a_ready, a_taken, scored, masked_ready, minus_ready, exped, inverse_ready, aligned, turned = (
            sem(n) for n in ("a_ready", "a_taken", "scored", "masked_ready", "minus_ready", "exped", "inverse_ready", "aligned", "turned"))
        alT_ready = [sem(f"alT_ready_{engine}") for engine in ("scalar", "vector")]
        c_ready, cT_ready, o_ready, hT_ready, o_turned, x_added = (
            sem(n) for n in ("c_ready", "cT_ready", "o_ready", "hT_ready", "o_turned", "x_added"))
        N_IN = 6
        TURNS = -(-KC // 4)
        FIRST_STEPS = 6

        def take_turned(copy, q, i, **more):
            chunks = range(4 * i, min(4 * i + 4, KC))
            n = len(chunks) * P
            rows = P if i < TURNS - 1 else LAST
            return copy(alT[0:rows, 4 * i:4 * i + len(chunks), q * P:(q + 1) * P],
                        t_ps[i % 2][0:rows, 0:n].rearrange("p (c q) -> p c q", q=P), **more)

        ctx.callback(clear, nc, sems)
        block = ctx.enter_context(nc.Block())

        @block.sync
        def _(sp):
            sp.dma_start(wa[:, :], t["L2_xcond_W_a"]).then_inc(w_in, 16)
            sp.dma_start(wc[:, :, :], t["L2_WcT"].rearrange("(a p) o -> p a o", p=P)).then_inc(w_in, 16)
            sp.dma_start(number[:, :], t["numbers"][None, :].to_broadcast([P, L])).then_inc(w_in, 16)
            sp.dma_start(keyno[:, :], t["key_numbers"]).then_inc(w_in, 16)
            sp.dma_start(centre[:, :], t["condB_pt"][None, :].to_broadcast([P, B])).then_inc(w_in, 16)
            sp.dma_start(length_int[:, :], t["_lenS2"][None, :].to_broadcast([P, B])).then_inc(w_in, 16)

            def load_keys(n):
                sp.dma_start(ctxT[:, :], t["ctxT"][bass.ds(n, 1), :, :].rearrange("o p l -> (o p) l")).then_inc(ctx_in, 16)

            def load_values(n):
                sp.dma_start(ctxn[:, 0:KC - 1, :], t["ctx_1024"][bass.ds(n, 1), 0:L - LAST, :].rearrange("o (c p) d -> (o p) c d", p=P)).then_inc(ctxn_in, 16)
                sp.dma_start(ctxn[0:LAST, KC - 1, :], t["ctx_1024"][bass.ds(n, 1), L - LAST:L, :].rearrange("o p d -> (o p) d")).then_inc(ctxn_in, 16)

            load_keys(0)
            load_values(0)
            sp.wait_ge(keys_ready, 1)
            load_keys(1)
            with sp.Fori(1, B - 1) as n:
                sp.wait_ge(values_ready, n)
                load_values(n)
                sp.wait_ge(keys_ready, n + 1)
                load_keys(n + 1)
            sp.wait_ge(values_ready, B - 1)
            load_values(B - 1)
            sp.wait_ge(w_in, 16 * N_IN)
            sp.wait_ge(ctxn_in, 32 * B)

        @block.gpsimd
        def _(pool):
            def keys(n, first):
                pool.wait_ge(ctx_in, 16 * n + 16)
                pool.wait_ge(valid_ready, n + 1)
                if not first:
                    pool.wait_ge(scored, 2 * n)
                nc.gpsimd.tensor_tensor(ctxv[:, :], ctxT[:, :], valid[:, :], ALU.mult).then_inc(keys_ready, 1)
                pool.wait_ge(keys_ready, n + 1)

            def values(n, first):
                pool.wait_ge(ctxn_in, 32 * n + 32)
                pool.wait_ge(gauss_now_ready, n + 1)
                if not first:
                    pool.wait_ge(c_ready, n)
                nc.gpsimd.tensor_tensor(ctxg[:, 0:KC - 1, :], ctxn[:, 0:KC - 1, :],
                                        gauss_now[:, 0:KC - 1, None].to_broadcast([P, KC - 1, D]), ALU.mult).then_inc(values_step, 1)
                pool.wait_ge(values_step, n + 1)
                nc.gpsimd.tensor_tensor(ctxg[0:LAST, KC - 1, :], ctxn[0:LAST, KC - 1, :],
                                        gauss_now[0:LAST, KC - 1:KC].to_broadcast([LAST, D]), ALU.mult).then_inc(values_ready, 1)
                pool.wait_ge(values_ready, n + 1)

            keys(0, True)
            values(0, True)
            keys(1, False)
            with pool.Fori(1, B - 1) as n:
                keys(n + 1, False)
                values(n, False)
            values(B - 1, False)

        @block.vector
        def _(dve):
            dve.wait_ge(w_in, 16 * N_IN)
            k = 0

            def done(instruction):
                nonlocal k
                k += 1
                instruction.then_inc(stepped, 1)
                dve.wait_ge(stepped, k)

            done(nc.vector.tensor_copy(length[:, :], length_int[:, :]))
            done(nc.vector.tensor_scalar(start[:, :], centre[:, :], WINDOW, 0.0, ALU.subtract, ALU.max))
            done(nc.vector.tensor_scalar(end[:, :], centre[:, :], WINDOW, None, ALU.add))
            done(nc.vector.tensor_tensor(end[:, :], end[:, :], length[:, :], ALU.min))
            keyno3, centre3 = keyno[:, None, :].to_broadcast([P, B, KC]), centre[:, :, None].to_broadcast([P, B, KC])
            done(nc.vector.tensor_tensor(gauss[:, :, :], keyno3, centre3, ALU.subtract))
            done(nc.vector.tensor_tensor(gauss[:, :, :], gauss[:, :, :], gauss[:, :, :], ALU.mult))
            assert k == FIRST_STEPS
            dve.wait_ge(gauss_ready, 1)

            def window(n, first):
                for i, column in enumerate((start, end)):
                    if not first:
                        dve.wait_ge(valid_ready, n)
                    nc.vector.tensor_copy(bounds[:, i:i + 1], column[:, bass.ds(n, 1)]).then_inc(bounds_ready, 1)
                dve.wait_ge(bounds_ready, 2 * n + 2)
                nc.vector.tensor_scalar(after[:, :], number[:, :], bounds[:, 0:1], None, ALU.is_ge).then_inc(after_ready, 1)
                dve.wait_ge(after_ready, n + 1)
                if not first:
                    dve.wait_ge(keys_ready, n)
                    dve.wait_ge(below_ready, n)
                nc.vector.scalar_tensor_tensor(valid[:, :], number[:, :], bounds[:, 1:2], after[:, :], ALU.is_le, ALU.mult).then_inc(valid_ready, 1)

            def addend(n, first):
                dve.wait_ge(valid_ready, n + 1)
                if not first:
                    dve.wait_ge(masked_ready, 2 * n)
                nc.vector.tensor_scalar(below[:, :], valid[:, :], -1.0, MASKED, ALU.add, ALU.mult).then_inc(below_ready, 1)

            def factors(n, first):
                if not first:
                    dve.wait_ge(values_ready, n)
                nc.vector.tensor_copy(gauss_now[:, :], gauss[:, bass.ds(n, 1), :].rearrange("p o c -> p (o c)")).then_inc(gauss_now_ready, 1)

            def mask(n, q, first):
                i = 2 * n + q
                dve.wait_ge(scored, i + 1)
                dve.wait_ge(below_ready, n + 1)
                if not first:
                    dve.wait_ge(turned, (i - 1) * TURNS)
                nc.vector.sem_inc(score_turn, 1)
                nc.vector.tensor_tensor_reduce(masked[q][:, :], s_ps[:, 0:L], below[:, :], 1.0, -3.4e38, ALU.add, ALU.max,
                                               stat[q][:, 0:1]).then_inc(masked_ready, 1)
                dve.wait_ge(masked_ready, i + 1)
                nc.vector.tensor_scalar(stat[q][:, 1:2], stat[q][:, 0:1], -1.0, None, ALU.mult).then_inc(minus_ready, 1)

            def divide(n, q):
                i = 2 * n + q
                dve.wait_ge(exped, i + 1)
                nc.vector.reciprocal(stat[q][:, 3:4], stat[q][:, 2:3]).then_inc(inverse_ready, 1)
                dve.wait_ge(inverse_ready, i + 1)
                nc.vector.tensor_scalar(masked[q][:, :], masked[q][:, :], stat[q][:, 3:4], None, ALU.mult).then_inc(aligned, 1)

            def take(b, q):
                for i in (1, 3):
                    dve.wait_ge(turned, (2 * b + q) * TURNS + i + 1)
                    take_turned(nc.vector.tensor_copy, q, i).then_inc(alT_ready[1], 1)

            def batch(b, last, before_last):
                take(b, 0)
                if not last:
                    mask(b + 1, 0, False)
                take(b, 1)
                if not last:
                    mask(b + 1, 1, False)
                if not (last or before_last):
                    window(b + 2, False)
                dve.wait_ge(c_ready, b + 1)
                nc.vector.tensor_copy(cT[:, :], c_ps[:, 0:S]).then_inc(cT_ready, 1)
                if not last:
                    factors(b + 1, False)
                    divide(b + 1, 0)
                    divide(b + 1, 1)
                if not (last or before_last):
                    addend(b + 2, False)
                dve.wait_ge(o_turned, b + 1)
                xs = m["x"][:, bass.ds(b * S, S)]
                nc.vector.tensor_tensor(xs, xs, c_ps[:, 0:S], ALU.add).then_inc(x_added, 1)

            window(0, True)
            addend(0, True)
            factors(0, True)
            for q in range(QT):
                mask(0, q, True)
            for q in range(QT):
                divide(0, q)
            window(1, False)
            addend(1, False)
            batch(0, False, False)
            with dve.Fori(1, B - 2) as b:
                batch(b, False, False)
            batch(B - 2, False, True)
            batch(B - 1, True, False)

        @block.scalar
        def _(act):
            act.wait_ge(stepped, FIRST_STEPS)
            nc.scalar.activation(gauss[:, :, :], gauss[:, :, :], ACT.Exp, scale=-1.0 / POWER).then_inc(gauss_ready, 1)

            def take_a(n):
                act.wait_ge(a_ready, n + 1)
                nc.scalar.activation(aT[:, :], o_ps[:, 0:S], ACT.Copy).then_inc(a_taken, 1)

            def exp(n, q):
                act.wait_ge(minus_ready, 2 * n + q + 1)
                nc.scalar.activation(masked[q][:, :], masked[q][:, :], ACT.Exp, bias=stat[q][:, 1:2],
                                     accum_out=stat[q][:, 2:3]).then_inc(exped, 1)

            def take(b, q, first):
                for i in (0, 2):
                    act.wait_ge(turned, (2 * b + q) * TURNS + i + 1)
                    if not first:
                        act.wait_ge(c_ready, b)
                    take_turned(nc.scalar.activation, q, i, func=ACT.Copy).then_inc(alT_ready[0], 1)

            def batch(b, first, last):
                take(b, 0, first)
                take(b, 1, first)
                if not last:
                    exp(b + 1, 0)
                    exp(b + 1, 1)
                act.wait_ge(o_ready, b + 1)
                nc.scalar.activation(hT[:, :], o_ps[:, 0:S], ACT.Tanh).then_inc(hT_ready, 1)
                if not (isinstance(b, int) and b >= B - 2):
                    take_a(b + 2)

            take_a(0)
            exp(0, 0)
            exp(0, 1)
            take_a(1)
            batch(0, True, False)
            with act.Fori(1, B - 2) as b:
                batch(b, False, False)
            batch(B - 2, False, False)
            batch(B - 1, False, True)

        @block.tensor
        def _(pe):
            pe.wait_ge(w_in, 16 * N_IN)

            def queries(b):
                return m["xnT"][:, bass.ds(b * S, S)]

            def product_a(n):
                nc.tensor.matmul(o_ps[:, 0:S], wa[:, :], queries(n), start=True, stop=True).then_inc(a_ready, 1)

            def scores(n, q, first):
                if q == 0:
                    pe.wait_ge(a_taken, n + 1)
                    pe.wait_ge(keys_ready, n + 1)
                if not first:
                    pe.wait_ge(masked_ready, 2 * n + q)
                for i in range(TURNS):
                    width = min(512, L - 512 * i)
                    last = nc.tensor.matmul(s_ps[:, 512 * i:512 * i + width], aT[:, q * P:(q + 1) * P], ctxv[:, 512 * i:512 * i + width],
                                            start=True, stop=True)
                last.then_inc(scored, 1)

            def turn(b, q, first):
                n = 2 * b + q
                pe.wait_ge(aligned, n + 1)
                for i in range(TURNS):
                    if i >= 2 or not first:
                        pe.wait_ge(alT_ready[i % 2], 2 * n + i // 2)
                    for k, c in enumerate(range(4 * i, min(4 * i + 4, KC))):
                        rows = chunk_rows(c)
                        last = nc.tensor.transpose(t_ps[i % 2][0:rows, k * P:(k + 1) * P], masked[q][:, c * P:c * P + rows], m["ident"][:, :])
                    last.then_inc(turned, 1)

            def batch(b, first, last):
                if not last:
                    scores(b + 1, 0, False)
                for q in range(QT):
                    turn(b, q, first and q == 0)
                if not last:
                    scores(b + 1, 1, False)
                for taken in alT_ready:
                    pe.wait_ge(taken, TURNS * (b + 1))
                pe.wait_ge(values_ready, b + 1)
                if not first:
                    pe.wait_ge(x_added, b)
                for c in range(KC):
                    rows = chunk_rows(c)
                    final = nc.tensor.matmul(c_ps[:, 0:S], ctxg[0:rows, c, :], alT[0:rows, c, :], start=c == 0, stop=c == KC - 1)
                final.then_inc(c_ready, 1)
                pe.wait_ge(cT_ready, b + 1)
                nc.tensor.matmul(o_ps[:, 0:S], wc[:, 0, :], cT[:, :], start=True, stop=False)
                nc.tensor.matmul(o_ps[:, 0:S], wc[:, 1, :], queries(b), start=False, stop=True).then_inc(o_ready, 1)
                pe.wait_ge(hT_ready, b + 1)
                for q in range(QT):
                    final = nc.tensor.transpose(c_ps[:, q * P:(q + 1) * P], hT[:, q * P:(q + 1) * P], m["ident"][:, :])
                final.then_inc(o_turned, 1)
                if not (isinstance(b, int) and b >= B - 2):
                    product_a(b + 2)

            product_a(0)
            scores(0, 0, True)
            scores(0, 1, False)
            product_a(1)
            batch(0, True, False)
            with pe.Fori(1, B - 2) as b:
                batch(b, False, False)
            batch(B - 2, False, False)
            batch(B - 1, False, True)



def kernel(**inputs):
    import numpy as np
    import concourse.bacc as bacc
    from concourse.bass_utils import run_bass_kernel_spmd

    a = {name: np.asarray(value) for name, value in inputs.items()}
    arrays = {name: a[name] for name in ("x", "ctx_1024", "condB_tau", "fside_BxS2_0", "condB_pt", "_lenS2", "L2_xcond_W_a", "L3_ffn_norm_scale")}
    arrays["ctxT"] = a["ctx_1024"].transpose(0, 2, 1)
    for layer in (0, 1, 3):
        arrays[f"L{layer}_Wq_groups"] = np.repeat(a[f"L{layer}_xcond_Wq"].T.reshape(D, G, 1, ROWS), 3, axis=2)
        for w in ("Wk", "Wv", "Wo"):
            arrays[f"L{layer}_{w}T"] = a[f"L{layer}_xcond_{w}"].T
        arrays[f"L{layer}_bq_rows"] = np.tile(a[f"L{layer}_xcond_bq"].reshape(G, ROWS).T, (3, 1))
        for v in ("bk", "bv", "bo"):
            arrays[f"L{layer}_xcond_{v}"] = a[f"L{layer}_xcond_{v}"]
    arrays["L0_w1T"], arrays["L0_w2T"] = a["L0_ffn_w1"].T, a["L0_ffn_w2"].T
    arrays["L2_WcT"] = a["L2_xcond_W_c"].T

    def by_chunk(w):
        e, h, d = w.shape
        return w.reshape(e, h // P, P, d).transpose(2, 0, 1, 3).reshape(P, e, h // P * d)

    arrays["L1_gateT"], arrays["L2_gateT"], arrays["L3_gateT"] = a["L1_ffn_gate_w"].T, a["L2_ffn_gate_w"].T, a["L3_ffn_w_router"].T
    for layer, up, down in (
            (1, np.concatenate([a["L1_ffn_w1"], a["L1_ffn_w3"]], axis=1).transpose(2, 0, 1), a["L1_ffn_w2"].transpose(0, 2, 1)),
            (2, a["L2_ffn_gate_up_proj"].transpose(1, 0, 2), a["L2_ffn_down_proj"]),
            (3, a["L3_ffn_w_up"].transpose(2, 0, 1), a["L3_ffn_w_down"].transpose(0, 2, 1))):
        arrays[f"L{layer}_experts"] = np.concatenate([up, by_chunk(down)], axis=2)

    row = np.arange(P)
    arrays["ident"] = np.eye(P, dtype=np.float32)
    arrays["qmask"] = (row[:, None] % ROWS // DK == np.arange(J)).astype(np.float32)
    shift = np.zeros((P, J), np.float32)
    shift[96:96 + J] = -np.eye(J)
    shift[100:102] = 1.0
    arrays["shiftmask"] = shift
    rest = np.zeros((P, J), np.float32)
    rest[96:96 + J, 0] = 1.0
    rest[100:102, 1] = 1.0
    arrays["restmask"] = rest
    arrays["numbers"] = np.arange(L, dtype=np.float32)
    arrays["key_numbers"] = (np.arange(KC) * P + row[:, None]).astype(np.float32)
    select = np.zeros((2 * E, E, P), np.float32)
    for part in range(2):
        select[part * E + np.arange(E), np.arange(E)] = 1.0
    arrays["select"] = select
    arrays = {name: np.ascontiguousarray(v) for name, v in arrays.items()}

    nc = bacc.Bacc("TRN2", target_bir_lowering=False, num_devices=1)
    t = {name: nc.dram_tensor(f"in_{name}", v.shape, mybir.dt.from_np(v.dtype), kind="ExternalInput").ap() for name, v in arrays.items()}
    out = nc.dram_tensor("out_x", (B, S, D), F32, kind="ExternalOutput").ap()
    build(nc, t, out)
    r = run_bass_kernel_spmd(nc, [{f"in_{name}": v for name, v in arrays.items()}], core_ids=[0])
    return r.results[0]["out_x"]
```
